# Optimizing a Trainium2 kernel written in Bass

```python
import numpy as np
import jax
import jax.numpy as jnp

def _softmax(x, axis=-1):
    return jax.nn.softmax(x, axis=axis)

def _gelu(x):
    return jax.nn.gelu(x, approximate=True)

def _silu(x):
    return jax.nn.silu(x)

def _sigmoid(x):
    return jax.nn.sigmoid(x)

def _layernorm(x, axis=-1, eps=1e-05):
    m = jnp.mean(x, axis=axis, keepdims=True)
    v = jnp.var(x, axis=axis, keepdims=True)
    return (x - m) / jnp.sqrt(v + eps)

def _scatter_add(tgt, idx, src, axis=0):
    return tgt.at[idx].add(src)

def _segment_sum(src, seg, n):
    return jax.ops.segment_sum(src, seg, n)
kernel_name = 'mk_adaln_ffn_d2_seqx_r8_f847ed'

def setup_inputs(seed: int=0):
    np.random.seed(seed)
    _w = jnp.asarray

    def _rec_inputs():
        import jax
        import jax.numpy as jnp
        _rk = jax.random.key(seed)
        x = -0.0003929 + 0.9999 * jax.random.normal(jax.random.fold_in(_rk, 1), (128, 32, 512), jnp.float32)
        _lenS = 32 - jax.random.randint(jax.random.fold_in(_rk, 7), (128,), 0, max(1, 32 // 4) + 1, jnp.int32)
        _lenS2 = 32 - jax.random.randint(jax.random.fold_in(_rk, 8), (128,), 0, max(1, 32 // 4) + 1, jnp.int32)
        cond_512 = 0.00782532 + 1.00527 * jax.random.normal(jax.random.fold_in(_rk, 11), (128, 64), jnp.float32)
        return (x, cond_512)
    x, cond_512 = _rec_inputs()

    def _L0_cond_setup():
        import jax, jax.numpy as jnp
        from jax import lax
        import numpy as np
        CIN, COUT, K, STYLE_DIM = (32, 32, 3, 64)
        N_LAYERS = 4
        TYPES = ('same', 'upsample', 'same', 'downsample')
        SCALE = 1.0 / float(np.sqrt(CIN * K ** 2))
        EPS = 1e-08
        _BK = np.array([1.0, 3.0, 3.0, 1.0], dtype=np.float32)
        BLUR_K = _BK / _BK.sum()

        def _blur(x, kern, pad):
            B, C, _ = x.shape
            xp = jnp.pad(x, ((0, 0), (0, 0), (pad[0], pad[1])))
            w = jnp.broadcast_to(kern.astype(x.dtype)[None, None, :], (C, 1, kern.shape[0]))
            return lax.conv_general_dilated(xp, w, (1,), 'VALID', feature_group_count=C, dimension_numbers=('NCH', 'OIH', 'NCH'))

        def _conv_same(x, w):
            p = (K - 1) // 2
            return lax.conv_general_dilated(x[None], w, (1,), [(p, p)], dimension_numbers=('NCH', 'OIH', 'NCH'))[0]

        def _conv_down(x, w):
            return lax.conv_general_dilated(x[None], w, (2,), 'VALID', dimension_numbers=('NCH', 'OIH', 'NCH'))[0]

        def _conv_up(x, w_t):
            return lax.conv_transpose(x[None], w_t, (2,), 'VALID', dimension_numbers=('NCH', 'IOH', 'NCH'), transpose_kernel=True)[0]

        def _layer(x, style, w, b, mw, mb, typ):
            s = style @ mw.T + mb
            weight = SCALE * w * s[:, None, :, None]
            demod = lax.rsqrt(jnp.sum(weight * weight, axis=(2, 3)) + EPS)
            weight = weight * demod[:, :, None, None]
            blur_k = jnp.asarray(BLUR_K)
            if typ == 'same':
                out = jax.vmap(_conv_same)(x, weight) + b[None, :, None]
            elif typ == 'upsample':
                out = jax.vmap(_conv_up)(x, weight.transpose(0, 2, 1, 3)) + b[None, :, None]
                out = _blur(out, 2.0 * blur_k, (1, 1))
            elif typ == 'downsample':
                xb = _blur(x, blur_k, (2, 2))
                out = jax.vmap(_conv_down)(xb, weight) + b[None, :, None]
            else:
                raise NotImplementedError(typ)
            return out
        key = jax.random.key(seed)
        ks = jax.random.split(key, 6)
        B, L = (16, 512)
        return {'x': jax.random.normal(ks[0], (B, CIN, L), dtype=jnp.float32), 'style': jax.random.normal(ks[1], (B, STYLE_DIM), dtype=jnp.float32), 'weights': jax.random.normal(ks[2], (N_LAYERS, COUT, CIN, K), dtype=jnp.float32), 'biases': jax.random.normal(ks[3], (N_LAYERS, COUT), dtype=jnp.float32) * 0.1, 'mod_w': jax.random.normal(ks[4], (N_LAYERS, CIN, STYLE_DIM), dtype=jnp.float32) / np.sqrt(STYLE_DIM), 'mod_b': 1.0 + 0.1 * jax.random.normal(ks[5], (N_LAYERS, CIN), dtype=jnp.float32)}
    _L0_cond_all = _L0_cond_setup()
    _L0_cond_in = {k: v for k, v in _L0_cond_all.items() if k in ('weights', 'biases', 'mod_w', 'mod_b')}
    del _L0_cond_all

    def _L0_ffn_setup():
        import jax, jax.numpy as jnp
        import numpy as np
        H = 512
        I = 1376
        B, S = (2, 256)
        key = jax.random.key(seed)
        k1, k2, k3 = jax.random.split(key, 3)
        x = jax.random.normal(k1, (B, S, H), dtype=jnp.float32)
        w_gate_up = jax.random.normal(k2, (2 * I, H), dtype=jnp.float32) * 0.02
        w_down = jax.random.normal(k3, (H, I), dtype=jnp.float32) * 0.02
        return {'x': x, 'w_gate_up': w_gate_up, 'w_down': w_down}
    _L0_ffn_all = _L0_ffn_setup()
    _L0_ffn_in = {k: v for k, v in _L0_ffn_all.items() if k in ('w_gate_up', 'w_down')}
    del _L0_ffn_all

    def _L1_cond_setup():
        import jax, jax.numpy as jnp
        from jax import lax
        import numpy as np
        CIN, COUT, K, STYLE_DIM = (32, 32, 3, 64)
        N_LAYERS = 4
        TYPES = ('same', 'upsample', 'same', 'downsample')
        SCALE = 1.0 / float(np.sqrt(CIN * K ** 2))
        EPS = 1e-08
        _BK = np.array([1.0, 3.0, 3.0, 1.0], dtype=np.float32)
        BLUR_K = _BK / _BK.sum()

        def _blur(x, kern, pad):
            B, C, _ = x.shape
            xp = jnp.pad(x, ((0, 0), (0, 0), (pad[0], pad[1])))
            w = jnp.broadcast_to(kern.astype(x.dtype)[None, None, :], (C, 1, kern.shape[0]))
            return lax.conv_general_dilated(xp, w, (1,), 'VALID', feature_group_count=C, dimension_numbers=('NCH', 'OIH', 'NCH'))

        def _conv_same(x, w):
            p = (K - 1) // 2
            return lax.conv_general_dilated(x[None], w, (1,), [(p, p)], dimension_numbers=('NCH', 'OIH', 'NCH'))[0]

        def _conv_down(x, w):
            return lax.conv_general_dilated(x[None], w, (2,), 'VALID', dimension_numbers=('NCH', 'OIH', 'NCH'))[0]

        def _conv_up(x, w_t):
            return lax.conv_transpose(x[None], w_t, (2,), 'VALID', dimension_numbers=('NCH', 'IOH', 'NCH'), transpose_kernel=True)[0]

        def _layer(x, style, w, b, mw, mb, typ):
            s = style @ mw.T + mb
            weight = SCALE * w * s[:, None, :, None]
            demod = lax.rsqrt(jnp.sum(weight * weight, axis=(2, 3)) + EPS)
            weight = weight * demod[:, :, None, None]
            blur_k = jnp.asarray(BLUR_K)
            if typ == 'same':
                out = jax.vmap(_conv_same)(x, weight) + b[None, :, None]
            elif typ == 'upsample':
                out = jax.vmap(_conv_up)(x, weight.transpose(0, 2, 1, 3)) + b[None, :, None]
                out = _blur(out, 2.0 * blur_k, (1, 1))
            elif typ == 'downsample':
                xb = _blur(x, blur_k, (2, 2))
                out = jax.vmap(_conv_down)(xb, weight) + b[None, :, None]
            else:
                raise NotImplementedError(typ)
            return out
        key = jax.random.key(seed)
        ks = jax.random.split(key, 6)
        B, L = (16, 512)
        return {'x': jax.random.normal(ks[0], (B, CIN, L), dtype=jnp.float32), 'style': jax.random.normal(ks[1], (B, STYLE_DIM), dtype=jnp.float32), 'weights': jax.random.normal(ks[2], (N_LAYERS, COUT, CIN, K), dtype=jnp.float32), 'biases': jax.random.normal(ks[3], (N_LAYERS, COUT), dtype=jnp.float32) * 0.1, 'mod_w': jax.random.normal(ks[4], (N_LAYERS, CIN, STYLE_DIM), dtype=jnp.float32) / np.sqrt(STYLE_DIM), 'mod_b': 1.0 + 0.1 * jax.random.normal(ks[5], (N_LAYERS, CIN), dtype=jnp.float32)}
    _L1_cond_all = _L1_cond_setup()
    _L1_cond_in = {k: v for k, v in _L1_cond_all.items() if k in ('weights', 'biases', 'mod_w', 'mod_b')}
    del _L1_cond_all

    def _L1_ffn_setup():
        import jax, jax.numpy as jnp
        import numpy as np
        B, L, H, Dh, M = (4, 256, 16, 32, 128)
        D = H * Dh
        key = jax.random.key(seed)
        kx, ku, kd, kp = jax.random.split(key, 4)
        x = jax.random.normal(kx, (B, L, D), dtype=jnp.float32)
        up = jax.random.normal(ku, (H, Dh, M), dtype=jnp.float32)
        down = jax.random.normal(kd, (H, M, Dh), dtype=jnp.float32)
        perm = jax.random.permutation(kp, D)
        return {'x': x, 'up': up, 'down': down, 'perm': perm}
    _L1_ffn_all = _L1_ffn_setup()
    _L1_ffn_in = {k: v for k, v in _L1_ffn_all.items() if k in ('up', 'down', 'perm')}
    del _L1_ffn_all
    return {'x': x, 'cond_512': cond_512, 'L0_cond_weights': _L0_cond_in['weights'], 'L0_cond_biases': _L0_cond_in['biases'], 'L0_cond_mod_w': _L0_cond_in['mod_w'], 'L0_cond_mod_b': _L0_cond_in['mod_b'], 'L0_ffn_w_gate_up': _L0_ffn_in['w_gate_up'], 'L0_ffn_w_down': _L0_ffn_in['w_down'], 'L1_cond_weights': _L1_cond_in['weights'], 'L1_cond_biases': _L1_cond_in['biases'], 'L1_cond_mod_w': _L1_cond_in['mod_w'], 'L1_cond_mod_b': _L1_cond_in['mod_b'], 'L1_ffn_up': _L1_ffn_in['up'], 'L1_ffn_down': _L1_ffn_in['down'], 'L1_ffn_perm': _L1_ffn_in['perm']}

def reference(x, cond_512, L0_cond_weights, L0_cond_biases, L0_cond_mod_w, L0_cond_mod_b, L0_ffn_w_gate_up, L0_ffn_w_down, L1_cond_weights, L1_cond_biases, L1_cond_mod_w, L1_cond_mod_b, L1_ffn_up, L1_ffn_down, L1_ffn_perm):
    import jax
    import jax.numpy as jnp

    def _L0_cond_ref(x, style, weights, biases, mod_w, mod_b):
        import jax, jax.numpy as jnp
        from jax import lax
        import numpy as np
        CIN, COUT, K, STYLE_DIM = (32, 32, 3, 64)
        N_LAYERS = 4
        TYPES = ('same', 'upsample', 'same', 'downsample')
        SCALE = 1.0 / float(np.sqrt(CIN * K ** 2))
        EPS = 1e-08
        _BK = np.array([1.0, 3.0, 3.0, 1.0], dtype=np.float32)
        BLUR_K = _BK / _BK.sum()

        def _blur(x, kern, pad):
            B, C, _ = x.shape
            xp = jnp.pad(x, ((0, 0), (0, 0), (pad[0], pad[1])))
            w = jnp.broadcast_to(kern.astype(x.dtype)[None, None, :], (C, 1, kern.shape[0]))
            return lax.conv_general_dilated(xp, w, (1,), 'VALID', feature_group_count=C, dimension_numbers=('NCH', 'OIH', 'NCH'))

        def _conv_same(x, w):
            p = (K - 1) // 2
            return lax.conv_general_dilated(x[None], w, (1,), [(p, p)], dimension_numbers=('NCH', 'OIH', 'NCH'))[0]

        def _conv_down(x, w):
            return lax.conv_general_dilated(x[None], w, (2,), 'VALID', dimension_numbers=('NCH', 'OIH', 'NCH'))[0]

        def _conv_up(x, w_t):
            return lax.conv_transpose(x[None], w_t, (2,), 'VALID', dimension_numbers=('NCH', 'IOH', 'NCH'), transpose_kernel=True)[0]

        def _layer(x, style, w, b, mw, mb, typ):
            s = style @ mw.T + mb
            weight = SCALE * w * s[:, None, :, None]
            demod = lax.rsqrt(jnp.sum(weight * weight, axis=(2, 3)) + EPS)
            weight = weight * demod[:, :, None, None]
            blur_k = jnp.asarray(BLUR_K)
            if typ == 'same':
                out = jax.vmap(_conv_same)(x, weight) + b[None, :, None]
            elif typ == 'upsample':
                out = jax.vmap(_conv_up)(x, weight.transpose(0, 2, 1, 3)) + b[None, :, None]
                out = _blur(out, 2.0 * blur_k, (1, 1))
            elif typ == 'downsample':
                xb = _blur(x, blur_k, (2, 2))
                out = jax.vmap(_conv_down)(xb, weight) + b[None, :, None]
            else:
                raise NotImplementedError(typ)
            return out
        out = x
        for i, typ in enumerate(TYPES):
            out = _layer(out, style, weights[i], biases[i], mod_w[i], mod_b[i], typ)
        return out

    def _L0_ffn_ref(x, w_gate_up, w_down):
        import jax, jax.numpy as jnp
        import numpy as np
        H = 512
        I = 1376
        B, S = (2, 256)
        gate_up = jnp.einsum('bsh,oh->bso', x, w_gate_up)
        d = gate_up.shape[-1] // 2
        h = jax.nn.silu(gate_up[..., :d]) * gate_up[..., d:]
        return jnp.einsum('bsi,hi->bsh', h, w_down)

    def _L1_cond_ref(x, style, weights, biases, mod_w, mod_b):
        import jax, jax.numpy as jnp
        from jax import lax
        import numpy as np
        CIN, COUT, K, STYLE_DIM = (32, 32, 3, 64)
        N_LAYERS = 4
        TYPES = ('same', 'upsample', 'same', 'downsample')
        SCALE = 1.0 / float(np.sqrt(CIN * K ** 2))
        EPS = 1e-08
        _BK = np.array([1.0, 3.0, 3.0, 1.0], dtype=np.float32)
        BLUR_K = _BK / _BK.sum()

        def _blur(x, kern, pad):
            B, C, _ = x.shape
            xp = jnp.pad(x, ((0, 0), (0, 0), (pad[0], pad[1])))
            w = jnp.broadcast_to(kern.astype(x.dtype)[None, None, :], (C, 1, kern.shape[0]))
            return lax.conv_general_dilated(xp, w, (1,), 'VALID', feature_group_count=C, dimension_numbers=('NCH', 'OIH', 'NCH'))

        def _conv_same(x, w):
            p = (K - 1) // 2
            return lax.conv_general_dilated(x[None], w, (1,), [(p, p)], dimension_numbers=('NCH', 'OIH', 'NCH'))[0]

        def _conv_down(x, w):
            return lax.conv_general_dilated(x[None], w, (2,), 'VALID', dimension_numbers=('NCH', 'OIH', 'NCH'))[0]

        def _conv_up(x, w_t):
            return lax.conv_transpose(x[None], w_t, (2,), 'VALID', dimension_numbers=('NCH', 'IOH', 'NCH'), transpose_kernel=True)[0]

        def _layer(x, style, w, b, mw, mb, typ):
            s = style @ mw.T + mb
            weight = SCALE * w * s[:, None, :, None]
            demod = lax.rsqrt(jnp.sum(weight * weight, axis=(2, 3)) + EPS)
            weight = weight * demod[:, :, None, None]
            blur_k = jnp.asarray(BLUR_K)
            if typ == 'same':
                out = jax.vmap(_conv_same)(x, weight) + b[None, :, None]
            elif typ == 'upsample':
                out = jax.vmap(_conv_up)(x, weight.transpose(0, 2, 1, 3)) + b[None, :, None]
                out = _blur(out, 2.0 * blur_k, (1, 1))
            elif typ == 'downsample':
                xb = _blur(x, blur_k, (2, 2))
                out = jax.vmap(_conv_down)(xb, weight) + b[None, :, None]
            else:
                raise NotImplementedError(typ)
            return out
        out = x
        for i, typ in enumerate(TYPES):
            out = _layer(out, style, weights[i], biases[i], mod_w[i], mod_b[i], typ)
        return out

    def _L1_ffn_ref(x, up, down, perm):
        import jax, jax.numpy as jnp
        import numpy as np
        B, L, H, Dh, M = (4, 256, 16, 32, 128)
        D = H * Dh
        b, l, Dm = x.shape
        h, d = (up.shape[0], up.shape[1])
        unperm = jnp.argsort(perm)
        t = x.reshape(b * l, Dm)
        t = t[:, perm]
        t = t.reshape(b * l, h, d)
        t = jnp.einsum('bhd,hdm->bhm', t, up)
        t = jax.nn.gelu(t, approximate=False)
        t = jnp.einsum('bhm,hmd->bhd', t, down)
        t = t.reshape(b * l, h * d)
        t = t[:, unperm]
        out = t.reshape(b, l, Dm)
        return out
    x = x + _L0_ffn_ref(_L0_cond_ref(x, cond_512, L0_cond_weights, L0_cond_biases, L0_cond_mod_w, L0_cond_mod_b), L0_ffn_w_gate_up, L0_ffn_w_down)
    x = x + _L1_ffn_ref(_L1_cond_ref(x, cond_512, L1_cond_weights, L1_cond_biases, L1_cond_mod_w, L1_cond_mod_b), L1_ffn_up, L1_ffn_down, L1_ffn_perm)
    return x

_drawn_inputs = setup_inputs


def setup_inputs(seed=0):
    import zlib

    import numpy as np

    out = dict(_drawn_inputs(seed))
    spreads = {}
    factors = {'L0_cond_biases': 2.784, 'L0_cond_mod_b': 4.904}
    for name, (base, spread) in spreads.items():
        noise = np.random.default_rng([zlib.crc32(name.encode()), seed]).standard_normal(out[name].shape)
        drawn = base * np.exp(spread * noise) if base else spread * noise
        out[name] = jnp.asarray(drawn.astype(out[name].dtype))
    for name, factor in factors.items():
        out[name] = (out[name] * factor).astype(out[name].dtype)
    return out
```

```python
from contextlib import ExitStack

import numpy as np
import concourse.bass as bass
from concourse import mybir

F32 = mybir.dt.float32
F32R = mybir.dt.float32r
I32 = mybir.dt.int32
ALU = mybir.AluOpType
ACT = mybir.ActivationFunctionType

BATCH, CH, LEN = 128, 32, 512
P = 128
J = 4
NBLK = LEN // J
STYLE = 64
KT = 3
LAYERS = 4
SCALE = float(1.0 / np.sqrt(CH * KT ** 2))
EPS = 1e-8
BLUR = [0.125, 0.375, 0.375, 0.125]

TB = 16
TOK = TB * CH
TURNS = BATCH // TB
GB = 4
GROUPS = BATCH // GB
SUBS = TB // GB
HB = TB // 2
HN = HB * CH
INNER = NBLK - 2

TQ, TL, TU = 5, 7, 9
WINDOWS = 3 * J

FF = 1376
FCH = [(c, min(P, FF - c)) for c in range(0, FF, P)]
NF = len(FCH)
HEADS, HM = 16, 128
HPQ = P // CH

SEG = 3
NX, N1, NY, NZ, NV, NVB = 12, 10, 17, 14, 12, 9

A0, A1, A2, A3, D3, D1, S2, S3 = range(8)
NTAB = 8


def compose_coefficients():
    kb = np.convolve(np.array(BLUR), np.array(BLUR)) * 2.0
    c = np.zeros((TQ, KT, TL), np.float32)
    for q in range(TQ):
        for k in range(KT):
            for la in range(TL):
                at = 2 * (la - 3) + 4 + k - q
                if 0 <= at < len(kb):
                    c[q, k, la] = kb[at]
    return c


def build(nc, d, out):
    x1_dram = nc.dram_tensor("x1_scratch", [BATCH, CH, J, NBLK], F32, kind="Internal").ap()
    with ExitStack() as top:
        xe1 = top.enter_context(nc.sbuf_tensor("xe1", [P, GROUPS, 2, 2 * J], F32))
        half(nc, d, 0, d["x0"], x1_dram, xe1)
        half(nc, d, 1, x1_dram, out, xe1)


def half(nc, d, L, x_dram, y_dram, xe1):
    with ExitStack() as ctx:
        def sb(name, shape, dt=F32, c=ctx):
            return c.enter_context(nc.sbuf_tensor(f"{name}_{L}", shape, dt))

        def sem(name):
            return ctx.enter_context(nc.semaphore(f"{name}_{L}"))

        bank = [ctx.enter_context(nc.psum_tensor(f"bank{i}_{L}", [P, 512], F32)) for i in range(8)]
        a4_dram = nc.dram_tensor(f"a4_rows_{L}", [BATCH, CH], F32, kind="Internal").ap()
        edge_dram = nc.dram_tensor(f"edge_rows_{L}", [2 * SEG, GROUPS, J, GB, CH], F32, kind="Internal").ap()

        tab = sb("tab", [P, A3 + 1, BATCH])
        lift1 = sb("lift1", [KT * CH, TQ * CH])
        lift2a = sb("lift2a", [P, TL, CH])
        lift2b = sb("lift2b", [CH, TL, CH])
        lift3a = sb("lift3a", [P, TU * CH])
        lift3b = sb("lift3b", [3 * CH, TU * CH])
        w4 = sb("w4", [KT * CH, CH])
        pick = sb("pick", [2 * SEG, P], F32R)
        if L == 0:
            gu_hi = sb("gu_hi", [P, J, 2 * FF], F32R)
            gu_lo = sb("gu_lo", [P, J, 2 * FF], F32R)
            dn_hi = sb("dn_hi", [P, NF, LEN], F32R)
            dn_lo = sb("dn_lo", [P, NF, LEN], F32R)
            cuts = [(j, c, min(c + 512, 2 * FF)) for j in range(J) for c in range(0, 2 * FF, 512)]
            pieces = [(d["gu"][j, :, a:b], gu_hi[:, j, a:b], gu_lo[:, j, a:b]) for j, a, b in cuts]
            pieces += [(d["dn"][i0:i0 + m, :], dn_hi[0:m, i, :], dn_lo[0:m, i, :])
                       for i, (i0, m) in enumerate(FCH)]
        else:
            up_hi = sb("up_hi", [P, HEADS, HM], F32R)
            up_lo = sb("up_lo", [P, HEADS, HM], F32R)
            hd_hi = sb("hd_hi", [P, HEADS, P], F32R)
            hd_lo = sb("hd_lo", [P, HEADS, P], F32R)
            gather = sb("gather", [P, J, LEN], F32R)
            scatter = sb("scatter", [P, J, LEN], F32R)
            pieces = [(d["up"][:, h:h + 4, :], up_hi[:, h:h + 4, :], up_lo[:, h:h + 4, :])
                      for h in range(0, HEADS, 4)]
            pieces += [(d["hd"][:, h:h + 4, :], hd_hi[:, h:h + 4, :], hd_lo[:, h:h + 4, :])
                       for h in range(0, HEADS, 4)]

        with ExitStack() as pre:
            def tmp(name, shape, dt=F32):
                return sb(name, shape, dt, pre)

            stage = tmp("stage", [P, SUBS, TOK])
            tab2 = tmp("tab2", [P, NTAB - A3 - 1, BATCH])
            cond = tmp("cond", [STYLE, BATCH])
            modw = tmp("modw", [STYLE, LAYERS, P])
            modb = tmp("modb", [P, LAYERS])
            bias = tmp("bias", [P, LAYERS])
            wio = tmp("wio", [CH, LAYERS, KT, CH])
            wsq = tmp("wsq", [CH, LAYERS, J, CH])
            bd = tmp("bd", [P, LAYERS * KT, P])
            w2r = tmp("w2r", [P, KT, CH])
            coef = tmp("coef", [P, 2, KT, TL])
            pickf = tmp("pickf", [2 * SEG, P])
            ident = tmp("ident", [P, P])
            sj = tmp("sj", [P, LAYERS, BATCH])
            sq = tmp("sq", [CH, LAYERS, BATCH])
            dj = tmp("dj", [P, LAYERS, BATCH])
            va = tmp("va", [P, LAYERS, BATCH])
            tg = tmp("tg", [P, NTAB, GROUPS])
            bt = tmp("bt", [P, 3, GROUPS])
            a4t = tmp("a4t", [BATCH, CH])
            nx = tmp("nx", [P, GROUPS, SEG, NX])
            n1 = tmp("n1", [P, GROUPS, SEG, N1])
            ny = tmp("ny", [P, GROUPS, SEG, NY])
            nz = tmp("nz", [P, GROUPS, SEG, NZ])
            ta = tmp("ta", [P, GROUPS, SEG, NZ])
            nv = tmp("nv", [P, GROUPS, SEG, NV])
            nvb = tmp("nvb", [P, GROUPS, SEG, NVB])
            no = tmp("no", [P, SEG, GROUPS, J])
            ehi = tmp("ehi", [P, SEG, P], F32R)
            elo = tmp("elo", [P, SEG, P], F32R)
            if L == 1:
                prow_i = tmp("prow_i", [P, LEN], I32)
                pcol_i = tmp("pcol_i", [P, J], I32)
                prow = tmp("prow", [P, LEN])
                pcol = tmp("pcol", [P, J])
                posrow = tmp("posrow", [P, LEN])
                poscol = tmp("poscol", [P, J])
                loads = [(prow_i[:], d["perm_row"].partition_broadcast(P)), (pcol_i[:], d["perm_col"]),
                         (posrow[:], d["pos_row"].partition_broadcast(P)), (poscol[:], d["pos_col"])]
            else:
                loads = [(xe1[:], d["xe0"])]
            small = [(cond[:], d["cond"]), (modw[:], d["modw"][L]), (modb[:], d["modb"][L]),
                     (wio[:], d["wio"][L]), (bias[:], d["bias"][L]), (bd[:], d["bd"][L]),
                     (lift1[:], d["lift1"][L]), (w2r[:], d["w2r"][L]), (coef[:], d["coef"]),
                     (lift3a[:], d["lift3a"][L]), (lift3b[:], d["lift3b"][L]), (w4[:], d["w4"][L]),
                     (pickf[:], d["pick"]), (ident[:], d["ident"])] + loads

            small_in = sem("small_in")
            piece_in = [sem(f"piece_in{i}") for i in range(SUBS)]
            piece_hi = sem("piece_hi")
            piece_lo = sem("piece_lo")
            vec = sem("vec")
            roots = sem("roots")
            mods = sem("mods")
            sums = sem("sums")
            net = sem("net")
            flip = sem("flip")
            stored = sem("stored")

            with nc.Block() as block:
                @block.sync
                def _(sp):
                    for dst, src in small:
                        sp.dma_start(dst, src).then_inc(small_in, 16)
                    for i, (src, hi, lo) in enumerate(pieces):
                        if i >= SUBS:
                            sp.wait_ge(piece_lo, i - SUBS + 1)
                        m, n = hi.shape[0], int(np.prod(hi.shape[1:]))
                        sp.dma_start(stage[0:m, i % SUBS, 0:n], src).then_inc(piece_in[i % SUBS], 16)

                def split_piece(i):
                    src, hi, lo = pieces[i]
                    m, n = hi.shape[0], int(np.prod(hi.shape[1:]))
                    raw = stage[0:m, i % SUBS, 0:n]
                    if len(hi.shape) == 3:
                        raw = raw.rearrange("p (a b) -> p a b", a=hi.shape[1])
                    return raw, hi, lo

                @block.gpsimd
                def _(pool):
                    for i in range(len(pieces)):
                        raw, hi, lo = split_piece(i)
                        pool.wait_ge(piece_hi, i + 1)
                        nc.gpsimd.tensor_tensor(lo, raw, hi.bitcast(F32), ALU.subtract).then_inc(piece_lo, 1)

                @block.scalar
                def _(act):
                    def piece(i):
                        raw, hi, lo = split_piece(i)
                        act.wait_ge(piece_in[i % SUBS], 16 * (i // SUBS + 1))
                        nc.scalar.activation(hi, raw, ACT.Copy).then_inc(piece_hi, 1)

                    act.wait_ge(vec, STEP_SUMS)
                    nc.scalar.activation(dj[:], va[:], ACT.Sqrt).then_inc(roots, 1)
                    for i in range(len(pieces)):
                        piece(i)
                    act.wait_ge(vec, STEP_A4)
                    act.dma_start(a4_dram, a4t[:]).then_inc(stored, 16)
                    act.wait_ge(vec, STEP_EDGE)
                    for part, tile in enumerate((ehi, elo)):
                        for s in range(SEG):
                            act.dma_start(edge_dram[part * SEG + s].rearrange("g j b o -> (g j) (b o)"),
                                          tile[:, s, :].bitcast(F32)).then_inc(stored, 16)
                    act.wait_ge(stored, 16 * 7)

                def net_chunks(n, size):
                    return [(g, min(size, n - g)) for g in range(0, n, size)]

                @block.tensor
                def _(pe):
                    pe.wait_ge(small_in, 16 * len(small))
                    for l in range(LAYERS):
                        last = nc.tensor.matmul(bank[0][:, l * BATCH:(l + 1) * BATCH], modw[:, l, :], cond[:],
                                                start=True, stop=True)
                    last.then_inc(mods, 1)
                    pe.wait_ge(vec, STEP_SQ)
                    for l in range(LAYERS):
                        last = nc.tensor.matmul(bank[1][:, l * BATCH:(l + 1) * BATCH],
                                                wsq[:, l, :, :].rearrange("p r o -> p (r o)"), sq[:, l, :],
                                                start=True, stop=True)
                    last.then_inc(sums, 1)
                    pe.wait_ge(vec, STEP_TAB)
                    nc.tensor.transpose(bank[2][:, 0:CH], tab2[0:CH, 0, :], ident[0:CH, 0:CH]).then_inc(flip, 1)

                    def taps(dst, l, ks, moving):
                        for n, (k, src) in enumerate(zip(ks, moving)):
                            last = nc.tensor.matmul(dst, bd[:, l * KT + k, :], src,
                                                    start=(n == 0), stop=(n == len(ks) - 1))
                        return last

                    def win(t, g0, gn, a, n, step=1):
                        return t[:, g0:g0 + gn, :, a:a + (n - 1) * step + 1:step].rearrange("p g s n -> p (g s) n")

                    def cols(b, gn, n):
                        return bank[b][:, 0:gn * SEG * n].rearrange("p (g n) -> p g n", n=n)

                    pe.wait_ge(vec, STEP_X)
                    for c, (g0, gn) in enumerate(net_chunks(GROUPS, 16)):
                        taps(cols(c, gn, N1), 0, range(KT),
                             [win(nx, g0, gn, k, N1) for k in range(KT)]).then_inc(net, 1)
                    pe.wait_ge(vec, STEP_1)
                    for c, (g0, gn) in enumerate(net_chunks(GROUPS, 16)):
                        taps(cols(3 + c, gn, 9), 1, (0, 2), [win(n1, g0, gn, 1, 9), win(n1, g0, gn, 0, 9)]).then_inc(net, 1)
                        taps(cols(5 + c, gn, 8), 1, (1,), [win(n1, g0, gn, 1, 8)]).then_inc(net, 1)
                    pe.wait_ge(vec, STEP_Z)
                    for c, (g0, gn) in enumerate(net_chunks(GROUPS, 8)):
                        taps(cols((0, 1, 2, 7)[c], gn, NV), 2, range(KT),
                             [win(nz, g0, gn, k, NV) for k in range(KT)]).then_inc(net, 1)
                    pe.wait_ge(vec, STEP_VB)
                    dst = bank[3][:, 0:SEG * P].rearrange("p (s g j) -> p g s j", s=SEG, j=J)
                    for k in range(KT):
                        last = nc.tensor.matmul(dst, bd[:, 3 * KT + k, :], nvb[:, :, :, k:k + 7:2],
                                                start=(k == 0), stop=(k == KT - 1))
                    last.then_inc(net, 1)
                    pe.wait_ge(vec, STEP_O)
                    for s in range(SEG):
                        last = nc.tensor.transpose(bank[4][:, s * P:(s + 1) * P],
                                                   no[:, s, :, :].rearrange("p g j -> p (g j)"), ident[:])
                    last.then_inc(flip, 1)

                @block.vector
                def _(dve):
                    done = [0]

                    def link(ins):
                        done[0] += 1
                        ins.then_inc(vec, 1)
                        dve.wait_ge(vec, done[0])

                    def at(step):
                        assert done[0] == step, (done[0], step)

                    V = nc.vector
                    dve.wait_ge(small_in, 16 * len(small))
                    link(V.tensor_copy(pick[:], pickf[:]))
                    link(V.tensor_tensor(wio[:], wio[:], wio[:], ALU.mult))
                    link(V.tensor_tensor(wsq[:, :, 0, :], wio[:, :, 0, :], wio[:, :, 1, :], ALU.add))
                    link(V.tensor_tensor(wsq[:, :, 0, :], wsq[:, :, 0, :], wio[:, :, 2, :], ALU.add))
                    link(V.tensor_copy(wsq[:, :, 1, :], wsq[:, :, 0, :]))
                    link(V.tensor_copy(wsq[:, :, 2:4, :], wsq[:, :, 0:2, :]))
                    link(V.tensor_scalar(modb[:], modb[:], SCALE, None, ALU.mult))
                    dve.wait_ge(mods, 1)
                    for l in range(LAYERS):
                        link(V.tensor_scalar(sj[:, l, :], bank[0][:, l * BATCH:(l + 1) * BATCH], SCALE,
                                             modb[:, l:l + 1], ALU.mult, ALU.add))
                    link(V.tensor_tensor(sq[:], sj[0:CH], sj[0:CH], ALU.mult))
                    at(STEP_SQ)
                    dve.wait_ge(sums, 1)
                    link(V.tensor_scalar(va[:], bank[1][:, :].rearrange("p (l b) -> p l b", l=LAYERS), EPS, None, ALU.add))
                    at(STEP_SUMS)
                    dve.wait_ge(roots, 1)
                    link(V.reciprocal(dj[:], dj[:]))
                    link(V.tensor_tensor(va[:], va[:], dj[:], ALU.mult))
                    link(V.tensor_tensor(va[:], va[:], dj[:], ALU.mult))
                    link(V.tensor_scalar(va[:], va[:], -0.5, 1.5, ALU.mult, ALU.add))
                    link(V.tensor_tensor(dj[:], dj[:], va[:], ALU.mult))
                    for to, a, b in ((A1, dj[:, 0], dj[:, 1]), (A2, sj[:, 1], sj[:, 2]), (A3, dj[:, 2], sj[:, 3])):
                        link(V.tensor_tensor(tab[:, to, :], a, b, ALU.mult))
                    for to, a in ((A0, sj[:, 0]), (D3, dj[:, 3]), (D1, dj[:, 1]), (S2, sj[:, 2]), (S3, sj[:, 3])):
                        link(V.tensor_copy(tab[:, to, :] if to <= A3 else tab2[:, to - D3, :], a))
                    at(STEP_TAB)
                    dve.wait_ge(flip, 1)
                    link(V.tensor_copy(a4t[:], bank[2][:, 0:CH]))
                    at(STEP_A4)
                    for r in range(GB):
                        q = slice(CH * r, CH * (r + 1))
                        link(V.tensor_copy(tg[q, 0:D3, :], tab[q, :, r::GB]))
                        link(V.tensor_copy(tg[q, D3:NTAB, :], tab2[q, :, r::GB]))
                    for n, f in enumerate((D1, S2, S3)):
                        link(V.tensor_scalar(bt[:, n, :], tg[:, f, :], bias[:, n:n + 1], None, ALU.mult))

                    def factor(t, g0, gn, n):
                        return t[:, g0:g0 + gn].unsqueeze(2).to_broadcast([P, gn, n])

                    link(V.memset(nx[:], 0.0))
                    s0 = tg[:, A0, :].unsqueeze(2).to_broadcast([P, GROUPS, 2 * J])
                    link(V.tensor_tensor(nx[:, :, 0, 4:12], xe1[:, :, 0, :], s0, ALU.mult))
                    link(V.tensor_tensor(nx[:, :, 1, 0:8], xe1[:, :, 1, :], s0, ALU.mult))
                    at(STEP_X)

                    def evacuate(b, dst, g0, gn, n, fa, fb):
                        src = bank[b][:, 0:gn * SEG * n].rearrange("p (g n) -> p g n", g=gn)
                        src = src.rearrange("p g (s n) -> p g s n", s=SEG)
                        a = tg[:, fa, g0:g0 + gn].unsqueeze(2).unsqueeze(3).to_broadcast([P, gn, SEG, n])
                        c = bt[:, fb, g0:g0 + gn].unsqueeze(2).unsqueeze(3).to_broadcast([P, gn, SEG, n])
                        link(V.tensor_tensor(dst, src, a, ALU.mult))
                        link(V.tensor_tensor(dst, dst, c, ALU.add))

                    for c, (g0, gn) in enumerate(net_chunks(GROUPS, 16)):
                        dve.wait_ge(net, c + 1)
                        evacuate(c, n1[:, g0:g0 + gn, :, :], g0, gn, N1, A1, 0)
                    link(V.memset(n1[:, :, 0, 0:3], 0.0))
                    link(V.memset(n1[:, :, 1, 7:10], 0.0))
                    at(STEP_1)
                    for c, (g0, gn) in enumerate(net_chunks(GROUPS, 16)):
                        dve.wait_ge(net, 2 + 2 * c + 1)
                        evacuate(3 + c, ny[:, g0:g0 + gn, :, 0:17:2], g0, gn, 9, A2, 1)
                        dve.wait_ge(net, 2 + 2 * c + 2)
                        evacuate(5 + c, ny[:, g0:g0 + gn, :, 1:17:2], g0, gn, 8, A2, 1)
                    link(V.memset(ny[:, :, 0, 0:4], 0.0))
                    link(V.memset(ny[:, :, 1, 13:17], 0.0))

                    def blur(dst, src, n, gain):
                        w = [src[:, :, :, t:t + n].rearrange("p g s n -> p (g s) n") for t in range(4)]
                        o = dst[:, :, :, 0:n].rearrange("p g s n -> p (g s) n")
                        u = ta[:, :, :, 0:n].rearrange("p g s n -> p (g s) n")
                        link(V.tensor_tensor(u, w[1], w[2], ALU.add))
                        link(V.tensor_scalar(u, u, gain * BLUR[1], None, ALU.mult))
                        link(V.tensor_tensor(o, w[0], w[3], ALU.add))
                        link(V.scalar_tensor_tensor(o, o, gain * BLUR[0], u, ALU.mult, ALU.add))

                    blur(nz, ny, NZ, 2.0)
                    link(V.memset(nz[:, :, 0, 0:3], 0.0))
                    link(V.memset(nz[:, :, 1, 11:14], 0.0))
                    at(STEP_Z)
                    for c, (g0, gn) in enumerate(net_chunks(GROUPS, 8)):
                        dve.wait_ge(net, 6 + c + 1)
                        evacuate((0, 1, 2, 7)[c], nv[:, g0:g0 + gn, :, :], g0, gn, NV, A3, 2)
                    link(V.memset(nv[:, :, 0, 0:2], 0.0))
                    link(V.memset(nv[:, :, 1, 10:12], 0.0))
                    blur(nvb, nv, NVB, 1.0)
                    at(STEP_VB)
                    dve.wait_ge(net, 11)
                    src = bank[3][:, 0:SEG * P].rearrange("p (s g j) -> p s g j", s=SEG, j=J)
                    d3 = tg[:, D3, :].unsqueeze(1).unsqueeze(3).to_broadcast([P, SEG, GROUPS, J])
                    link(V.tensor_tensor(no[:], src, d3, ALU.mult))
                    link(V.tensor_scalar(no[:], no[:], bias[:, 3:4], None, ALU.add))
                    at(STEP_O)
                    dve.wait_ge(flip, 2)
                    src = bank[4][:, 0:SEG * P].rearrange("p (s n) -> p s n", s=SEG)
                    link(V.tensor_copy(ehi[:], src))
                    link(V.tensor_tensor(elo[:], src, ehi[:].bitcast(F32), ALU.subtract))
                    at(STEP_EDGE)
                    for lift, which, m in ((lift2a, 0, P), (lift2b, 1, CH)):
                        t = ta[0:m, 0:GROUPS, :, :].rearrange("p g s n -> p (g s n)")[:, 0:TL * CH]
                        t = t.rearrange("p (a b) -> p a b", a=TL)
                        for k in range(KT):
                            w = w2r[0:m, k, :].unsqueeze(1).to_broadcast([m, TL, CH])
                            f = coef[0:m, which, k, :].unsqueeze(2).to_broadcast([m, TL, CH])
                            if k == 0:
                                link(V.tensor_tensor(lift[:], w, f, ALU.mult))
                            else:
                                link(V.tensor_tensor(t, w, f, ALU.mult))
                                link(V.tensor_tensor(lift[:], lift[:], t, ALU.add))
                    if L == 1:
                        link(V.tensor_copy(prow[:], prow_i[:]))
                        link(V.tensor_copy(pcol[:], pcol_i[:]))
                        for j in range(J):
                            link(V.tensor_scalar(gather[:, j, :], prow[:], poscol[:, j:j + 1], None, ALU.is_equal))
                            link(V.tensor_scalar(scatter[:, j, :], posrow[:], pcol[:, j:j + 1], None, ALU.is_equal))

        taps_e = sb("taps_e", [P, WINDOWS, TOK])
        xin = sb("xin", [P, TB, NBLK])
        rows = sb("rows", [2 * SEG, SUBS, 512], F32R)
        a4 = sb("a4", [KT * CH, TOK])
        z_hi = sb("z_hi", [P, J, TOK], F32R)
        z_lo = sb("z_lo", [P, J, TOK], F32R)
        r0 = sb("r0", [KT * CH, HN])
        h1a = sb("h1a", [P, HN])
        h1b = sb("h1b", [CH, HN])
        h2a = sb("h2a", [P, HN])
        h2b = sb("h2b", [3 * CH, HN])
        h3 = sb("h3", [P, 3, HN])
        NH = 2 if L == 0 else 3
        hid = sb("hid", [P, NH, TOK])
        hid_hi = sb("hid_hi", [P, NH, TOK], F32R)
        hid_lo = sb("hid_lo", [P, NH, TOK], F32R)
        if L == 1:
            t_hi = sb("t_hi", [P, 2, TOK], F32R)
            t_lo = sb("t_lo", [P, 2, TOK], F32R)
            y_hi = sb("y_hi", [P, J, TOK], F32R)
            y_lo = sb("y_lo", [P, J, TOK], F32R)
        NR = 2 if L == 0 else SUBS
        res = sb("res", [P, NR, TOK])

        x_in = sem("x_in")
        rows_in = sem("rows_in")
        a4_in = sem("a4_in")
        res_in = [sem(f"res_in{s}") for s in range(NR)]
        out_done = [sem(f"out_done{s}") for s in range(NR)]
        e_in = sem("e_in")
        zeroed = sem("zeroed")
        conv_ready = sem("conv_ready")
        z_high = sem("z_high")
        z_ready = sem("z_ready")
        seed = sem("seed")
        lifted = sem("lifted")
        kept = sem("kept")
        first_ready = sem("first_ready")
        second_ready = sem("second_ready")
        act_done = sem("act_done")
        mul_done = sem("mul_done")
        high_done = sem("high_done")
        hid_ready = sem("hid_ready")
        down_done = sem("down_done")
        perm_ready = sem("perm_ready")
        t_high = sem("t_high")
        t_ready = sem("t_ready")
        sum_ready = sem("sum_ready")
        y_high = sem("y_high")
        y_ready = sem("y_ready")
        acc_ready = sem("acc_ready")
        out_ready = sem("out_ready")
        ends_kept = sem("ends_kept")

        E_DMAS = J * J
        STEPS = 6

        CHUNKS = NF if L == 0 else HEADS
        x_rows = x_dram.rearrange("b c j n -> (b c) (j n)")
        y_rows = y_dram.rearrange("b c j n -> (b c) (j n)")

        def compose_banks(step):
            if L == 1:
                return bank[6], bank[7]
            pair = (step + 1) % 2
            return bank[2 * pair], bank[2 * pair + 1]

        with nc.Block() as block:
            @block.sync
            def _(sp):
                def load_x(t):
                    for j in range(J):
                        sp.dma_start(xin[CH * j:CH * (j + 1), :, :],
                                     x_dram[bass.ds(t * TB, TB), :, j, :].rearrange("b c n -> c b n")).then_inc(x_in, 16)

                def load_rows(t):
                    for g in range(SUBS):
                        for b in range(GB):
                            sp.dma_start(rows[:, g, P * b:P * (b + 1)].bitcast(F32).rearrange("r (j o) -> r j o", j=J),
                                         edge_dram[:, bass.ds(t * SUBS + g, 1), :, b, :].rearrange("r g j o -> r (g j) o")
                                         ).then_inc(rows_in, 16)

                def load_a4(t):
                    sp.dma_start(a4[:], a4_dram.rearrange("b o -> (b o)")[bass.ds(t * TOK, TOK)]
                                 .partition_broadcast(KT * CH)).then_inc(a4_in, 16)

                def load_res(t, s):
                    sp.dma_start(res[:, s % NR, :], x_rows[bass.ds(t * TOK + s * P, P), :]).then_inc(res_in[s % NR], 16)

                def spread(t, half_):
                    for g in range(J):
                        tiles = 3 if g == 0 else 2
                        for j in range(J):
                            sp.dma_start(taps_e[CH * j:CH * (j + 1), g + j:g + j + J * (tiles - 1) + 1:J,
                                                half_ * HN:(half_ + 1) * HN],
                                         h3[CH * g:CH * (g + 1), 0:tiles, :]).then_inc(e_in, 16)

                load_a4(0)
                load_x(0)
                load_rows(0)
                sp.wait_ge(zeroed, 2)
                for hh in range(2):
                    sp.wait_ge(kept, 3 * (hh + 1))
                    spread(0, hh)
                for s in range(NR):
                    load_res(0, s)

                def turn(t, more):
                    if more:
                        sp.wait_ge(seed, 4 * t + 4)
                        load_a4(t + 1)
                        sp.wait_ge(conv_ready, SUBS * t + SUBS)
                        load_x(t + 1)
                        load_rows(t + 1)
                        for hh in range(2):
                            sp.wait_ge(kept, STEPS * t + STEPS + 3 * (hh + 1))
                            spread(t + 1, hh)
                    per = SUBS // NR
                    for s in range(SUBS):
                        sp.wait_ge(out_ready, SUBS * t + s + 2)
                        sp.dma_start(y_rows[bass.ds(t * TOK + s * P, P), :], res[:, s % NR, :]).then_inc(out_done[s % NR], 16)
                        if s + NR < SUBS or more:
                            if L == 0:
                                sp.wait_ge(ends_kept, SUBS * t + s + 1)
                            sp.wait_ge(out_done[s % NR], 16 * (per * t + s // NR + 1))
                            load_res(*((t, s + NR) if s + NR < SUBS else (t + 1, s + NR - SUBS)))
                    if not more:
                        for s in range(NR):
                            sp.wait_ge(out_done[s], 16 * per * TURNS)

                with sp.Fori(0, TURNS - 1) as t:
                    turn(t, True)
                turn(TURNS - 1, False)

            @block.gpsimd
            def _(pool):
                nc.gpsimd.memset(taps_e[:, 0:J, :], 0.0).then_inc(zeroed, 1)
                nc.gpsimd.memset(taps_e[:, 2 * J:3 * J, :], 0.0).then_inc(zeroed, 1)
                if L == 0:
                    def turn(t):
                        for s in range(SUBS):
                            pool.wait_ge(out_ready, SUBS * t + s + 2)
                            tile = res[:, s % NR, :].rearrange("p (j n) -> p n j", j=J)
                            ends = xe1[:, bass.ds(t * SUBS + s, 1), :, :]
                            for e, n0 in ((0, 0), (1, NBLK - 2)):
                                last = nc.gpsimd.tensor_copy(ends[:, 0, e, :].rearrange("p (n j) -> p n j", j=J),
                                                             tile[:, n0:n0 + 2, :])
                            last.then_inc(ends_kept, 1)
                    with pool.Fori(0, TURNS) as t:
                        turn(t)

            @block.tensor
            def _(pe):
                MM = nc.tensor.matmul

                def step(t, n):
                    a, b = compose_banks(n)
                    hh, st = divmod(n, 3)
                    if n > 0:
                        pe.wait_ge(kept, STEPS * t + n)
                    if st == 0:
                        pe.wait_ge(seed, 4 * t + 2 * (hh + 1))
                        MM(a[:, 0:HN], lift1[:, 0:P], r0[:], start=True, stop=True)
                        last = MM(a[0:CH, HN:2 * HN], lift1[:, P:P + CH], r0[:], start=True, stop=True)
                    if st == 1:
                        la, lb = (x[:].rearrange("p a b -> p (a b)") for x in (lift2a, lift2b))
                        for c0, m, at in ((0, P, 0), (P, 3 * CH, HN)):
                            MM(a[0:m, at:at + HN], la[:, c0:c0 + m], h1a[:], start=True, stop=False)
                            last = MM(a[0:m, at:at + HN], lb[:, c0:c0 + m], h1b[:], start=False, stop=True)
                    if st == 2:
                        for c0, at in ((0, 0), (P, HN)):
                            MM(a[:, at:at + HN], lift3a[:, c0:c0 + P], h2a[:], start=True, stop=False)
                            MM(a[:, at:at + HN], lift3b[:, c0:c0 + P], h2b[:], start=False, stop=True)
                        last = MM(b[0:CH, 0:HN], lift3a[:, 2 * P:2 * P + CH], h2a[:], start=True, stop=True)
                    last.then_inc(lifted, 1)

                def convolve(t):
                    pe.wait_ge(x_in, 16 * J * t + 16 * J)
                    pe.wait_ge(rows_in, 16 * TB * t + 16 * TB)
                    pe.wait_ge(e_in, 16 * 2 * E_DMAS * t + 16 * 2 * E_DMAS)
                    for g in range(SUBS):
                        MM(bank[g][:, :], pick[:], rows[:, g, :], start=True, stop=False)
                        for bb in range(GB):
                            b = GB * g + bb
                            dst = bank[g][0:INNER, P * bb:P * (bb + 1)].rearrange("p (j o) -> p j o", j=J)
                            for s in (-1, 0, 1):
                                last = MM(dst, xin[:, b, 1 + s:1 + s + INNER],
                                          taps_e[:, J * (1 - s):J * (2 - s), CH * b:CH * (b + 1)],
                                          start=False, stop=(bb == GB - 1 and s == 1))
                        last.then_inc(conv_ready, 1)

                def three(dst, w_hi, w_lo, m_hi, m_lo, first, final):
                    MM(dst, w_hi, m_hi, start=first, stop=False)
                    MM(dst, w_hi, m_lo, start=False, stop=False)
                    return MM(dst, w_lo, m_hi, start=False, stop=final)

                def gate_up(t, c):
                    i0, m = FCH[c]
                    pair = c % 2
                    if c >= 2:
                        pe.wait_ge(mul_done, CHUNKS * t + c - 1)
                    for which, ready in ((0, first_ready), (1, second_ready)):
                        col = which * FF + i0
                        dst = bank[2 * pair + which][0:m, :]
                        for j in range(J):
                            last = three(dst, gu_hi[:, j, col:col + m], gu_lo[:, j, col:col + m],
                                         z_hi[:, j, :], z_lo[:, j, :], j == 0, j == J - 1)
                        last.then_inc(ready, 1)

                def down(t, c):
                    i0, m = FCH[c]
                    pe.wait_ge(hid_ready, CHUNKS * t + c + 1)
                    for s in range(SUBS):
                        hi = hid_hi[0:m, c % NH, P * s:P * (s + 1)]
                        lo = hid_lo[0:m, c % NH, P * s:P * (s + 1)]
                        last = three(bank[4 + s][:, :], hi, lo, dn_hi[0:m, c, :], dn_lo[0:m, c, :],
                                     c == 0, c == NF - 1)
                        if c == NF - 1:
                            last.then_inc(acc_ready, 1)
                    if c < NF - 1:
                        last.then_inc(down_done, 1)

                def gated(t, more):
                    pe.wait_ge(z_ready, SUBS * t + SUBS)
                    for c in range(NF):
                        if more and 1 <= c <= STEPS:
                            pe.wait_ge(kept, STEPS * t + STEPS + c)
                        gate_up(t, c)
                        if more and c < STEPS:
                            if c >= 1:
                                pe.wait_ge(mul_done, CHUNKS * t + c)
                            step(t + 1, c)
                        if c >= 1:
                            if c == 1:
                                tail_wait(t)
                            down(t, c - 1)
                    down(t, NF - 1)

                def tail_wait(t):
                    pe.wait_ge(out_ready, SUBS * t + 1)

                def permute(t, q):
                    if q >= 2:
                        pe.wait_ge(t_ready, J * t + q - 1)
                    dst = bank[q % 2][:, :]
                    for j in range(J):
                        w = gather[:, j, P * q:P * (q + 1)]
                        MM(dst, w, z_hi[:, j, :], start=(j == 0), stop=False)
                        last = MM(dst, w, z_lo[:, j, :], start=False, stop=(j == J - 1))
                    last.then_inc(perm_ready, 1)

                def head_up(t, h):
                    q = h // HPQ
                    if h % HPQ == 0:
                        pe.wait_ge(t_ready, J * t + q + 1)
                    if h >= 2:
                        pe.wait_ge(act_done, HEADS * t + h - 1)
                    three(bank[2 + h % 2][:, :], up_hi[:, h, :], up_lo[:, h, :],
                          t_hi[:, q % 2, :], t_lo[:, q % 2, :], True, True).then_inc(first_ready, 1)

                def head_down(t, h):
                    q, r = divmod(h, HPQ)
                    pe.wait_ge(hid_ready, HEADS * t + h + 1)
                    if r == 0 and q >= 2:
                        pe.wait_ge(y_ready, J * t + q - 1)
                    last = three(bank[4 + q % 2][:, :], hd_hi[:, h, :], hd_lo[:, h, :],
                                 hid_hi[:, h % NH, :], hid_lo[:, h % NH, :], r == 0, r == HPQ - 1)
                    last.then_inc(sum_ready if r == HPQ - 1 else down_done, 1)

                def grouped(t, more):
                    pe.wait_ge(z_ready, SUBS * t + SUBS)
                    permute(t, 0)
                    permute(t, 1)
                    for h in range(HEADS + 2):
                        if h < HEADS:
                            head_up(t, h)
                        if h % 4 == 2 and 2 + h // 4 < J:
                            permute(t, 2 + h // 4)
                        if more and h % 2 == 1 and h // 2 < STEPS:
                            n = h // 2
                            if n == 0:
                                pe.wait_ge(out_ready, SUBS * t + 1)
                            step(t + 1, n)
                        if h >= 2:
                            head_down(t, h - 2)
                    if more:
                        pe.wait_ge(kept, STEPS * t + 2 * STEPS)
                    for s in range(SUBS):
                        dst = bank[(6, 7, 0, 1)[s]][:, :]
                        for q in range(J):
                            if s == 0:
                                pe.wait_ge(y_ready, J * t + q + 1)
                            MM(dst, y_hi[:, q, P * s:P * (s + 1)], scatter[:, q, :], start=(q == 0), stop=False)
                            last = MM(dst, y_lo[:, q, P * s:P * (s + 1)], scatter[:, q, :], start=False, stop=(q == J - 1))
                        last.then_inc(acc_ready, 1)

                def turn(t, more):
                    if L == 1:
                        pe.wait_ge(out_ready, SUBS * t + 1)
                    convolve(t)
                    (gated if L == 0 else grouped)(t, more)

                for n in range(STEPS):
                    step(0, n)
                with pe.Fori(0, TURNS - 1) as t:
                    turn(t, True)
                turn(TURNS - 1, False)

            @block.scalar
            def _(act):
                def turn(t, more):
                    for g in range(SUBS):
                        act.wait_ge(conv_ready, SUBS * t + g + 1)
                        dst = z_hi[:, :, P * g:P * (g + 1)].rearrange("p j (b o) -> p b j o", b=GB)
                        src = bank[g][:, :].rearrange("p (b j o) -> p b j o", b=GB, j=J)
                        nc.scalar.activation(dst, src, ACT.Copy).then_inc(z_high, 1)
                    if L == 0:
                        for c in range(NF):
                            m = FCH[c][1]
                            act.wait_ge(first_ready, NF * t + c + 1)
                            if c >= 2:
                                act.wait_ge(hid_ready, NF * t + c - 1)
                            nc.scalar.activation(hid[0:m, c % NH, :], bank[2 * (c % 2)][0:m, :], ACT.Silu).then_inc(act_done, 1)
                    else:
                        for q in range(2):
                            t_part(t, q)
                        for h in range(HEADS + 2):
                            if h < HEADS:
                                act.wait_ge(first_ready, HEADS * t + h + 1)
                                if h >= NH:
                                    act.wait_ge(hid_ready, HEADS * t + h - NH + 1)
                                nc.scalar.activation(hid[:, h % NH, :], bank[2 + h % 2][:, :], ACT.Gelu).then_inc(act_done, 1)
                            if h % 4 == 2 and 2 + h // 4 < J:
                                t_part(t, 2 + h // 4)
                            if h >= 5 and (h - 5) % 4 == 0:
                                y_part(t, (h - 5) // 4)

                def t_part(t, q):
                    act.wait_ge(perm_ready, J * t + q + 1)
                    if q >= 2:
                        act.wait_ge(first_ready, HEADS * t + HPQ * (q - 1))
                    nc.scalar.activation(t_hi[:, q % 2, :], bank[q % 2][:, :], ACT.Copy).then_inc(t_high, 1)

                def y_part(t, q):
                    act.wait_ge(sum_ready, J * t + q + 1)
                    nc.scalar.activation(y_hi[:, q, :], bank[4 + q % 2][:, :], ACT.Copy).then_inc(y_high, 1)

                with act.Fori(0, TURNS - 1) as t:
                    turn(t, True)
                turn(TURNS - 1, False)

            @block.vector
            def _(dve):
                V = nc.vector

                def first_matrix(t, hh):
                    b0 = t * TB + hh * HB
                    out3 = r0[:].rearrange("p (b o) -> p b o", b=HB)
                    f = tab[0:KT * CH, A3, bass.ds(b0, HB)].unsqueeze(2).to_broadcast([KT * CH, HB, CH])
                    w = w4[:].unsqueeze(1).to_broadcast([KT * CH, HB, CH])
                    V.tensor_tensor(out3, w, f, ALU.mult).then_inc(seed, 1)
                    dve.wait_ge(a4_in, 16 * t + 16)
                    dve.wait_ge(seed, 4 * t + 2 * hh + 1)
                    V.tensor_tensor(r0[:], r0[:], a4[:, hh * HN:(hh + 1) * HN], ALU.mult).then_inc(seed, 1)

                def keep(t, n):
                    a, b = compose_banks(n)
                    hh, st = divmod(n, 3)
                    dve.wait_ge(lifted, STEPS * t + n + 1)
                    if st == 2:
                        n_e = 16 * E_DMAS
                        if not (isinstance(t, int) and t == 0 and hh == 0):
                            dve.wait_ge(e_in, n_e * 2 * t + n_e * hh)
                    tiles = {0: ((h1a[:], a, 0, P), (h1b[:], a, HN, CH)),
                             1: ((h2a[:], a, 0, P), (h2b[:], a, HN, 3 * CH)),
                             2: ((h3[:, 0, :], a, 0, P), (h3[:, 1, :], a, HN, P), (h3[0:CH, 2, :], b, 0, CH))}[st]
                    for dst, src, at, m in tiles:
                        f = tab[0:m, (A2, A1, A0)[st], bass.ds(t * TB + hh * HB, HB)].unsqueeze(2).to_broadcast([m, HB, CH])
                        last = V.tensor_tensor(dst.rearrange("p (b o) -> p b o", b=HB),
                                               src[0:m, at:at + HN].rearrange("p (b o) -> p b o", b=HB), f, ALU.mult)
                    last.then_inc(kept, 1)

                def compose_part(t, n):
                    keep(t, n)
                    if n == 0:
                        first_matrix(t, 1)

                def hidden(t, c, m):
                    k = c % NH
                    if c >= NH:
                        down_wait(t, c - NH)
                    V.tensor_copy(hid_hi[0:m, k, :], hid[0:m, k, :]).then_inc(high_done, 1)
                    dve.wait_ge(high_done, CHUNKS * t + c + 1)
                    V.tensor_tensor(hid_lo[0:m, k, :], hid[0:m, k, :], hid_hi[0:m, k, :].bitcast(F32),
                                    ALU.subtract).then_inc(hid_ready, 1)

                def down_wait(t, c):
                    if L == 0:
                        dve.wait_ge(down_done, (NF - 1) * t + c + 1)
                    elif c % HPQ == HPQ - 1:
                        dve.wait_ge(sum_ready, J * t + c // HPQ + 1)
                    else:
                        dve.wait_ge(down_done, (HEADS - J) * t + c - c // HPQ + 1)

                def t_part(t, q):
                    dve.wait_ge(t_high, J * t + q + 1)
                    V.tensor_tensor(t_lo[:, q % 2, :], bank[q % 2][:, :], t_hi[:, q % 2, :].bitcast(F32),
                                    ALU.subtract).then_inc(t_ready, 1)

                def y_part(t, q):
                    dve.wait_ge(y_high, J * t + q + 1)
                    V.tensor_tensor(y_lo[:, q, :], bank[4 + q % 2][:, :], y_hi[:, q, :].bitcast(F32),
                                    ALU.subtract).then_inc(y_ready, 1)

                def turn(t, more):
                    for g in range(SUBS):
                        dve.wait_ge(z_high, SUBS * t + g + 1)
                        dst = z_lo[:, :, P * g:P * (g + 1)].rearrange("p j (b o) -> p b j o", b=GB)
                        hi = z_hi[:, :, P * g:P * (g + 1)].bitcast(F32).rearrange("p j (b o) -> p b j o", b=GB)
                        src = bank[g][:, :].rearrange("p (b j o) -> p b j o", b=GB, j=J)
                        V.tensor_tensor(dst, src, hi, ALU.subtract).then_inc(z_ready, 1)
                    if more:
                        first_matrix(t + 1, 0)
                    if L == 0:
                        for c in range(NF):
                            m = FCH[c][1]
                            dve.wait_ge(act_done, NF * t + c + 1)
                            dve.wait_ge(second_ready, NF * t + c + 1)
                            V.tensor_tensor(hid[0:m, c % NH, :], hid[0:m, c % NH, :], bank[2 * (c % 2) + 1][0:m, :],
                                            ALU.mult).then_inc(mul_done, 1)
                            dve.wait_ge(mul_done, NF * t + c + 1)
                            hidden(t, c, m)
                            if more and c < STEPS:
                                compose_part(t + 1, c)
                    else:
                        for q in range(2):
                            t_part(t, q)
                        for h in range(HEADS + 2):
                            if h < HEADS:
                                dve.wait_ge(act_done, HEADS * t + h + 1)
                                hidden(t, h, P)
                            if h % 4 == 2 and 2 + h // 4 < J:
                                t_part(t, 2 + h // 4)
                            if more and h % 2 == 1 and h // 2 < STEPS:
                                compose_part(t + 1, h // 2)
                            if h >= 5 and (h - 5) % 4 == 0:
                                y_part(t, (h - 5) // 4)
                    for s in range(SUBS):
                        src = bank[4 + s if L == 0 else (6, 7, 0, 1)[s]]
                        dve.wait_ge(acc_ready, SUBS * t + s + 1)
                        dve.wait_ge(res_in[s % NR], 16 * (SUBS // NR * t + s // NR + 1))
                        V.tensor_tensor(res[:, s % NR, :], src[:, :], res[:, s % NR, :], ALU.add).then_inc(out_ready, 1)

                dve.engine_nop().then_inc(out_ready, 1)
                first_matrix(0, 0)
                for n in range(STEPS):
                    compose_part(0, n)
                with dve.Fori(0, TURNS - 1) as t:
                    turn(t, True)
                turn(TURNS - 1, False)


STEP_SQ = 12
STEP_SUMS = 13
STEP_TAB = 26
STEP_A4 = 27
STEP_X = 41
STEP_1 = 47
STEP_Z = 63
STEP_VB = 77
STEP_O = 79
STEP_EDGE = 81


def layouts(x, cond_512, w, perm, L1_ffn_up, L1_ffn_down, L0_ffn_w_gate_up, L0_ffn_w_down):
    f = np.float32
    a = {}
    a["x0"] = x.reshape(BATCH, CH, NBLK, J).transpose(0, 1, 3, 2)
    ends = np.stack([x[:, :, 0:2 * J], x[:, :, LEN - 2 * J:]], 2)
    a["xe0"] = ends.reshape(GROUPS, GB * CH, 2, 2 * J).transpose(1, 0, 2, 3)
    a["cond"] = cond_512.T
    per = {k: [] for k in ("modw", "modb", "bias", "wio", "bd", "lift1", "w2r", "lift3a", "lift3b", "w4")}
    for weights, biases, mod_w, mod_b in w:
        per["modw"].append(np.tile(mod_w.transpose(2, 0, 1), (1, 1, J)))
        per["modb"].append(np.tile(mod_b.T, (J, 1)))
        per["bias"].append(np.tile(biases.T, (GB, 1)))
        per["wio"].append(weights.transpose(2, 0, 3, 1))
        bd = np.zeros((P, LAYERS * KT, P), f)
        for l in range(LAYERS):
            for k in range(KT):
                m = weights[l, :, :, k] if l == 1 else weights[l, :, :, k].T
                for g in range(GB):
                    bd[g * CH:(g + 1) * CH, l * KT + k, g * CH:(g + 1) * CH] = m
        per["bd"].append(bd)
        lift1 = np.zeros((KT, CH, TQ, CH), f)
        for k4 in range(KT):
            for k3 in range(KT):
                lift1[k4, :, k4 + k3, :] = weights[2, :, :, k3]
        per["lift1"].append(lift1.reshape(KT * CH, TQ * CH))
        per["w2r"].append(np.tile(weights[1].transpose(1, 2, 0), (J, 1, 1)))
        lift3 = np.zeros((TL, CH, TU, CH), f)
        for la in range(TL):
            for u in range(TU):
                k1 = (4 - u) - (la - 3) + 1
                if 0 <= k1 < KT:
                    lift3[la, :, u, :] = weights[0, :, :, k1]
        lift3 = lift3.reshape(TL * CH, TU * CH)
        per["lift3a"].append(lift3[:P])
        per["lift3b"].append(lift3[P:])
        per["w4"].append(weights[3].transpose(2, 1, 0).reshape(KT * CH, CH))
    for k, v in per.items():
        a[k] = np.stack(v)
    c = compose_coefficients()
    coef = np.zeros((P, 2, KT, TL), f)
    coef[:, 0] = np.repeat(c[:4], CH, 0)
    coef[:CH, 1] = c[4]
    a["coef"] = coef
    pick = np.zeros((2, SEG, P), f)
    pick[:, 0, P - 2] = 1
    pick[:, 1, P - 1] = 1
    pick[:, 2, :INNER] = 1
    a["pick"] = pick.reshape(2 * SEG, P)
    a["ident"] = np.eye(P, dtype=f)
    block_of = np.array(list(range(1, NBLK - 1)) + [0, NBLK - 1])
    pos = block_of[:, None] * J + np.arange(J)[None]
    a["gu"] = L0_ffn_w_gate_up.T[pos].transpose(1, 0, 2)
    natural = (np.arange(NBLK)[None] * J + np.arange(J)[:, None]).reshape(-1)
    a["dn"] = L0_ffn_w_down.T[:, natural]
    up = np.zeros((HPQ, CH, HEADS, HM), f)
    hd = np.zeros((HM, HEADS, HPQ, CH), f)
    for h in range(HEADS):
        up[h % HPQ, :, h] = L1_ffn_up[h]
        hd[:, h, h % HPQ] = L1_ffn_down[h]
    a["up"] = up.reshape(P, HEADS, HM)
    a["hd"] = hd.reshape(HM, HEADS, P)
    a["perm_row"] = perm.reshape(1, LEN)
    a["perm_col"] = perm.reshape(J, P).T
    a["pos_row"] = natural.astype(f).reshape(1, LEN)
    a["pos_col"] = pos.astype(f)
    return a, natural


def kernel(x, cond_512, L0_cond_weights, L0_cond_biases, L0_cond_mod_w, L0_cond_mod_b, L0_ffn_w_gate_up,
           L0_ffn_w_down, L1_cond_weights, L1_cond_biases, L1_cond_mod_w, L1_cond_mod_b, L1_ffn_up,
           L1_ffn_down, L1_ffn_perm):
    import concourse.bacc as bacc
    from concourse.bass_utils import run_bass_kernel_spmd

    w = [(L0_cond_weights, L0_cond_biases, L0_cond_mod_w, L0_cond_mod_b),
         (L1_cond_weights, L1_cond_biases, L1_cond_mod_w, L1_cond_mod_b)]
    w = [tuple(np.asarray(v) for v in layer) for layer in w]
    arrays, natural = layouts(np.asarray(x), np.asarray(cond_512), w, np.asarray(L1_ffn_perm),
                              np.asarray(L1_ffn_up), np.asarray(L1_ffn_down),
                              np.asarray(L0_ffn_w_gate_up), np.asarray(L0_ffn_w_down))
    nc = bacc.Bacc("TRN2", target_bir_lowering=False, num_devices=1, dynamic_dma_scratch_size=1024)
    ins, d = {}, {}
    for name, v in arrays.items():
        v = np.ascontiguousarray(v)
        ins[f"in_{name}"] = v
        d[name] = nc.dram_tensor(f"in_{name}", v.shape, mybir.dt.from_np(v.dtype), kind="ExternalInput").ap()
    out = nc.dram_tensor("out_y", [BATCH, CH, J, NBLK], F32, kind="ExternalOutput").ap()
    build(nc, d, out)
    r = run_bass_kernel_spmd(nc, [ins], core_ids=[0])
    y = r.results[0]["out_y"]
    return np.ascontiguousarray(y.transpose(0, 1, 3, 2)).reshape(BATCH, CH, LEN)
```

```python
from contextlib import ExitStack

import numpy as np
import concourse.bass as bass
from concourse import mybir

F32 = mybir.dt.float32
F32R = mybir.dt.float32r
I32 = mybir.dt.int32
ALU = mybir.AluOpType
ACT = mybir.ActivationFunctionType

BATCH, CH, LEN = 128, 32, 512
P = 128
J = 4
NBLK = LEN // J
STYLE = 64
KT = 3
LAYERS = 4
SCALE = float(1.0 / np.sqrt(CH * KT ** 2))
EPS = 1e-8
BLUR = [0.125, 0.375, 0.375, 0.125]

TB = 16
TOK = TB * CH
TURNS = BATCH // TB
GB = 4
GROUPS = BATCH // GB
SUBS = TB // GB
HB = TB // 2
HN = HB * CH
INNER = NBLK - 2

TQ, TL, TU = 5, 7, 9
WINDOWS = 3 * J

FF = 1376
FCH = [(c, min(P, FF - c)) for c in range(0, FF, P)]
NF = len(FCH)
HEADS, HM = 16, 128
HPQ = P // CH

SEG = 3
NX, N1, NY, NZ, NV, NVB = 12, 10, 17, 14, 12, 9

A0, A1, A2, A3, D3, D1, S2, S3 = range(8)
NTAB = 8


def compose_coefficients():
    kb = np.convolve(np.array(BLUR), np.array(BLUR)) * 2.0
    c = np.zeros((TQ, KT, TL), np.float32)
    for q in range(TQ):
        for k in range(KT):
            for la in range(TL):
                at = 2 * (la - 3) + 4 + k - q
                if 0 <= at < len(kb):
                    c[q, k, la] = kb[at]
    return c


class Sems:

    def __init__(self, ctx, nc, L):
        def sem(name):
            return ctx.enter_context(nc.semaphore(f"{name}_{L}"))

        self.style_in = sem("style_in")
        self.lift_in = sem("lift_in")
        self.net_in = sem("net_in")
        self.vec = sem("vec")
        self.roots = sem("roots")
        self.prods = sem("prods")
        self.net = sem("net")
        self.a4_out = sem("a4_out")
        self.edge_out = sem("edge_out")
        self.piece_in = [sem(f"piece_in{i}") for i in range(4)]
        self.piece_hi = sem("piece_hi")
        self.piece_lo = sem("piece_lo")
        self.x_in = sem("x_in")
        self.rows_in = sem("rows_in")
        self.a4_in = sem("a4_in")
        self.res_in = [sem(f"res_in{s}") for s in range(SUBS)]
        self.out_done = [sem(f"out_done{s}") for s in range(SUBS)]
        self.e_in = [sem(f"e_in{hh}") for hh in range(2)]
        self.conv_ready = sem("conv_ready")
        self.z_high = sem("z_high")
        self.z_ready = sem("z_ready")
        self.seed = sem("seed")
        self.lifted = sem("lifted")
        self.kept = sem("kept")
        self.first_ready = sem("first_ready")
        self.act_done = sem("act_done")
        self.acc_ready = sem("acc_ready")
        self.out_ready = sem("out_ready")
        if L == 0:
            self.second_ready = sem("second_ready")
            self.mul_done = sem("mul_done")
            self.high_done = sem("high_done")
            self.hid_ready = sem("hid_ready")
            self.down_done = sem("down_done")
            self.ends_kept = sem("ends_kept")
        else:
            self.onehot = sem("onehot")
            self.perm_ready = sem("perm_ready")
            self.t_high = sem("t_high")
            self.t_ready = sem("t_ready")
            self.sum_ready = sem("sum_ready")
            self.y_high = sem("y_high")
            self.y_ready = sem("y_ready")


OUT0 = 3
E_DMAS = J * J
STEPS = 6

STEP_SQ, STEP_SUMS, STEP_TAB, STEP_A4 = 11, 12, 25, 26
STEP_LIFT = 36
STEP_X, STEP_1, STEP_Y, STEP_Z, STEP_VB, STEP_O, STEP_EDGE = 50, 56, 66, 72, 86, 88, 90


def net_chunks(size):
    return [(g, min(size, GROUPS - g)) for g in range(0, GROUPS, size)]


def build(nc, d, out):
    x1_dram = nc.dram_tensor("x1_scratch", [BATCH, CH, J, NBLK], F32, kind="Internal").ap()
    x_of = [d["x0"], x1_dram]
    y_of = [x1_dram, out]
    a4_dram = [nc.dram_tensor(f"a4_rows_{L}", [BATCH, CH], F32, kind="Internal").ap() for L in range(2)]
    edge_dram = [nc.dram_tensor(f"edge_rows_{L}", [2 * SEG, J, GROUPS, GB, CH], F32, kind="Internal").ap()
                 for L in range(2)]
    MM = nc.tensor.matmul
    V = nc.vector

    with ExitStack() as top:
        def sb(name, shape, dt=F32, c=top):
            return c.enter_context(nc.sbuf_tensor(name, shape, dt))

        bank = [top.enter_context(nc.psum_tensor(f"bank{i}", [P, 512], F32)) for i in range(8)]
        sems = [Sems(top, nc, L) for L in range(2)]
        zeroed = top.enter_context(nc.semaphore("zeroed"))
        pick_in = top.enter_context(nc.semaphore("pick_in"))
        pick_ready = top.enter_context(nc.semaphore("pick_ready"))

        xe1 = sb("xe1", [P, GROUPS, 2, 2 * J])
        tab = sb("tab", [P, A3 + 1, BATCH])
        tg = sb("tg", [P, NTAB, GROUPS])
        bt = sb("bt", [P, 3, GROUPS])
        modb = sb("modb", [P, LAYERS])
        bias = sb("bias", [P, LAYERS])
        w2r = sb("w2r", [P, KT, CH])
        coef = sb("coef", [P, 2, KT, TL])
        ident = sb("ident", [P, P])
        a4t = sb("a4t", [BATCH, CH])
        lift1 = sb("lift1", [KT * CH, TQ * CH])
        lift2a = sb("lift2a", [P, TL, CH])
        lift3a = sb("lift3a", [P, TU * CH])
        lift_rest = sb("lift_rest", [P, TU * CH])
        lift3b = lift_rest[0:3 * CH, :]
        lift2b = lift_rest[3 * CH:P, 0:TL * CH].rearrange("p (a b) -> p a b", a=TL)
        w4 = sb("w4", [KT * CH, CH])
        pick = sb("pick", [2 * SEG, P], F32R)
        taps_e = sb("taps_e", [P, WINDOWS, TOK])
        xin = sb("xin", [P, TB, NBLK])
        a4 = sb("a4", [KT * CH, TOK])
        r0_h1b = sb("r0_h1b", [P, HN])
        r0, h1b = r0_h1b[0:KT * CH, :], r0_h1b[KT * CH:P, :]
        h1a = sb("h1a", [P, HN])
        h2a = sb("h2a", [P, HN])
        h2b = sb("h2b", [3 * CH, HN])
        h3 = sb("h3", [P, 3, HN])

        fa = xin[:].rearrange("p b n -> p (b n)")
        fb = taps_e[:, J:2 * J, :].rearrange("p w n -> p (w n)")

        pick_raw = a4[0:2 * SEG, 0:P]

        def by_layer(v):
            return v.rearrange("p (l n) -> p l n", l=LAYERS)

        sj, dj, va = (by_layer(fa[:, n:n + 512]) for n in (0, 512, 1024))
        sq = by_layer(fa[0:CH, 1536:2048])
        modw = by_layer(fb[0:STYLE, 0:512])
        cond = fb[0:STYLE, 512:640]
        wio = fb[0:CH, 640:1024].rearrange("p (l k o) -> p l k o", l=LAYERS, k=KT)
        wsq = fb[0:CH, 1024:1536].rearrange("p (l r o) -> p l r o", l=LAYERS, r=J)
        tab2 = by_layer(fb[:, 1536:2048])

        class Link:

            def __init__(self, eng, vec):
                self.eng, self.vec, self.done = eng, vec, 0

            def __call__(self, ins):
                self.done += 1
                ins.then_inc(self.vec, 1)
                self.eng.wait_ge(self.vec, self.done)

            def at(self, step):
                assert self.done == step, (self.done, step)

        def load_styles(sp, L):
            S = sems[L]
            for dst, src in ((cond, d["cond"]), (modw, d["modw"][L]), (wio, d["wio"][L]),
                             (modb[:], d["modb"][L])):
                sp.dma_start(dst, src).then_inc(S.style_in, 16)

        def load_lifts(sp, L):
            S = sems[L]
            for dst, src in ((w2r[:], d["w2r"][L]), (coef[:], d["coef"]), (w4[:], d["w4"][L]),
                             (bias[:], d["bias"][L]), (ident[:], d["ident"]), (lift1[:], d["lift1"][L]),
                             (lift3a[:], d["lift3a"][L]), (lift3b, d["lift3b"][L])):
                sp.dma_start(dst, src).then_inc(S.lift_in, 16)

        N_STYLE, N_LIFT = 4, 8

        def load_a4(q, L, t):
            q.dma_start(a4[:], a4_dram[L].rearrange("b o -> (b o)")[bass.ds(t * TOK, TOK)]
                        .partition_broadcast(KT * CH)).then_inc(sems[L].a4_in, 16)

        def spread(sp, L, hh):
            for g in range(J):
                tiles = 3 if g == 0 else 2
                for j in range(J):
                    sp.dma_start(taps_e[CH * j:CH * (j + 1), g + j:g + j + J * (tiles - 1) + 1:J,
                                        hh * HN:(hh + 1) * HN],
                                 h3[CH * g:CH * (g + 1), 0:tiles, :]).then_inc(sems[L].e_in[hh], 16)

        def style_products(pe, L, b):
            pe.wait_ge(sems[L].style_in, 16 * N_STYLE)
            for l in range(LAYERS):
                last = MM(b[:, l * BATCH:(l + 1) * BATCH], modw[:, l, :], cond, start=True, stop=True)
            last.then_inc(sems[L].prods, 1)

        def style_sums(pe, L, b):
            pe.wait_ge(sems[L].vec, STEP_SQ)
            for l in range(LAYERS):
                last = MM(b[:, l * BATCH:(l + 1) * BATCH], wsq[:, l, :, :].rearrange("p r o -> p (r o)"),
                          sq[:, l, :], start=True, stop=True)
            last.then_inc(sems[L].prods, 1)

        def style_flip(pe, L, b):
            pe.wait_ge(sems[L].vec, STEP_TAB)
            pe.wait_ge(sems[L].lift_in, 16 * N_LIFT)
            nc.tensor.transpose(b[:, 0:CH], tab2[0:CH, 0, :], ident[0:CH, 0:CH]).then_inc(sems[L].prods, 1)

        def style_root(act, L):
            act.wait_ge(sems[L].vec, STEP_SUMS)
            nc.scalar.activation(dj, va, ACT.Sqrt).then_inc(sems[L].roots, 1)

        def style_factors_1(dve, L, link, b):
            S = sems[L]
            dve.wait_ge(S.style_in, 16 * N_STYLE)
            link(V.tensor_tensor(wio, wio, wio, ALU.mult))
            link(V.tensor_tensor(wsq[:, :, 0, :], wio[:, :, 0, :], wio[:, :, 1, :], ALU.add))
            link(V.tensor_tensor(wsq[:, :, 0, :], wsq[:, :, 0, :], wio[:, :, 2, :], ALU.add))
            link(V.tensor_copy(wsq[:, :, 1, :], wsq[:, :, 0, :]))
            link(V.tensor_copy(wsq[:, :, 2:4, :], wsq[:, :, 0:2, :]))
            link(V.tensor_scalar(modb[:], modb[:], SCALE, None, ALU.mult))
            dve.wait_ge(S.prods, 1)
            for l in range(LAYERS):
                link(V.tensor_scalar(sj[:, l, :], b[:, l * BATCH:(l + 1) * BATCH], SCALE,
                                     modb[:, l:l + 1], ALU.mult, ALU.add))
            link(V.tensor_tensor(sq, sj[0:CH], sj[0:CH], ALU.mult))
            link.at(STEP_SQ)

        def style_factors_2(dve, L, link, b):
            S = sems[L]
            dve.wait_ge(S.prods, 2)
            link(V.tensor_scalar(va, by_layer(b[:, :]), EPS, None, ALU.add))
            link.at(STEP_SUMS)
            dve.wait_ge(S.roots, 1)
            link(V.reciprocal(dj, dj))
            link(V.tensor_tensor(va, va, dj, ALU.mult))
            link(V.tensor_tensor(va, va, dj, ALU.mult))
            link(V.tensor_scalar(va, va, -0.5, 1.5, ALU.mult, ALU.add))
            link(V.tensor_tensor(dj, dj, va, ALU.mult))
            for to, x, y in ((A1, dj[:, 0], dj[:, 1]), (A2, sj[:, 1], sj[:, 2]), (A3, dj[:, 2], sj[:, 3])):
                link(V.tensor_tensor(tab[:, to, :], x, y, ALU.mult))
            for to, x in ((A0, sj[:, 0]), (D3, dj[:, 3]), (D1, dj[:, 1]), (S2, sj[:, 2]), (S3, sj[:, 3])):
                link(V.tensor_copy(tab[:, to, :] if to <= A3 else tab2[:, to - D3, :], x))
            link.at(STEP_TAB)

        def style_factors_3(dve, L, link, b):
            S = sems[L]
            dve.wait_ge(S.prods, 3)
            link(V.tensor_copy(a4t[:], b[:, 0:CH]))
            link.at(STEP_A4)
            dve.wait_ge(S.lift_in, 16 * N_LIFT)
            for lift, which, p0, m in ((lift2a[:], 0, 0, P), (lift2b, 1, 3 * CH, CH)):
                t = h1a[p0:p0 + m, 0:TL * CH].rearrange("p (a b) -> p a b", a=TL)
                for k in range(KT):
                    w = w2r[p0:p0 + m, k, :].unsqueeze(1).to_broadcast([m, TL, CH])
                    f = coef[p0:p0 + m, which, k, :].unsqueeze(2).to_broadcast([m, TL, CH])
                    if k == 0:
                        link(V.tensor_tensor(lift, w, f, ALU.mult))
                    else:
                        link(V.tensor_tensor(t, w, f, ALU.mult))
                        link(V.tensor_tensor(lift, lift, t, ALU.add))
            link.at(STEP_LIFT)

        def style_factors_4(dve, L, link):
            for r in range(GB):
                q = slice(CH * r, CH * (r + 1))
                link(V.tensor_copy(tg[q, 0:D3, :], tab[q, :, r::GB]))
                link(V.tensor_copy(tg[q, D3:NTAB, :], tab2[q, :, r::GB]))
            for n, f in enumerate((D1, S2, S3)):
                link(V.tensor_scalar(bt[:, n, :], tg[:, f, :], bias[:, n:n + 1], None, ALU.mult))

        def step(pe, L, t, n, banks):
            S = sems[L]
            a, b = banks
            hh, st = divmod(n, 3)
            if n > 0:
                pe.wait_ge(S.kept, STEPS * t + n)
            if st == 0:
                pe.wait_ge(S.seed, 4 * t + 2 * (hh + 1))
                MM(a[:, 0:HN], lift1[:, 0:P], r0, start=True, stop=True)
                last = MM(a[0:CH, HN:2 * HN], lift1[:, P:P + CH], r0, start=True, stop=True)
            if st == 1:
                la, lb = (x.rearrange("p a b -> p (a b)") for x in (lift2a[:], lift2b))
                for c0, m, at in ((0, P, 0), (P, 3 * CH, HN)):
                    MM(a[0:m, at:at + HN], la[:, c0:c0 + m], h1a[:], start=True, stop=False)
                    last = MM(a[0:m, at:at + HN], lb[:, c0:c0 + m], h1b, start=False, stop=True)
            if st == 2:
                for c0, at in ((0, 0), (P, HN)):
                    MM(a[:, at:at + HN], lift3a[:, c0:c0 + P], h2a[:], start=True, stop=False)
                    MM(a[:, at:at + HN], lift3b[:, c0:c0 + P], h2b[:], start=False, stop=True)
                last = MM(b[0:CH, 0:HN], lift3a[:, 2 * P:2 * P + CH], h2a[:], start=True, stop=True)
            last.then_inc(S.lifted, 1)

        def first_matrix(dve, L, t, hh):
            S = sems[L]
            f = tab[0:KT * CH, A3, bass.ds(t * TB + hh * HB, HB)].unsqueeze(2).to_broadcast([KT * CH, HB, CH])
            w = w4[:].unsqueeze(1).to_broadcast([KT * CH, HB, CH])
            V.tensor_tensor(r0.rearrange("p (b o) -> p b o", b=HB), w, f, ALU.mult).then_inc(S.seed, 1)
            dve.wait_ge(S.a4_in, 16 * t + 16)
            dve.wait_ge(S.seed, 4 * t + 2 * hh + 1)
            V.tensor_tensor(r0, r0, a4[:, hh * HN:(hh + 1) * HN], ALU.mult).then_inc(S.seed, 1)

        def keep(dve, L, t, n, banks):
            S = sems[L]
            a, b = banks
            hh, st = divmod(n, 3)
            dve.wait_ge(S.lifted, STEPS * t + n + 1)
            if st == 2 and not (isinstance(t, int) and t == 0 and hh == 0):
                dve.wait_ge(S.e_in[1 - hh], 16 * E_DMAS * t + 16 * E_DMAS * hh)
            tiles = {0: ((h1a[:], a, 0, P), (h1b, a, HN, CH)),
                     1: ((h2a[:], a, 0, P), (h2b[:], a, HN, 3 * CH)),
                     2: ((h3[:, 0, :], a, 0, P), (h3[:, 1, :], a, HN, P), (h3[0:CH, 2, :], b, 0, CH))}[st]
            for dst, src, at, m in tiles:
                f = tab[0:m, (A2, A1, A0)[st], bass.ds(t * TB + hh * HB, HB)].unsqueeze(2).to_broadcast([m, HB, CH])
                last = V.tensor_tensor(dst.rearrange("p (b o) -> p b o", b=HB),
                                       src[0:m, at:at + HN].rearrange("p (b o) -> p b o", b=HB), f, ALU.mult)
            last.then_inc(S.kept, 1)
            if n == 0:
                first_matrix(dve, L, t, 1)

        def net_tiles(L, c):
            wide = GROUPS * SEG
            one = sb(f"net_one_{L}", [P, wide * NY], F32, c)
            two = sb(f"net_two_{L}", [P, wide * NZ], F32, c)
            ta = sb(f"net_ta_{L}", [P, wide * NZ], F32, c)

            def view(t, n):
                return t[:, 0:wide * n].rearrange("p (g s n) -> p g s n", g=GROUPS, s=SEG)

            T = {"nx": view(one, NX), "n1": view(two, N1), "ny": view(one, NY), "nz": view(two, NZ),
                 "nv": view(one, NV), "nvb": view(two, NVB), "ta": ta, "view": view,
                 "no": ta[:, 0:SEG * P].rearrange("p (s j g) -> p s g j", s=SEG, j=J),
                 "bd": sb(f"bd_{L}", [P, LAYERS * KT, P], F32, c),
                 "ehi": sb(f"ehi_{L}", [P, SEG, P], F32R, c),
                 "elo": sb(f"elo_{L}", [P, SEG, P], F32R, c)}
            return T

        NB1, NB2, NB3, NB4, NBF = (0, 1), (2, 3, 6, 7), (0, 1, 2, 3), 6, 7

        def net_products(pe, L, T, stage):
            S = sems[L]
            bd = T["bd"]

            def taps(dst, l, ks, moving):
                for n, (k, src) in enumerate(zip(ks, moving)):
                    last = MM(dst, bd[:, l * KT + k, :], src, start=(n == 0), stop=(n == len(ks) - 1))
                last.then_inc(S.net, 1)

            def win(t, g0, gn, a, n):
                return T[t][:, g0:g0 + gn, :, a:a + n].rearrange("p g s n -> p (g s) n")

            def cols(b, gn, n):
                return bank[b][:, 0:gn * SEG * n].rearrange("p (g n) -> p g n", n=n)

            if stage == 1:
                pe.wait_ge(S.net_in, 16 * (2 if L == 0 else 1))
                pe.wait_ge(S.vec, STEP_X)
                for c, (g0, gn) in enumerate(net_chunks(16)):
                    taps(cols(NB1[c], gn, N1), 0, range(KT), [win("nx", g0, gn, k, N1) for k in range(KT)])
            if stage == 2:
                pe.wait_ge(S.vec, STEP_1)
                for c, (g0, gn) in enumerate(net_chunks(16)):
                    taps(cols(NB2[2 * c], gn, 9), 1, (0, 2), [win("n1", g0, gn, 1, 9), win("n1", g0, gn, 0, 9)])
                    taps(cols(NB2[2 * c + 1], gn, 8), 1, (1,), [win("n1", g0, gn, 1, 8)])
            if stage == 3:
                pe.wait_ge(S.vec, STEP_Z)
                for c, (g0, gn) in enumerate(net_chunks(8)):
                    taps(cols(NB3[c], gn, NV), 2, range(KT), [win("nz", g0, gn, k, NV) for k in range(KT)])
            if stage == 4:
                pe.wait_ge(S.vec, STEP_VB)
                dst = bank[NB4][:, 0:SEG * P].rearrange("p (s g j) -> p g s j", s=SEG, j=J)
                taps(dst, 3, range(KT), [T["nvb"][:, :, :, k:k + 7:2] for k in range(KT)])
            if stage == 5:
                pe.wait_ge(S.vec, STEP_O)
                for s in range(SEG):
                    last = nc.tensor.transpose(bank[NBF][:, s * P:(s + 1) * P],
                                               T["ta"][:, s * P:(s + 1) * P], ident[:])
                last.then_inc(S.net, 1)

        def net_values(dve, L, T, link, stage):
            S = sems[L]

            def evacuate(b, dst, g0, gn, n, fa_, fb_):
                src = bank[b][:, 0:gn * SEG * n].rearrange("p (g s n) -> p g s n", g=gn, s=SEG)
                x = tg[:, fa_, g0:g0 + gn].unsqueeze(2).unsqueeze(3).to_broadcast([P, gn, SEG, n])
                y = bt[:, fb_, g0:g0 + gn].unsqueeze(2).unsqueeze(3).to_broadcast([P, gn, SEG, n])
                link(V.tensor_tensor(dst, src, x, ALU.mult))
                link(V.tensor_tensor(dst, dst, y, ALU.add))

            def blur(dst, src, n, gain):
                w = [src[:, :, :, t:t + n].rearrange("p g s n -> p (g s) n") for t in range(4)]
                o = dst[:, :, :, 0:n].rearrange("p g s n -> p (g s) n")
                u = T["view"](T["ta"], n).rearrange("p g s n -> p (g s) n")
                link(V.tensor_tensor(u, w[1], w[2], ALU.add))
                link(V.tensor_scalar(u, u, gain * BLUR[1], None, ALU.mult))
                link(V.tensor_tensor(o, w[0], w[3], ALU.add))
                link(V.scalar_tensor_tensor(o, o, gain * BLUR[0], u, ALU.mult, ALU.add))

            nx, n1, ny, nz, nv, nvb, no = (T[k] for k in ("nx", "n1", "ny", "nz", "nv", "nvb", "no"))
            if stage == 0:
                if L == 0:
                    dve.wait_ge(S.net_in, 32)
                link(V.memset(nx[:, :, :, :], 0.0))
                s0 = tg[:, A0, :].unsqueeze(2).to_broadcast([P, GROUPS, 2 * J])
                link(V.tensor_tensor(nx[:, :, 0, 4:12], xe1[:, :, 0, :], s0, ALU.mult))
                link(V.tensor_tensor(nx[:, :, 1, 0:8], xe1[:, :, 1, :], s0, ALU.mult))
                link.at(STEP_X)
            if stage == 1:
                for c, (g0, gn) in enumerate(net_chunks(16)):
                    dve.wait_ge(S.net, c + 1)
                    evacuate(NB1[c], n1[:, g0:g0 + gn, :, :], g0, gn, N1, A1, 0)
                link(V.memset(n1[:, :, 0, 0:3], 0.0))
                link(V.memset(n1[:, :, 1, 7:10], 0.0))
                link.at(STEP_1)
            if stage == 2:
                for c, (g0, gn) in enumerate(net_chunks(16)):
                    dve.wait_ge(S.net, 2 + 2 * c + 1)
                    evacuate(NB2[2 * c], ny[:, g0:g0 + gn, :, 0:17:2], g0, gn, 9, A2, 1)
                    dve.wait_ge(S.net, 2 + 2 * c + 2)
                    evacuate(NB2[2 * c + 1], ny[:, g0:g0 + gn, :, 1:17:2], g0, gn, 8, A2, 1)
                link(V.memset(ny[:, :, 0, 0:4], 0.0))
                link(V.memset(ny[:, :, 1, 13:17], 0.0))
                link.at(STEP_Y)
            if stage == 3:
                blur(nz, ny, NZ, 2.0)
                link(V.memset(nz[:, :, 0, 0:3], 0.0))
                link(V.memset(nz[:, :, 1, 11:14], 0.0))
                link.at(STEP_Z)
            if stage == 4:
                for c, (g0, gn) in enumerate(net_chunks(8)):
                    dve.wait_ge(S.net, 6 + c + 1)
                    evacuate(NB3[c], nv[:, g0:g0 + gn, :, :], g0, gn, NV, A3, 2)
                link(V.memset(nv[:, :, 0, 0:2], 0.0))
                link(V.memset(nv[:, :, 1, 10:12], 0.0))
                blur(nvb, nv, NVB, 1.0)
                link.at(STEP_VB)
            if stage == 5:
                dve.wait_ge(S.net, 11)
                src = bank[NB4][:, 0:SEG * P].rearrange("p (s g j) -> p s g j", s=SEG, j=J)
                d3 = tg[:, D3, :].unsqueeze(1).unsqueeze(3).to_broadcast([P, SEG, GROUPS, J])
                link(V.tensor_tensor(no, src, d3, ALU.mult))
                link(V.tensor_scalar(no, no, bias[:, 3:4], None, ALU.add))
                link.at(STEP_O)
            if stage == 6:
                dve.wait_ge(S.net, 12)
                src = bank[NBF][:, 0:SEG * P].rearrange("p (s n) -> p s n", s=SEG)
                link(V.tensor_copy(T["ehi"][:], src))
                link(V.tensor_tensor(T["elo"][:], src, T["ehi"][:].bitcast(F32), ALU.subtract))
                link.at(STEP_EDGE)

        def store_edges(sp, L, T):
            sp.wait_ge(sems[L].vec, STEP_EDGE)
            for part, tile in enumerate((T["ehi"], T["elo"])):
                for s in range(SEG):
                    sp.dma_start(edge_dram[L][part * SEG + s].rearrange("j g b o -> (j g) (b o)"),
                                 tile[:, s, :].bitcast(F32)).then_inc(sems[L].edge_out, 16)
            sp.wait_ge(sems[L].edge_out, 16 * 2 * SEG)

        def load_x(sp, L, t):
            for j in range(J):
                sp.dma_start(xin[CH * j:CH * (j + 1), :, :],
                             x_of[L][bass.ds(t * TB, TB), :, j, :].rearrange("b c n -> c b n")
                             ).then_inc(sems[L].x_in, 16)

        def load_rows(sp, L, t, rows):
            for j in range(J):
                sp.dma_start(rows[:].bitcast(F32).rearrange("r g (b j o) -> r (g b) j o", b=GB, j=J)[:, :, j, :],
                             edge_dram[L][:, j, bass.ds(t * SUBS, SUBS), :, :].rearrange("r g b o -> r (g b) o")
                             ).then_inc(sems[L].rows_in, 16)

        def load_res(sp, L, t, s, res):
            NR = res.shape[1]
            x_rows = x_of[L].rearrange("b c j n -> (b c) (j n)")
            sp.dma_start(res[:, s % NR, :], x_rows[bass.ds(t * TOK + s * P, P), :]).then_inc(sems[L].res_in[s % NR], 16)

        def store_out(sp, L, t, s, res):
            NR = res.shape[1]
            y_rows = y_of[L].rearrange("b c j n -> (b c) (j n)")
            sp.wait_ge(sems[L].out_ready, SUBS * t + s + 1 + OUT0)
            sp.dma_start(y_rows[bass.ds(t * TOK + s * P, P), :], res[:, s % NR, :]).then_inc(sems[L].out_done[s % NR], 16)

        def reload_res(sp, L, t, s, res):
            NR = res.shape[1]
            if L == 0:
                sp.wait_ge(sems[L].ends_kept, SUBS * t + s + 1)
            sp.wait_ge(sems[L].out_done[s % NR], 16 * (SUBS // NR * t + s // NR + 1))
            load_res(sp, L, *((t, s + NR) if s + NR < SUBS else (t + 1, s + NR - SUBS)), res)

        def sync_turn(sp, L, t, rows, res):
            S = sems[L]
            NR = res.shape[1]
            sp.wait_ge(S.conv_ready, SUBS * t + SUBS)
            load_x(sp, L, t + 1)
            load_rows(sp, L, t + 1, rows)
            for hh in range(2):
                sp.wait_ge(S.kept, STEPS * t + STEPS + 3 * (hh + 1))
                spread(sp, L, hh)
            for s in range(SUBS):
                store_out(sp, L, t, s, res)
                reload_res(sp, L, t, s, res)

        def convolve(pe, L, t, rows):
            S = sems[L]
            pe.wait_ge(S.x_in, 16 * J * t + 16 * J)
            pe.wait_ge(S.rows_in, 16 * J * t + 16 * J)
            for g in range(SUBS):
                if g % 2 == 0:
                    pe.wait_ge(S.e_in[g // 2], 16 * E_DMAS * t + 16 * E_DMAS)
                MM(bank[g][:, :], pick[:], rows[:, g, :], start=True, stop=False)
                for bb in range(GB):
                    b = GB * g + bb
                    dst = bank[g][0:INNER, P * bb:P * (bb + 1)].rearrange("p (j o) -> p j o", j=J)
                    for s in (-1, 0, 1):
                        last = MM(dst, xin[:, b, 1 + s:1 + s + INNER],
                                  taps_e[:, J * (1 - s):J * (2 - s), CH * b:CH * (b + 1)],
                                  start=False, stop=(bb == GB - 1 and s == 1))
                last.then_inc(S.conv_ready, 1)

        def three(dst, w_hi, w_lo, m_hi, m_lo, first, final):
            MM(dst, w_hi, m_hi, start=first, stop=False)
            MM(dst, w_hi, m_lo, start=False, stop=False)
            return MM(dst, w_lo, m_hi, start=False, stop=final)

        def z_view(z, g):
            return z[:, :, P * g:P * (g + 1)].rearrange("p j (b o) -> p b j o", b=GB)

        def z_bank(g):
            return bank[g][:, :].rearrange("p (b j o) -> p b j o", b=GB, j=J)

        def z_high_parts(act, L, t, z_hi):
            for g in range(SUBS):
                act.wait_ge(sems[L].conv_ready, SUBS * t + g + 1)
                nc.scalar.activation(z_view(z_hi, g), z_bank(g), ACT.Copy).then_inc(sems[L].z_high, 1)

        def z_low_parts(dve, L, t, z_hi, z_lo):
            for g in range(SUBS):
                dve.wait_ge(sems[L].z_high, SUBS * t + g + 1)
                V.tensor_tensor(z_view(z_lo, g), z_bank(g), z_view(z_hi, g).bitcast(F32),
                                ALU.subtract).then_inc(sems[L].z_ready, 1)

        def add_residual(dve, L, t, res, banks):
            S = sems[L]
            NR = res.shape[1]
            for s in range(SUBS):
                dve.wait_ge(S.acc_ready, SUBS * t + s + 1)
                dve.wait_ge(S.res_in[s % NR], 16 * (SUBS // NR * t + s // NR + 1))
                V.tensor_tensor(res[:, s % NR, :], banks[s][:, :], res[:, s % NR, :], ALU.add).then_inc(S.out_ready, 1)

        with ExitStack() as ctx:
            S, N = sems
            gu_hi = sb("gu_hi", [P, J, 2 * FF], F32R, ctx)
            gu_lo = sb("gu_lo", [P, J, 2 * FF], F32R, ctx)
            dn_hi = sb("dn_hi", [P, NF, LEN], F32R, ctx)
            dn_lo = sb("dn_lo", [P, NF, LEN], F32R, ctx)
            hid = sb("hid", [P, 2, TOK], F32, ctx)
            res = sb("res0", [P, 2, TOK], F32, ctx)
            with ExitStack() as pre:
                T = net_tiles(0, pre)
            rows = sb("rows_0", [2 * SEG, SUBS, 512], F32R, ctx)
            z_hi = sb("z_hi_0", [P, J, TOK], F32R, ctx)
            z_lo = sb("z_lo_0", [P, J, TOK], F32R, ctx)
            hid_hi = sb("hid_hi", [P, 2, TOK], F32R, ctx)
            hid_lo = sb("hid_lo", [P, 2, TOK], F32R, ctx)
            stage = [hid[:, 0, :], hid[:, 1, :], res[:, 0, :], res[:, 1, :]]

            cuts = [(j, a, min(a + 512, 2 * FF)) for j in range(J) for a in range(0, 2 * FF, 512)]
            pieces = [(d["gu"][j, :, a:b], gu_hi[:, j, a:b], gu_lo[:, j, a:b]) for j, a, b in cuts]
            N_GU = len(pieces)
            pieces += [(d["dn"][i0:i0 + m, :], dn_hi[0:m, i, :], dn_lo[0:m, i, :])
                       for i, (i0, m) in enumerate(FCH)]

            BRIDGE_STYLE = {1: 0, 2: 1, 3: 2}
            BRIDGE_STEP = {5: 0, 6: 1, 7: 2, 8: 3, 9: 4, 10: 5}

            def pair(c):
                return bank[2 * (c % 2)], bank[2 * (c % 2) + 1]

            with nc.Block() as block:
                @block.sync
                def _(sp):
                    load_styles(sp, 0)
                    sp.dma_start(pick_raw, d["pick"]).then_inc(pick_in, 16)
                    load_lifts(sp, 0)
                    sp.dma_start(xe1[:], d["xe0"]).then_inc(S.net_in, 16)
                    sp.dma_start(T["bd"][:], d["bd"][0]).then_inc(S.net_in, 16)
                    sp.wait_ge(S.vec, STEP_A4)
                    sp.dma_start(a4_dram[0], a4t[:]).then_inc(S.a4_out, 16)
                    sp.wait_ge(S.a4_out, 16)
                    sp.wait_ge(pick_ready, 1)
                    load_a4(sp, 0, 0)
                    sp.wait_ge(S.vec, STEP_X)
                    load_x(sp, 0, 0)
                    sp.wait_ge(zeroed, 2)
                    for hh in range(2):
                        sp.wait_ge(S.kept, 3 * (hh + 1))
                        spread(sp, 0, hh)
                    store_edges(sp, 0, T)
                    load_rows(sp, 0, 0, rows)
                    sp.wait_ge(S.piece_lo, len(pieces))
                    for s in range(2):
                        load_res(sp, 0, 0, s, res)
                    with sp.Fori(0, TURNS - 1) as t:
                        sync_turn(sp, 0, t, rows, res)
                    t = TURNS - 1
                    sp.wait_ge(S.conv_ready, SUBS * TURNS)
                    load_styles(sp, 1)
                    load_lifts(sp, 1)
                    sp.wait_ge(N.vec, STEP_A4)
                    sp.dma_start(a4_dram[1], a4t[:]).then_inc(N.a4_out, 16)
                    sp.wait_ge(N.a4_out, 16)
                    load_a4(sp, 1, 0)
                    sp.wait_ge(N.kept, 3)
                    spread(sp, 1, 0)
                    for s in range(SUBS):
                        store_out(sp, 0, t, s, res)
                        if s < 2:
                            reload_res(sp, 0, t, s, res)
                    sp.wait_ge(N.kept, 6)
                    spread(sp, 1, 1)

                @block.gpsimd
                def _(pool):
                    for i, (src, hi, lo) in enumerate(pieces):
                        if i == 2:
                            nc.gpsimd.memset(taps_e[:, 0:J, :], 0.0).then_inc(zeroed, 1)
                            nc.gpsimd.memset(taps_e[:, 2 * J:3 * J, :], 0.0).then_inc(zeroed, 1)
                        raw = stage[i % 4][0:hi.shape[0], 0:hi.shape[1]]
                        pool.wait_ge(S.piece_hi, i + 1)
                        nc.gpsimd.tensor_tensor(lo, raw, hi.bitcast(F32), ALU.subtract).then_inc(S.piece_lo, 1)
                    with pool.Fori(0, TURNS) as t:
                        for s in range(SUBS):
                            pool.wait_ge(S.out_ready, SUBS * t + s + 1 + OUT0)
                            tile = res[:, s % 2, :].rearrange("p (j n) -> p n j", j=J)
                            ends = xe1[:, bass.ds(t * SUBS + s, 1), :, :]
                            for e, n0 in ((0, 0), (1, NBLK - 2)):
                                last = nc.gpsimd.tensor_copy(ends[:, 0, e, :].rearrange("p (n j) -> p n j", j=J),
                                                             tile[:, n0:n0 + 2, :])
                            last.then_inc(S.ends_kept, 1)

                @block.tensor
                def _(pe):
                    def gate_up(t, c):
                        i0, m = FCH[c]
                        if c >= 2:
                            pe.wait_ge(S.mul_done, NF * t + c - 1)
                        for which, ready in ((0, S.first_ready), (1, S.second_ready)):
                            col = which * FF + i0
                            dst = pair(c)[which][0:m, :]
                            for j in range(J):
                                last = three(dst, gu_hi[:, j, col:col + m], gu_lo[:, j, col:col + m],
                                             z_hi[:, j, :], z_lo[:, j, :], j == 0, j == J - 1)
                            last.then_inc(ready, 1)

                    def down(t, c):
                        i0, m = FCH[c]
                        pe.wait_ge(S.hid_ready, NF * t + c + 1)
                        for s in range(SUBS):
                            hi = hid_hi[0:m, c % 2, P * s:P * (s + 1)]
                            lo = hid_lo[0:m, c % 2, P * s:P * (s + 1)]
                            last = three(bank[4 + s][:, :], hi, lo, dn_hi[0:m, c, :], dn_lo[0:m, c, :],
                                         c == 0, c == NF - 1)
                            if c == NF - 1:
                                last.then_inc(S.acc_ready, 1)
                        if c < NF - 1:
                            last.then_inc(S.down_done, 1)

                    def turn(t, more):
                        convolve(pe, 0, t, rows)
                        pe.wait_ge(S.out_ready, SUBS * t + OUT0)
                        if more:
                            step(pe, 0, t + 1, 0, (bank[4], bank[5]))
                        pe.wait_ge(S.z_ready, SUBS * t + SUBS)
                        for c in range(NF):
                            if more and 2 <= c <= STEPS:
                                pe.wait_ge(S.kept, STEPS * t + STEPS + c)
                            if not more and c - 1 in BRIDGE_STYLE:
                                pe.wait_ge(N.vec, (STEP_SQ, STEP_SUMS, STEP_A4)[BRIDGE_STYLE[c - 1]])
                            if not more and c - 1 in BRIDGE_STEP:
                                pe.wait_ge(N.kept, BRIDGE_STEP[c - 1] + 1)
                            gate_up(t, c)
                            other = pair(c + 1)
                            if c >= 1:
                                pe.wait_ge(S.mul_done, NF * t + c)
                            if more and 1 <= c < STEPS:
                                step(pe, 0, t + 1, c, other)
                            if not more and c in BRIDGE_STYLE:
                                (style_products, style_sums, style_flip)[BRIDGE_STYLE[c]](pe, 1, other[0])
                            if not more and c in BRIDGE_STEP:
                                step(pe, 1, 0, BRIDGE_STEP[c], other)
                            if c == 1 and more:
                                pe.wait_ge(S.kept, STEPS * t + STEPS + 1)
                            if c >= 1:
                                down(t, c - 1)
                        down(t, NF - 1)

                    style_products(pe, 0, bank[0])
                    style_sums(pe, 0, bank[1])
                    style_flip(pe, 0, bank[2])
                    first = (bank[4], bank[5])
                    step(pe, 0, 0, 0, first)
                    step(pe, 0, 0, 1, first)
                    net_products(pe, 0, T, 1)
                    step(pe, 0, 0, 2, first)
                    step(pe, 0, 0, 3, first)
                    net_products(pe, 0, T, 2)
                    step(pe, 0, 0, 4, first)
                    step(pe, 0, 0, 5, first)
                    net_products(pe, 0, T, 3)
                    net_products(pe, 0, T, 4)
                    net_products(pe, 0, T, 5)
                    pe.wait_ge(pick_ready, 1)
                    pe.wait_ge(S.vec, STEP_EDGE)
                    pe.wait_ge(S.piece_lo, len(pieces))
                    with pe.Fori(0, TURNS - 1) as t:
                        turn(t, True)
                    turn(TURNS - 1, False)

                @block.scalar
                def _(act):
                    def load_piece(i):
                        src, hi, lo = pieces[i]
                        act.dma_start(stage[i % 4][0:hi.shape[0], 0:hi.shape[1]], src).then_inc(S.piece_in[i % 4], 16)

                    for i in range(4):
                        load_piece(i)
                    act.wait_ge(pick_in, 16)
                    nc.scalar.activation(pick[:], pick_raw, ACT.Copy).then_inc(pick_ready, 1)
                    style_root(act, 0)
                    for i, (src, hi, lo) in enumerate(pieces):
                        act.wait_ge(S.piece_in[i % 4], 16 * (i // 4 + 1))
                        nc.scalar.activation(hi, stage[i % 4][0:hi.shape[0], 0:hi.shape[1]],
                                             ACT.Copy).then_inc(S.piece_hi, 1)
                        if i >= 1 and i + 3 < len(pieces):
                            act.wait_ge(S.piece_lo, i)
                            load_piece(i + 3)

                    def turn(t, more):
                        if more:
                            act.wait_ge(S.seed, 4 * t + 4)
                            load_a4(act, 0, t + 1)
                        z_high_parts(act, 0, t, z_hi)
                        for c in range(NF):
                            m = FCH[c][1]
                            act.wait_ge(S.first_ready, NF * t + c + 1)
                            if c >= 2:
                                act.wait_ge(S.hid_ready, NF * t + c - 1)
                            nc.scalar.activation(hid[0:m, c % 2, :], pair(c)[0][0:m, :], ACT.Silu).then_inc(S.act_done, 1)
                            if not more and c == 2:
                                style_root(act, 1)

                    with act.Fori(0, TURNS - 1) as t:
                        turn(t, True)
                    turn(TURNS - 1, False)

                @block.vector
                def _(dve):
                    link = Link(dve, S.vec)
                    style_factors_1(dve, 0, link, bank[0])
                    style_factors_2(dve, 0, link, bank[1])
                    style_factors_3(dve, 0, link, bank[2])
                    first = (bank[4], bank[5])
                    dve.engine_nop().then_inc(S.out_ready, OUT0)
                    first_matrix(dve, 0, 0, 0)
                    style_factors_4(dve, 0, link)
                    keep(dve, 0, 0, 0, first)
                    net_values(dve, 0, T, link, 0)
                    keep(dve, 0, 0, 1, first)
                    net_values(dve, 0, T, link, 1)
                    keep(dve, 0, 0, 2, first)
                    keep(dve, 0, 0, 3, first)
                    net_values(dve, 0, T, link, 2)
                    keep(dve, 0, 0, 4, first)
                    net_values(dve, 0, T, link, 3)
                    keep(dve, 0, 0, 5, first)
                    net_values(dve, 0, T, link, 4)
                    net_values(dve, 0, T, link, 5)
                    net_values(dve, 0, T, link, 6)
                    bridge = Link(dve, N.vec)

                    def hidden(t, c, m):
                        k = c % 2
                        if c >= 2:
                            dve.wait_ge(S.down_done, (NF - 1) * t + c - 1)
                        V.tensor_copy(hid_hi[0:m, k, :], hid[0:m, k, :]).then_inc(S.high_done, 1)
                        dve.wait_ge(S.high_done, NF * t + c + 1)
                        V.tensor_tensor(hid_lo[0:m, k, :], hid[0:m, k, :], hid_hi[0:m, k, :].bitcast(F32),
                                        ALU.subtract).then_inc(S.hid_ready, 1)

                    def turn(t, more):
                        if more:
                            first_matrix(dve, 0, t + 1, 0)
                        z_low_parts(dve, 0, t, z_hi, z_lo)
                        if more:
                            keep(dve, 0, t + 1, 0, (bank[4], bank[5]))
                        for c in range(NF):
                            m = FCH[c][1]
                            dve.wait_ge(S.act_done, NF * t + c + 1)
                            dve.wait_ge(S.second_ready, NF * t + c + 1)
                            V.tensor_tensor(hid[0:m, c % 2, :], hid[0:m, c % 2, :], pair(c)[1][0:m, :],
                                            ALU.mult).then_inc(S.mul_done, 1)
                            dve.wait_ge(S.mul_done, NF * t + c + 1)
                            hidden(t, c, m)
                            other = pair(c + 1)
                            if more and 1 <= c < STEPS:
                                keep(dve, 0, t + 1, c, other)
                            if not more and c in BRIDGE_STYLE:
                                (style_factors_1, style_factors_2, style_factors_3)[BRIDGE_STYLE[c]](
                                    dve, 1, bridge, other[0])
                            if not more and c == 4:
                                style_factors_4(dve, 1, bridge)
                                first_matrix(dve, 1, 0, 0)
                            if not more and c in BRIDGE_STEP:
                                keep(dve, 1, 0, BRIDGE_STEP[c], other)
                        add_residual(dve, 0, t, res, bank[4:8])

                    with dve.Fori(0, TURNS - 1) as t:
                        turn(t, True)
                    turn(TURNS - 1, False)

        with ExitStack() as ctx:
            B, S = sems
            up_hi = sb("up_hi", [P, HEADS, HM], F32R, ctx)
            up_lo = sb("up_lo", [P, HEADS, HM], F32R, ctx)
            hd = sb("hd", [HM, HEADS, CH], F32, ctx)
            gather = sb("gather", [P, J, LEN], F32R, ctx)
            scatter = sb("scatter", [P, J, LEN], F32R, ctx)
            stage = sb("stage", [P, HEADS, HM], F32, ctx)
            prow_i = sb("prow_i", [P, LEN], I32, ctx)
            pcol_i = sb("pcol_i", [P, J], I32, ctx)
            prow = sb("prow", [P, LEN], F32, ctx)
            pcol = sb("pcol", [P, J], F32, ctx)
            posrow = sb("posrow", [P, LEN], F32, ctx)
            poscol = sb("poscol", [P, J], F32, ctx)
            res = sb("res1", [P, SUBS, TOK], F32, ctx)
            with ExitStack() as pre:
                T = net_tiles(1, pre)
            rows = sb("rows_1", [2 * SEG, SUBS, 512], F32R, ctx)
            z_hi = sb("z_hi_1", [P, J, TOK], F32R, ctx)
            z_lo = sb("z_lo_1", [P, J, TOK], F32R, ctx)
            NH = 2 * HPQ
            STEP_AT = {1: 1, 3: 2, 5: 3, 7: 4, 9: 5}
            hid = sb("hid1", [P, NH, TOK], F32, ctx)
            tp = sb("tp", [P, 2, 2, TOK], F32R, ctx)
            y_hi = sb("y_hi", [P, J, TOK], F32R, ctx)
            y_lo = sb("y_lo", [P, J, TOK], F32R, ctx)
            cbanks = (bank[6], bank[7])
            obanks = (bank[0], bank[1], bank[6], bank[7])

            with nc.Block() as block:
                @block.sync
                def _(sp):
                    sp.dma_start(T["bd"][:], d["bd"][1]).then_inc(S.net_in, 16)
                    for s in range(2):
                        sp.wait_ge(B.out_done[s], 16 * 2 * TURNS)
                    load_x(sp, 1, 0)
                    for s in range(SUBS):
                        load_res(sp, 1, 0, s, res)
                    store_edges(sp, 1, T)
                    load_rows(sp, 1, 0, rows)
                    with sp.Fori(0, TURNS - 1) as t:
                        sync_turn(sp, 1, t, rows, res)
                    for s in range(SUBS):
                        store_out(sp, 1, TURNS - 1, s, res)
                    for s in range(SUBS):
                        sp.wait_ge(S.out_done[s], 16 * TURNS)

                @block.gpsimd
                def _(pool):
                    G = nc.gpsimd
                    for i in range(4):
                        h = slice(4 * i, 4 * i + 4)
                        pool.wait_ge(S.piece_hi, i + 1)
                        G.tensor_tensor(up_lo[:, h, :], stage[:, h, :], up_hi[:, h, :].bitcast(F32),
                                        ALU.subtract).then_inc(S.piece_lo, 1)
                    pool.wait_ge(S.piece_in[1], 16 * 4)
                    G.tensor_copy(prow[:], prow_i[:]).then_inc(S.onehot, 1)
                    G.tensor_copy(pcol[:], pcol_i[:]).then_inc(S.onehot, 1)
                    pool.wait_ge(S.onehot, 2)
                    for j in range(J):
                        G.tensor_scalar(gather[:, j, :], prow[:], poscol[:, j:j + 1], None, ALU.is_equal).then_inc(S.onehot, 1)
                    for j in range(J):
                        G.tensor_scalar(scatter[:, j, :], posrow[:], pcol[:, j:j + 1], None, ALU.is_equal).then_inc(S.onehot, 1)

                @block.tensor
                def _(pe):
                    def permute(t, q):
                        if q >= 2:
                            pe.wait_ge(S.t_ready, J * t + q - 1)
                        dst = bank[q % 2][:, :]
                        for j in range(J):
                            w = gather[:, j, P * q:P * (q + 1)]
                            MM(dst, w, z_hi[:, j, :], start=(j == 0), stop=False)
                            last = MM(dst, w, z_lo[:, j, :], start=False, stop=(j == J - 1))
                        last.then_inc(S.perm_ready, 1)

                    def head_up(t, h):
                        q = h // HPQ
                        if h % HPQ == 0:
                            pe.wait_ge(S.t_ready, J * t + q + 1)
                        if h >= 2:
                            pe.wait_ge(S.act_done, HEADS * t + h - 1)
                        pair = h % HPQ // 2
                        own = slice(64 * pair, 64 * pair + 64)
                        MM(bank[2 + h % 2][:, :], up_hi[:, h, :], tp[:, q % 2, pair, :], start=True, stop=False)
                        MM(bank[2 + h % 2][:, :], up_lo[own, h, :], tp[own, q % 2, pair, :],
                           start=False, stop=True).then_inc(S.first_ready, 1)

                    def heads_down(t, q):
                        pe.wait_ge(S.act_done, HEADS * t + HPQ * (q + 1))
                        if q >= 2:
                            pe.wait_ge(S.y_ready, J * t + q - 1)
                        for r in range(HPQ):
                            h = HPQ * q + r
                            last = MM(bank[4 + q % 2][CH * r:CH * (r + 1), :], hd[:, h, :], hid[:, h % NH, :],
                                      start=True, stop=True)
                        last.then_inc(S.sum_ready, 1)

                    def turn(t, more):
                        pe.wait_ge(S.out_ready, SUBS * t + OUT0 - 2)
                        convolve(pe, 1, t, rows)
                        pe.wait_ge(S.out_ready, SUBS * t + OUT0)
                        if more:
                            step(pe, 1, t + 1, 0, cbanks)
                        pe.wait_ge(S.z_ready, SUBS * t + SUBS)
                        permute(t, 0)
                        permute(t, 1)
                        for h in range(HEADS + 2):
                            if h < HEADS:
                                head_up(t, h)
                            if h % 4 == 2 and 2 + h // 4 < J:
                                permute(t, 2 + h // 4)
                            if more and h in STEP_AT:
                                step(pe, 1, t + 1, STEP_AT[h], cbanks)
                            if h >= 5 and h % 4 == 1:
                                heads_down(t, (h - 5) // 4)
                        if more:
                            pe.wait_ge(S.kept, STEPS * t + 2 * STEPS)
                        for qs in (range(J - 1), range(J - 1, J)):
                            for s in range(SUBS):
                                for q in qs:
                                    if s == 0:
                                        pe.wait_ge(S.y_ready, J * t + q + 1)
                                    MM(obanks[s][:, :], y_hi[:, q, P * s:P * (s + 1)], scatter[:, q, :],
                                       start=(q == 0), stop=False)
                                    last = MM(obanks[s][:, :], y_lo[:, q, P * s:P * (s + 1)], scatter[:, q, :],
                                              start=False, stop=(q == J - 1))
                                if q == J - 1:
                                    last.then_inc(S.acc_ready, 1)

                    for n in range(1, 6):
                        net_products(pe, 1, T, n)
                    pe.wait_ge(S.vec, STEP_EDGE)
                    pe.wait_ge(S.kept, STEPS)
                    pe.wait_ge(S.piece_in[2], 16)
                    pe.wait_ge(S.piece_lo, 4)
                    pe.wait_ge(S.onehot, 2 + 2 * J)
                    with pe.Fori(0, TURNS - 1) as t:
                        turn(t, True)
                    turn(TURNS - 1, False)

                def t_tail(t, q, act=None, dve=None):
                    if act is not None:
                        act.wait_ge(S.perm_ready, J * t + q + 1)
                        if q >= 2:
                            act.wait_ge(S.first_ready, HEADS * t + HPQ * (q - 1))
                        for pair in range(2):
                            own = slice(64 * pair, 64 * pair + 64)
                            nc.scalar.activation(tp[own, q % 2, pair, :], bank[q % 2][own, :], ACT.Copy).then_inc(S.t_high, 1)
                    else:
                        for pair in range(2):
                            own = slice(64 * pair, 64 * pair + 64)
                            rest = slice(64 - 64 * pair, P - 64 * pair)
                            dve.wait_ge(S.t_high, 2 * J * t + 2 * q + pair + 1)
                            last = V.tensor_tensor(tp[rest, q % 2, pair, :], bank[q % 2][own, :],
                                                   tp[own, q % 2, pair, :].bitcast(F32), ALU.subtract)
                        last.then_inc(S.t_ready, 1)

                @block.scalar
                def _(act):
                    act.dma_start(hd[:], d["hd"]).then_inc(S.piece_in[2], 16)
                    act.dma_start(stage[:], d["up"]).then_inc(S.piece_in[0], 16)
                    for dst, src in ((prow_i[:], d["perm_row"].partition_broadcast(P)), (pcol_i[:], d["perm_col"]),
                                     (posrow[:], d["pos_row"].partition_broadcast(P)), (poscol[:], d["pos_col"])):
                        act.dma_start(dst, src).then_inc(S.piece_in[1], 16)
                    act.wait_ge(S.piece_in[0], 16)
                    for i in range(4):
                        h = slice(4 * i, 4 * i + 4)
                        nc.scalar.activation(up_hi[:, h, :], stage[:, h, :], ACT.Copy).then_inc(S.piece_hi, 1)

                    def turn(t, more):
                        if more:
                            act.wait_ge(S.seed, 4 * t + 4)
                            load_a4(act, 1, t + 1)
                        z_high_parts(act, 1, t, z_hi)
                        for q in range(2):
                            t_tail(t, q, act=act)
                        for h in range(HEADS + 2):
                            if h < HEADS:
                                act.wait_ge(S.first_ready, HEADS * t + h + 1)
                                if h >= NH:
                                    act.wait_ge(S.sum_ready, J * t + h // HPQ - 1)
                                nc.scalar.activation(hid[:, h % NH, :], bank[2 + h % 2][:, :], ACT.Gelu).then_inc(S.act_done, 1)
                            if h % 4 == 2 and 2 + h // 4 < J:
                                t_tail(t, 2 + h // 4, act=act)
                            if h >= 5 and h % 4 == 1:
                                q = (h - 5) // 4
                                act.wait_ge(S.sum_ready, J * t + q + 1)
                                nc.scalar.activation(y_hi[:, q, :], bank[4 + q % 2][:, :], ACT.Copy).then_inc(S.y_high, 1)

                    with act.Fori(0, TURNS - 1) as t:
                        turn(t, True)
                    turn(TURNS - 1, False)

                @block.vector
                def _(dve):
                    link = Link(dve, S.vec)
                    link.done = STEP_LIFT + 11
                    dve.wait_ge(B.ends_kept, SUBS * TURNS)
                    dve.engine_nop().then_inc(S.out_ready, OUT0)
                    for n in range(7):
                        net_values(dve, 1, T, link, n)

                    def turn(t, more):
                        if more:
                            first_matrix(dve, 1, t + 1, 0)
                        z_low_parts(dve, 1, t, z_hi, z_lo)
                        if more:
                            keep(dve, 1, t + 1, 0, cbanks)
                        for q in range(2):
                            t_tail(t, q, dve=dve)
                        for h in range(HEADS + 2):
                            if more and h in STEP_AT:
                                keep(dve, 1, t + 1, STEP_AT[h], cbanks)
                            if h % 4 == 2 and 2 + h // 4 < J:
                                t_tail(t, 2 + h // 4, dve=dve)
                            if h >= 5 and h % 4 == 1:
                                q = (h - 5) // 4
                                dve.wait_ge(S.y_high, J * t + q + 1)
                                V.tensor_tensor(y_lo[:, q, :], bank[4 + q % 2][:, :], y_hi[:, q, :].bitcast(F32),
                                                ALU.subtract).then_inc(S.y_ready, 1)
                        add_residual(dve, 1, t, res, obanks)

                    with dve.Fori(0, TURNS - 1) as t:
                        turn(t, True)
                    turn(TURNS - 1, False)


def layouts(x, cond_512, w, perm, L1_ffn_up, L1_ffn_down, L0_ffn_w_gate_up, L0_ffn_w_down):
    f = np.float32
    a = {}
    a["x0"] = x.reshape(BATCH, CH, NBLK, J).transpose(0, 1, 3, 2)
    ends = np.stack([x[:, :, 0:2 * J], x[:, :, LEN - 2 * J:]], 2)
    a["xe0"] = ends.reshape(GROUPS, GB * CH, 2, 2 * J).transpose(1, 0, 2, 3)
    a["cond"] = cond_512.T
    per = {k: [] for k in ("modw", "modb", "bias", "wio", "bd", "lift1", "w2r", "lift3a", "lift3b", "w4")}
    for weights, biases, mod_w, mod_b in w:
        per["modw"].append(np.tile(mod_w.transpose(2, 0, 1), (1, 1, J)))
        per["modb"].append(np.tile(mod_b.T, (J, 1)))
        per["bias"].append(np.tile(biases.T, (GB, 1)))
        per["wio"].append(weights.transpose(2, 0, 3, 1))
        bd = np.zeros((P, LAYERS * KT, P), f)
        for l in range(LAYERS):
            for k in range(KT):
                m = weights[l, :, :, k] if l == 1 else weights[l, :, :, k].T
                for g in range(GB):
                    bd[g * CH:(g + 1) * CH, l * KT + k, g * CH:(g + 1) * CH] = m
        per["bd"].append(bd)
        lift1 = np.zeros((KT, CH, TQ, CH), f)
        for k4 in range(KT):
            for k3 in range(KT):
                lift1[k4, :, k4 + k3, :] = weights[2, :, :, k3]
        per["lift1"].append(lift1.reshape(KT * CH, TQ * CH))
        per["w2r"].append(np.tile(weights[1].transpose(1, 2, 0), (J, 1, 1)))
        lift3 = np.zeros((TL, CH, TU, CH), f)
        for la in range(TL):
            for u in range(TU):
                k1 = (4 - u) - (la - 3) + 1
                if 0 <= k1 < KT:
                    lift3[la, :, u, :] = weights[0, :, :, k1]
        lift3 = lift3.reshape(TL * CH, TU * CH)
        per["lift3a"].append(lift3[:P])
        per["lift3b"].append(lift3[P:])
        per["w4"].append(weights[3].transpose(2, 1, 0).reshape(KT * CH, CH))
    for k, v in per.items():
        a[k] = np.stack(v)
    c = compose_coefficients()
    coef = np.zeros((P, 2, KT, TL), f)
    coef[:, 0] = np.repeat(c[:4], CH, 0)
    coef[3 * CH:, 1] = c[4]
    a["coef"] = coef
    pick = np.zeros((2, SEG, P), f)
    pick[:, 0, P - 2] = 1
    pick[:, 1, P - 1] = 1
    pick[:, 2, :INNER] = 1
    a["pick"] = pick.reshape(2 * SEG, P)
    a["ident"] = np.eye(P, dtype=f)
    block_of = np.array(list(range(1, NBLK - 1)) + [0, NBLK - 1])
    pos = block_of[:, None] * J + np.arange(J)[None]
    a["gu"] = L0_ffn_w_gate_up.T[pos].transpose(1, 0, 2)
    natural = (np.arange(NBLK)[None] * J + np.arange(J)[:, None]).reshape(-1)
    a["dn"] = L0_ffn_w_down.T[:, natural]
    up = np.zeros((HPQ, CH, HEADS, HM), f)
    for h in range(HEADS):
        up[h % 2::2, :, h] = L1_ffn_up[h]
    a["up"] = up.reshape(P, HEADS, HM)
    a["hd"] = L1_ffn_down.transpose(1, 0, 2)
    a["perm_row"] = perm.reshape(1, LEN)
    a["perm_col"] = perm.reshape(J, P).T
    a["pos_row"] = natural.astype(f).reshape(1, LEN)
    a["pos_col"] = pos.astype(f)
    return a, natural


def kernel(x, cond_512, L0_cond_weights, L0_cond_biases, L0_cond_mod_w, L0_cond_mod_b, L0_ffn_w_gate_up,
           L0_ffn_w_down, L1_cond_weights, L1_cond_biases, L1_cond_mod_w, L1_cond_mod_b, L1_ffn_up,
           L1_ffn_down, L1_ffn_perm):
    import concourse.bacc as bacc
    from concourse.bass_utils import run_bass_kernel_spmd

    w = [(L0_cond_weights, L0_cond_biases, L0_cond_mod_w, L0_cond_mod_b),
         (L1_cond_weights, L1_cond_biases, L1_cond_mod_w, L1_cond_mod_b)]
    w = [tuple(np.asarray(v) for v in layer) for layer in w]
    arrays, natural = layouts(np.asarray(x), np.asarray(cond_512), w, np.asarray(L1_ffn_perm),
                              np.asarray(L1_ffn_up), np.asarray(L1_ffn_down),
                              np.asarray(L0_ffn_w_gate_up), np.asarray(L0_ffn_w_down))
    nc = bacc.Bacc("TRN2", target_bir_lowering=False, num_devices=1, dynamic_dma_scratch_size=1024)
    ins, d = {}, {}
    for name, v in arrays.items():
        v = np.ascontiguousarray(v)
        ins[f"in_{name}"] = v
        d[name] = nc.dram_tensor(f"in_{name}", v.shape, mybir.dt.from_np(v.dtype), kind="ExternalInput").ap()
    out = nc.dram_tensor("out_y", [BATCH, CH, J, NBLK], F32, kind="ExternalOutput").ap()
    build(nc, d, out)
    r = run_bass_kernel_spmd(nc, [ins], core_ids=[0])
    y = r.results[0]["out_y"]
    return np.ascontiguousarray(y.transpose(0, 1, 3, 2)).reshape(BATCH, CH, LEN)
```

```python
from contextlib import ExitStack

import numpy as np
import concourse.bass as bass
from concourse import mybir

F32 = mybir.dt.float32
F32R = mybir.dt.float32r
I32 = mybir.dt.int32
ALU = mybir.AluOpType
ACT = mybir.ActivationFunctionType

BATCH, CH, LEN = 128, 32, 512
P = 128
J = 4
NBLK = LEN // J
STYLE = 64
KT = 3
LAYERS = 4
SCALE = float(1.0 / np.sqrt(CH * KT ** 2))
EPS = 1e-8
BLUR = [0.125, 0.375, 0.375, 0.125]

TB = 16
TOK = TB * CH
TURNS = BATCH // TB
GB = 4
GROUPS = BATCH // GB
SUBS = TB // GB
HB = TB // 2
HN = HB * CH
INNER = NBLK - 2

TQ, TL, TU = 5, 7, 9
WINDOWS = 3 * J

FF = 1376
FCH = [(c, min(P, FF - c)) for c in range(0, FF, P)]
NF = len(FCH)
HEADS, HM = 16, 128
HPQ = P // CH

SEG = 3
NX, N1, NY, NZ, NV, NVB = 12, 10, 17, 14, 12, 9

A0, A1, A2, A3, D3, D1, S2, S3 = range(8)
NTAB = 8


def compose_coefficients():
    kb = np.convolve(np.array(BLUR), np.array(BLUR)) * 2.0
    c = np.zeros((TQ, KT, TL), np.float32)
    for q in range(TQ):
        for k in range(KT):
            for la in range(TL):
                at = 2 * (la - 3) + 4 + k - q
                if 0 <= at < len(kb):
                    c[q, k, la] = kb[at]
    return c


class Sems:

    def __init__(self, ctx, nc, L):
        def sem(name):
            return ctx.enter_context(nc.semaphore(f"{name}_{L}"))

        self.style_in = sem("style_in")
        self.lift_in = sem("lift_in")
        self.net_in = sem("net_in")
        self.vec = sem("vec")
        self.roots = sem("roots")
        self.prods = sem("prods")
        self.net = sem("net")
        self.a4_out = sem("a4_out")
        self.edge_out = sem("edge_out")
        self.piece_in = [sem(f"piece_in{i}") for i in range(4)]
        self.piece_hi = sem("piece_hi")
        self.piece_lo = sem("piece_lo")
        self.x_in = sem("x_in")
        self.rows_in = sem("rows_in")
        self.a4_in = sem("a4_in")
        self.res_in = [sem(f"res_in{s}") for s in range(SUBS)]
        self.out_done = [sem(f"out_done{s}") for s in range(SUBS)]
        self.e_in = [sem(f"e_in{hh}") for hh in range(2)]
        self.conv_ready = sem("conv_ready")
        self.z_high = sem("z_high")
        self.z_ready = sem("z_ready")
        self.seed = sem("seed")
        self.lifted = sem("lifted")
        self.kept = sem("kept")
        self.first_ready = sem("first_ready")
        self.act_done = sem("act_done")
        self.acc_ready = sem("acc_ready")
        self.out_ready = sem("out_ready")
        if L == 0:
            self.res_end_in = sem("res_end_in")
            self.second_ready = sem("second_ready")
            self.mul_done = sem("mul_done")
            self.high_done = sem("high_done")
            self.hid_ready = sem("hid_ready")
            self.down_done = sem("down_done")
            self.ends_kept = sem("ends_kept")
        else:
            self.up_high = sem("up_high")
            self.gathers = sem("gathers")
            self.onehot = sem("onehot")
            self.perm_ready = sem("perm_ready")
            self.t_high = sem("t_high")
            self.t_ready = sem("t_ready")
            self.sum_ready = sem("sum_ready")
            self.y_high = sem("y_high")
            self.y_ready = sem("y_ready")


OUT0 = 1
E_DMAS = J * J
STEPS = 6

STEP_STYLES, STEP_SQ = 10, 11
STEP_LIFT, STEP_SUMS, STEP_TAB, STEP_A4 = (36, 21), (12, 22), (25, 35), (26, 36)
STEP_STYLED = 49


class NetSteps:

    def __init__(self, g0, groups, vec_before, net_before):
        self.g0, self.groups = g0, groups
        self.one_chunks = [(g, 16) for g in range(0, groups, 16)]
        self.v_chunks = [(g, 8) for g in range(0, groups, 8)]
        n1, n3 = len(self.one_chunks), len(self.v_chunks)
        self.before = vec_before
        self.x = self.before + 3
        self.one = self.x + 2 * n1 + 2
        self.y = self.one + 4 * n1 + 2
        self.z = self.y + 5
        self.v = self.z + 2 * n3 + 2
        self.vb = self.v + 3
        self.o = self.vb + 2
        self.edge = self.o + 2
        self.p1 = net_before
        self.p2 = self.p1 + n1
        self.p3 = self.p2 + 2 * n1
        self.p4 = self.p3 + n3
        self.p5 = self.p4 + 1
        self.p_end = self.p5 + 1


def build(nc, d, out):
    x1_dram = nc.dram_tensor("x1_scratch", [BATCH, CH, J, NBLK], F32, kind="Internal").ap()
    x_of = [d["x0"], x1_dram]
    y_of = [x1_dram, out]
    a4_dram = [nc.dram_tensor(f"a4_rows_{L}", [BATCH, CH], F32, kind="Internal").ap() for L in range(2)]
    edge_dram = [nc.dram_tensor(f"edge_rows_{L}", [2 * SEG, J, GROUPS, GB, CH], F32, kind="Internal").ap()
                 for L in range(2)]
    MM = nc.tensor.matmul
    V = nc.vector

    with ExitStack() as top:
        def sb(name, shape, dt=F32, c=top):
            return c.enter_context(nc.sbuf_tensor(name, shape, dt))

        bank = [top.enter_context(nc.psum_tensor(f"bank{i}", [P, 512], F32)) for i in range(8)]
        sems = [Sems(top, nc, L) for L in range(2)]
        zeroed = top.enter_context(nc.semaphore("zeroed"))
        pick_in = top.enter_context(nc.semaphore("pick_in"))
        zeros_ready = top.enter_context(nc.semaphore("zeros_ready"))
        pick_ready = top.enter_context(nc.semaphore("pick_ready"))

        xe1 = sb("xe1", [P, GROUPS, 2, 2 * J])
        tab = sb("tab", [P, A3 + 1, BATCH])
        tg = sb("tg", [P, NTAB, GROUPS])
        bt = sb("bt", [P, 3, GROUPS])
        modb = sb("modb", [P, LAYERS])
        bias = sb("bias", [P, LAYERS])
        w2r = sb("w2r", [P, KT, CH])
        coef = sb("coef", [P, 2, KT, TL])
        ident = sb("ident", [P, P])
        a4t = sb("a4t", [BATCH, CH])
        lift1_2b = sb("lift1_2b", [P, TL * CH])
        lift1 = lift1_2b[0:KT * CH, 0:TQ * CH]
        lift2b = lift1_2b[KT * CH:P, :].rearrange("p (a b) -> p a b", a=TL)
        lift2a = sb("lift2a", [P, TL, CH])
        lift3a = sb("lift3a", [P, 5 * CH])
        lift3b = sb("lift3b", [P, 8 * CH])
        w4 = sb("w4", [KT * CH, CH])
        with ExitStack() as place:
            before_rows = sb("before_rows", [P, SUBS * 512], F32, place)
        rows = sb("rows", [2 * SEG, SUBS, 512], F32R)
        pick = sb("pick", [2 * SEG, P], F32R)
        with ExitStack() as place:
            sb("before_e", [P, (2 * J + 1) * TOK - 2 * SEG * P], F32, place)
            mid_e = sb("mid_e", [P, 2 * SEG * P], F32R, place)
        taps_e = sb("taps_e", [P, WINDOWS, TOK])
        xin = sb("xin", [P, TB, NBLK])
        a4 = sb("a4", [KT * CH, TOK])
        r0_h1b = sb("r0_h1b", [P, HN])
        r0, h1b = r0_h1b[0:KT * CH, :], r0_h1b[KT * CH:P, :]
        h1a = sb("h1a", [P, HN])
        h2a = sb("h2a", [P, HN])
        h2b = sb("h2b", [P, HN])
        h3 = sb("h3", [P, 3, HN])

        fa = xin[:].rearrange("p b n -> p (b n)")
        middle = taps_e[:, J - 1:2 * J + 1, :].rearrange("p w n -> p (w n)")
        fb = middle[:, 0:2048]

        pick_raw = a4[0:2 * SEG, 0:P]

        def by_layer(v):
            return v.rearrange("p (l n) -> p l n", l=LAYERS)

        sj, dj, va = (by_layer(fa[:, n:n + 512]) for n in (0, 512, 1024))
        sq = by_layer(fa[0:CH, 1536:2048])
        modw = by_layer(fb[0:STYLE, 0:512])
        cond = fb[0:STYLE, 512:640]
        wio = fb[0:CH, 640:1024].rearrange("p (l k o) -> p l k o", l=LAYERS, k=KT)
        wsq = fb[0:CH, 1024:1536].rearrange("p (l r o) -> p l r o", l=LAYERS, r=J)
        tab2 = by_layer(fb[:, 1536:2048])

        class Link:

            def __init__(self, eng, vec):
                self.eng, self.vec, self.done = eng, vec, 0

            def __call__(self, ins):
                self.done += 1
                ins.then_inc(self.vec, 1)
                self.eng.wait_ge(self.vec, self.done)

            def at(self, step):
                assert self.done == step, (self.done, step)

        def load_styles(sp, L):
            S = sems[L]
            for dst, src in ((cond, d["cond"]), (modw, d["modw"][L]), (wio, d["wio"][L]),
                             (modb[:], d["modb"][L])):
                sp.dma_start(dst, src).then_inc(S.style_in, 16)

        def load_lifts(sp, L):
            S = sems[L]
            for dst, src in ((w2r[:], d["w2r"][L]), (coef[:], d["coef"]), (w4[:], d["w4"][L]),
                             (bias[:], d["bias"][L]), (ident[:], d["ident"]), (lift1, d["lift1"][L]),
                             (lift3a[:], d["lift3a"][L]), (lift3b[:], d["lift3b"][L])):
                sp.dma_start(dst, src).then_inc(S.lift_in, 16)

        N_STYLE, N_LIFT = 4, 8

        def load_a4(q, L, t):
            q.dma_start(a4[:], a4_dram[L].rearrange("b o -> (b o)")[bass.ds(t * TOK, TOK)]
                        .partition_broadcast(KT * CH)).then_inc(sems[L].a4_in, 16)

        def spread(sp, L, hh):
            for g in range(J):
                tiles = 3 if g == 0 else 2
                for j in range(J):
                    sp.dma_start(taps_e[CH * j:CH * (j + 1), g + j:g + j + J * (tiles - 1) + 1:J,
                                        hh * HN:(hh + 1) * HN],
                                 h3[CH * g:CH * (g + 1), 0:tiles, :]).then_inc(sems[L].e_in[hh], 16)

        def style_products(pe, L, b):
            pe.wait_ge(sems[L].style_in, 16 * N_STYLE)
            for l in range(LAYERS):
                last = MM(b[:, l * BATCH:(l + 1) * BATCH], modw[:, l, :], cond, start=True, stop=True)
            last.then_inc(sems[L].prods, 1)

        def style_sums(pe, L, b):
            pe.wait_ge(sems[L].vec, STEP_SQ)
            for l in range(LAYERS):
                last = MM(b[:, l * BATCH:(l + 1) * BATCH], wsq[:, l, :, :].rearrange("p r o -> p (r o)"),
                          sq[:, l, :], start=True, stop=True)
            last.then_inc(sems[L].prods, 1)

        def style_flip(pe, L, b):
            pe.wait_ge(sems[L].vec, STEP_TAB[L])
            pe.wait_ge(sems[L].lift_in, 16 * N_LIFT)
            nc.tensor.transpose(b[:, 0:CH], tab2[0:CH, 0, :], ident[0:CH, 0:CH]).then_inc(sems[L].prods, 1)

        def style_root(act, L):
            act.wait_ge(sems[L].vec, STEP_SUMS[L])
            nc.scalar.activation(dj, va, ACT.Sqrt).then_inc(sems[L].roots, 1)

        def style_weights(dve, L, link):
            S = sems[L]
            dve.wait_ge(S.style_in, 16 * N_STYLE)
            link(V.tensor_tensor(wio, wio, wio, ALU.mult))
            link(V.tensor_tensor(wsq[:, :, 0, :], wio[:, :, 0, :], wio[:, :, 1, :], ALU.add))
            link(V.tensor_tensor(wsq[:, :, 0, :], wsq[:, :, 0, :], wio[:, :, 2, :], ALU.add))
            link(V.tensor_copy(wsq[:, :, 1, :], wsq[:, :, 0, :]))
            link(V.tensor_copy(wsq[:, :, 2:4, :], wsq[:, :, 0:2, :]))
            link(V.tensor_scalar(modb[:], modb[:], SCALE, None, ALU.mult))

        def styles(dve, L, link, b):
            S = sems[L]
            dve.wait_ge(S.prods, 1)
            for l in range(LAYERS):
                link(V.tensor_scalar(sj[:, l, :], b[:, l * BATCH:(l + 1) * BATCH], SCALE,
                                     modb[:, l:l + 1], ALU.mult, ALU.add))
            link(V.tensor_tensor(sq, sj[0:CH], sj[0:CH], ALU.mult))
            link.at(STEP_SQ)

        def second_lifts(dve, L, link):
            dve.wait_ge(sems[L].lift_in, 16 * N_LIFT)
            for lift, which, p0, m in ((lift2a[:], 0, 0, P), (lift2b, 1, 3 * CH, CH)):
                t = h1a[p0:p0 + m, 0:TL * CH].rearrange("p (a b) -> p a b", a=TL)
                for k in range(KT):
                    w = w2r[p0:p0 + m, k, :].unsqueeze(1).to_broadcast([m, TL, CH])
                    f = coef[p0:p0 + m, which, k, :].unsqueeze(2).to_broadcast([m, TL, CH])
                    if k == 0:
                        link(V.tensor_tensor(lift, w, f, ALU.mult))
                    else:
                        link(V.tensor_tensor(t, w, f, ALU.mult))
                        link(V.tensor_tensor(lift, lift, t, ALU.add))
            link.at(STEP_LIFT[L])

        def sums_of_squares(dve, L, link, b):
            dve.wait_ge(sems[L].prods, 2)
            link(V.tensor_scalar(va, by_layer(b[:, :]), EPS, None, ALU.add))
            link.at(STEP_SUMS[L])

        def demodulation(dve, L, link):
            dve.wait_ge(sems[L].roots, 1)
            link(V.reciprocal(dj, dj))
            link(V.tensor_tensor(va, va, dj, ALU.mult))
            link(V.tensor_tensor(va, va, dj, ALU.mult))
            link(V.tensor_scalar(va, va, -0.5, 1.5, ALU.mult, ALU.add))
            link(V.tensor_tensor(dj, dj, va, ALU.mult))

        def factor_tables(dve, L, link):
            for to, x, y in ((A1, dj[:, 0], dj[:, 1]), (A2, sj[:, 1], sj[:, 2]), (A3, dj[:, 2], sj[:, 3])):
                link(V.tensor_tensor(tab[:, to, :], x, y, ALU.mult))
            for to, x in ((A0, sj[:, 0]), (D3, dj[:, 3]), (D1, dj[:, 1]), (S2, sj[:, 2]), (S3, sj[:, 3])):
                link(V.tensor_copy(tab[:, to, :] if to <= A3 else tab2[:, to - D3, :], x))
            link.at(STEP_TAB[L])

        def last_factors(dve, L, link, b):
            dve.wait_ge(sems[L].prods, 3)
            link(V.tensor_copy(a4t[:], b[:, 0:CH]))
            link.at(STEP_A4[L])

        def group_factors(dve, L, link):
            for r in range(GB):
                q = slice(CH * r, CH * (r + 1))
                link(V.tensor_copy(tg[q, 0:D3, :], tab[q, :, r::GB]))
                link(V.tensor_copy(tg[q, D3:NTAB, :], tab2[q, :, r::GB]))
            for n, f in enumerate((D1, S2, S3)):
                link(V.tensor_scalar(bt[:, n, :], tg[:, f, :], bias[:, n:n + 1], None, ALU.mult))
            link(V.tensor_scalar(tg[:, A3, :], tg[:, A3, :], 2.0 * BLUR[0], None, ALU.mult))
            link(V.tensor_scalar(tg[:, D3, :], tg[:, D3, :], BLUR[0], None, ALU.mult))
            link.at(STEP_STYLED)

        def step(pe, L, t, n, banks):
            S = sems[L]
            a, b = banks
            hh, st = divmod(n, 3)
            if n > 0:
                pe.wait_ge(S.kept, STEPS * t + n)
            if st == 0:
                pe.wait_ge(S.seed, 4 * t + 2 * (hh + 1))
                MM(a[:, 0:HN], lift1[:, 0:P], r0, start=True, stop=True)
                last = MM(a[0:CH, HN:2 * HN], lift1[:, P:P + CH], r0, start=True, stop=True)
            if st == 1:
                la, lb = (x.rearrange("p a b -> p (a b)") for x in (lift2a[:], lift2b))
                for c0, at in ((0, 0), (3 * CH, HN)):
                    MM(a[:, at:at + HN], la[:, c0:c0 + P], h1a[:], start=True, stop=False)
                    last = MM(a[:, at:at + HN], lb[:, c0:c0 + P], h1b, start=False, stop=True)
            if st == 2:
                MM(a[:, 0:HN], lift3b[:, 0:P], h2b[:], start=True, stop=True)
                MM(a[:, HN:2 * HN], lift3a[:, 0:P], h2a[:], start=True, stop=False)
                MM(a[:, HN:2 * HN], lift3b[:, P:2 * P], h2b[:], start=False, stop=True)
                last = MM(b[0:CH, 0:HN], lift3a[:, P:P + CH], h2a[:], start=True, stop=True)
            last.then_inc(S.lifted, 1)

        def first_matrix(dve, L, t, hh):
            S = sems[L]
            f = tab[0:KT * CH, A3, bass.ds(t * TB + hh * HB, HB)].unsqueeze(2).to_broadcast([KT * CH, HB, CH])
            w = w4[:].unsqueeze(1).to_broadcast([KT * CH, HB, CH])
            V.tensor_tensor(r0.rearrange("p (b o) -> p b o", b=HB), w, f, ALU.mult).then_inc(S.seed, 1)
            dve.wait_ge(S.a4_in, 16 * t + 16)
            dve.wait_ge(S.seed, 4 * t + 2 * hh + 1)
            V.tensor_tensor(r0, r0, a4[:, hh * HN:(hh + 1) * HN], ALU.mult).then_inc(S.seed, 1)

        def keep(dve, L, t, n, banks):
            S = sems[L]
            a, b = banks
            hh, st = divmod(n, 3)
            dve.wait_ge(S.lifted, STEPS * t + n + 1)
            if st == 2 and not (isinstance(t, int) and t == 0 and hh == 0):
                dve.wait_ge(S.e_in[1 - hh], 16 * E_DMAS * t + 16 * E_DMAS * hh)
            tiles = {0: ((h1a[:], a, 0, P), (h1b, a, HN, CH)),
                     1: ((h2a[:], a, 0, P), (h2b[:], a, HN, P)),
                     2: ((h3[:, 0, :], a, 0, P), (h3[:, 1, :], a, HN, P), (h3[0:CH, 2, :], b, 0, CH))}[st]
            for dst, src, at, m in tiles:
                f = tab[0:m, (A2, A1, A0)[st], bass.ds(t * TB + hh * HB, HB)].unsqueeze(2).to_broadcast([m, HB, CH])
                last = V.tensor_tensor(dst.rearrange("p (b o) -> p b o", b=HB),
                                       src[0:m, at:at + HN].rearrange("p (b o) -> p b o", b=HB), f, ALU.mult)
            last.then_inc(S.kept, 1)
            if n == 0:
                first_matrix(dve, L, t, 1)

        def net_tiles(steps, one, two, ta, bd, e, banks, net_in):
            G = steps.groups
            wide = G * SEG

            def view(t, n):
                return t[:, 0:wide * n].rearrange("p (g s n) -> p g s n", g=G, s=SEG)

            return {"nx": view(one, NX), "n1": view(two, N1), "ny": view(one, NY), "nz": view(two, NZ),
                    "nv": view(one, NV), "nvb": view(two, NVB), "ta": ta, "view": view,
                    "no": ta[:, 0:SEG * G * J].rearrange("p (s j g) -> p s g j", s=SEG, j=J),
                    "bd": bd.rearrange("p (l n) -> p l n", n=P),
                    "e": e.rearrange("p (r s n) -> p r s n", r=2, s=SEG),
                    "steps": steps, "banks": banks, "net_in": net_in}

        def net_products(pe, L, T, stage):
            S = sems[L]
            bd, at = T["bd"], T["steps"]
            G = at.groups
            banks = T["banks"][stage]

            def taps(dst, l, ks, moving):
                for n, (k, src) in enumerate(zip(ks, moving)):
                    last = MM(dst, bd[:, l * KT + k, :], src, start=(n == 0), stop=(n == len(ks) - 1))
                last.then_inc(S.net, 1)

            def win(t, g0, gn, a, n):
                return T[t][:, g0:g0 + gn, :, a:a + n].rearrange("p g s n -> p (g s) n")

            def cols(b, gn, n):
                return b[:, 0:gn * SEG * n].rearrange("p (g n) -> p g n", n=n)

            if stage == 1:
                pe.wait_ge(S.net_in, T["net_in"])
                pe.wait_ge(S.vec, at.x)
                for c, (g0, gn) in enumerate(at.one_chunks):
                    taps(cols(banks[c], gn, N1), 0, range(KT), [win("nx", g0, gn, k, N1) for k in range(KT)])
            if stage == 2:
                pe.wait_ge(S.vec, at.one)
                for c, (g0, gn) in enumerate(at.one_chunks):
                    taps(cols(banks[2 * c], gn, 9), 1, (0, 2), [win("n1", g0, gn, 1, 9), win("n1", g0, gn, 0, 9)])
                    taps(cols(banks[2 * c + 1], gn, 8), 1, (1,), [win("n1", g0, gn, 1, 8)])
            if stage == 3:
                pe.wait_ge(S.vec, at.z)
                for c, (g0, gn) in enumerate(at.v_chunks):
                    taps(cols(banks[c], gn, NV), 2, range(KT), [win("nz", g0, gn, k, NV) for k in range(KT)])
            if stage == 4:
                pe.wait_ge(S.vec, at.vb)
                dst = banks[0][:, 0:SEG * G * J].rearrange("p (s g j) -> p g s j", s=SEG, j=J)
                taps(dst, 3, range(KT), [T["nvb"][:, :, :, k:k + 7:2] for k in range(KT)])
            if stage == 5:
                pe.wait_ge(S.vec, at.o)
                for s in range(SEG):
                    last = nc.tensor.transpose(banks[0][0:G * J, s * P:(s + 1) * P],
                                               T["ta"][:, s * G * J:(s + 1) * G * J], ident[:])
                last.then_inc(S.net, 1)

        def net_values(dve, L, T, link, stage):
            S = sems[L]
            at = T["steps"]
            G = at.groups
            own = slice(at.g0, at.g0 + G)
            banks = T["banks"].get(stage)

            def evacuate(b, dst, g0, gn, n, fa_, fb_):
                src = b[:, 0:gn * SEG * n].rearrange("p (g s n) -> p g s n", g=gn, s=SEG)
                g = slice(at.g0 + g0, at.g0 + g0 + gn)
                x = tg[:, fa_, g].unsqueeze(2).unsqueeze(3).to_broadcast([P, gn, SEG, n])
                y = bt[:, fb_, g].unsqueeze(2).unsqueeze(3).to_broadcast([P, gn, SEG, n])
                link(V.tensor_tensor(dst, src, x, ALU.mult))
                link(V.tensor_tensor(dst, dst, y, ALU.add))

            def blur(dst, src, n):
                w = [src[:, :, :, t:t + n].rearrange("p g s n -> p (g s) n") for t in range(4)]
                o = dst[:, :, :, 0:n].rearrange("p g s n -> p (g s) n")
                u = T["view"](T["ta"], n).rearrange("p g s n -> p (g s) n")
                link(V.tensor_tensor(u, w[1], w[2], ALU.add))
                link(V.tensor_tensor(o, w[0], w[3], ALU.add))
                link(V.scalar_tensor_tensor(o, u, BLUR[1] / BLUR[0], o, ALU.mult, ALU.add))

            nx, n1, ny, nz, nv, nvb, no = (T[k] for k in ("nx", "n1", "ny", "nz", "nv", "nvb", "no"))
            if stage == 0:
                link.at(at.before)
                if L == 0:
                    dve.wait_ge(S.net_in, 32)
                else:
                    dve.wait_ge(sems[0].ends_kept, at.g0 + G)
                link(V.memset(nx[:, :, :, :], 0.0))
                s0 = tg[:, A0, own].unsqueeze(2).to_broadcast([P, G, 2 * J])
                link(V.tensor_tensor(nx[:, :, 0, 4:12], xe1[:, own, 0, :], s0, ALU.mult))
                link(V.tensor_tensor(nx[:, :, 1, 0:8], xe1[:, own, 1, :], s0, ALU.mult))
                link.at(at.x)
            if stage == 1:
                for c, (g0, gn) in enumerate(at.one_chunks):
                    dve.wait_ge(S.net, at.p1 + c + 1)
                    evacuate(banks[c], n1[:, g0:g0 + gn, :, :], g0, gn, N1, A1, 0)
                link(V.memset(n1[:, :, 0, 0:3], 0.0))
                link(V.memset(n1[:, :, 1, 7:10], 0.0))
                link.at(at.one)
            if stage == 2:
                for c, (g0, gn) in enumerate(at.one_chunks):
                    dve.wait_ge(S.net, at.p2 + 2 * c + 1)
                    evacuate(banks[2 * c], ny[:, g0:g0 + gn, :, 0:17:2], g0, gn, 9, A2, 1)
                    dve.wait_ge(S.net, at.p2 + 2 * c + 2)
                    evacuate(banks[2 * c + 1], ny[:, g0:g0 + gn, :, 1:17:2], g0, gn, 8, A2, 1)
                link(V.memset(ny[:, :, 0, 0:4], 0.0))
                link(V.memset(ny[:, :, 1, 13:17], 0.0))
                link.at(at.y)
            if stage == "blur 2":
                blur(nz, ny, NZ)
                link(V.memset(nz[:, :, 0, 0:3], 0.0))
                link(V.memset(nz[:, :, 1, 11:14], 0.0))
                link.at(at.z)
            if stage == 3:
                for c, (g0, gn) in enumerate(at.v_chunks):
                    dve.wait_ge(S.net, at.p3 + c + 1)
                    evacuate(banks[c], nv[:, g0:g0 + gn, :, :], g0, gn, NV, A3, 2)
                link(V.memset(nv[:, :, 0, 0:2], 0.0))
                link(V.memset(nv[:, :, 1, 10:12], 0.0))
                link.at(at.v)
            if stage == "blur 3":
                blur(nvb, nv, NVB)
                link.at(at.vb)
            if stage == 4:
                dve.wait_ge(S.net, at.p4 + 1)
                src = banks[0][:, 0:SEG * G * J].rearrange("p (s g j) -> p s g j", s=SEG, j=J)
                d3 = tg[:, D3, own].unsqueeze(1).unsqueeze(3).to_broadcast([P, SEG, G, J])
                link(V.tensor_tensor(no, src, d3, ALU.mult))
                link(V.tensor_scalar(no, no, bias[:, 3:4], None, ALU.add))
                link.at(at.o)
            if stage == 5:
                dve.wait_ge(S.net, at.p5 + 1)
                src = banks[0][0:G * J, 0:SEG * P].rearrange("p (s n) -> p s n", s=SEG)
                link(V.tensor_copy(T["e"][:, 0], src))
                link(V.tensor_tensor(T["e"][:, 1], src, T["e"][:, 0].bitcast(F32), ALU.subtract))
                link.at(at.edge)

        def net_left(pe, L, T, stage):
            at = T["steps"]
            pe.wait_ge(sems[L].vec, (at.x, at.one, at.y, at.v, at.o, at.edge)[stage])

        def store_edges(sp, L, T, stored):
            at = T["steps"]
            sp.wait_ge(sems[L].vec, at.edge)
            G = at.groups
            for j in range(J):
                sp.dma_start(edge_dram[L][:, j, at.g0:at.g0 + G, :, :].rearrange("r g b o -> g r (b o)"),
                             T["e"][j * G:(j + 1) * G].rearrange("p r s n -> p (r s) n").bitcast(F32)
                             ).then_inc(sems[L].edge_out, 16)
            sp.wait_ge(sems[L].edge_out, 16 * J * stored)

        def load_x(sp, L, t):
            for j in range(J):
                sp.dma_start(xin[CH * j:CH * (j + 1), :, :],
                             x_of[L][bass.ds(t * TB, TB), :, j, :].rearrange("b c n -> c b n")
                             ).then_inc(sems[L].x_in, 16)

        def load_rows(sp, L, t):
            for j in range(J):
                sp.dma_start(rows[:].bitcast(F32).rearrange("r g (b j o) -> r (g b) j o", b=GB, j=J)[:, :, j, :],
                             edge_dram[L][:, j, bass.ds(t * SUBS, SUBS), :, :].rearrange("r g b o -> r (g b) o")
                             ).then_inc(sems[L].rows_in, 16)

        def load_res(sp, L, t, s, res):
            NR = res.shape[1]
            x_rows = x_of[L].rearrange("b c j n -> (b c) (j n)")
            sp.dma_start(res[:, s % NR, :], x_rows[bass.ds(t * TOK + s * P, P), :]).then_inc(sems[L].res_in[s % NR], 16)

        def store_out(sp, L, t, s, res):
            NR = res.shape[1]
            y_rows = y_of[L].rearrange("b c j n -> (b c) (j n)")
            sp.wait_ge(sems[L].out_ready, SUBS * t + s + 1 + OUT0)
            sp.dma_start(y_rows[bass.ds(t * TOK + s * P, P), :], res[:, s % NR, :]).then_inc(sems[L].out_done[s % NR], 16)

        def reload_res(sp, L, t, s, res):
            NR = res.shape[1]
            if L == 0:
                sp.wait_ge(sems[L].ends_kept, SUBS * t + s + 1)
            sp.wait_ge(sems[L].out_done[s % NR], 16 * (SUBS // NR * t + s // NR + 1))
            load_res(sp, L, *((t, s + NR) if s + NR < SUBS else (t + 1, s + NR - SUBS)), res)

        def sync_turn(sp, L, t, res, edges=None):
            S = sems[L]
            NR = res.shape[1]
            sp.wait_ge(S.conv_ready, SUBS * t + SUBS)
            load_x(sp, L, t + 1)
            load_rows(sp, L, t + 1)
            for hh in range(2):
                sp.wait_ge(S.kept, STEPS * t + STEPS + 3 * (hh + 1))
                spread(sp, L, hh)
            if edges is not None:
                store_edges(sp, L, edges, 2)
            for s in range(SUBS):
                store_out(sp, L, t, s, res)
                reload_res(sp, L, t, s, res)

        def conv_bank(L, g):
            return bank[(g + 2) % SUBS if L == 1 else g]

        def convolve_group(pe, L, t, g, first_rows, final):
            S = sems[L]
            if g % 2 == 0:
                pe.wait_ge(S.e_in[g // 2], 16 * E_DMAS * t + 16 * E_DMAS)
            if g == 2 and L == 1 and not (isinstance(t, int) and t == 0):
                pe.wait_ge(S.out_ready, SUBS * t - SUBS + 2 + OUT0)
            MM(conv_bank(L, g)[:, :], pick[:], first_rows, start=True, stop=False)
            for bb in range(GB):
                b = GB * g + bb
                dst = conv_bank(L, g)[0:INNER, P * bb:P * (bb + 1)].rearrange("p (j o) -> p j o", j=J)
                for s in (-1, 0, 1):
                    last = MM(dst, xin[:, b, 1 + s:1 + s + INNER],
                              taps_e[:, J * (1 - s):J * (2 - s), CH * b:CH * (b + 1)],
                              start=False, stop=(final and bb == GB - 1 and s == 1))
            if final:
                last.then_inc(S.conv_ready, 1)

        def convolve(pe, L, t):
            S = sems[L]
            pe.wait_ge(S.x_in, 16 * J * t + 16 * J)
            pe.wait_ge(S.rows_in, 16 * J * t + 16 * J)
            for g in range(SUBS):
                convolve_group(pe, L, t, g, rows[:, g, :], True)

        def three(dst, w_hi, w_lo, m_hi, m_lo, first, final):
            MM(dst, w_hi, m_hi, start=first, stop=False)
            MM(dst, w_hi, m_lo, start=False, stop=False)
            return MM(dst, w_lo, m_hi, start=False, stop=final)

        def z_view(z, g):
            return z[:, :, P * g:P * (g + 1)].rearrange("p j (b o) -> p b j o", b=GB)

        def z_bank(L, g):
            return conv_bank(L, g)[:, :].rearrange("p (b j o) -> p b j o", b=GB, j=J)

        def z_high_parts(act, L, t, z_hi):
            for g in range(SUBS):
                act.wait_ge(sems[L].conv_ready, SUBS * t + g + 1)
                nc.scalar.activation(z_view(z_hi, g), z_bank(L, g), ACT.Copy).then_inc(sems[L].z_high, 1)

        def z_low_parts(dve, L, t, z_hi, z_lo):
            for g in range(SUBS):
                dve.wait_ge(sems[L].z_high, SUBS * t + g + 1)
                V.tensor_tensor(z_view(z_lo, g), z_bank(L, g), z_view(z_hi, g).bitcast(F32),
                                ALU.subtract).then_inc(sems[L].z_ready, 1)

        def add_residual(dve, L, t, res, banks, end=None):
            S = sems[L]
            NR = res.shape[1]
            for s in range(SUBS):
                dve.wait_ge(S.acc_ready, SUBS * t + s + 1)
                if end is not None and s >= 2:
                    dve.wait_ge(S.res_end_in, 16)
                    V.tensor_tensor(end[:, s % 2, :], banks[s][:, :], end[:, s % 2, :], ALU.add).then_inc(S.out_ready, 1)
                    continue
                dve.wait_ge(S.res_in[s % NR], 16 * (SUBS // NR * t + s // NR + 1))
                V.tensor_tensor(res[:, s % NR, :], banks[s][:, :], res[:, s % NR, :], ALU.add).then_inc(S.out_ready, 1)

        with ExitStack() as ctx:
            S, N = sems
            with ExitStack() as second:
                up = sb("up", [3 * CH, HEADS, HM], F32R, second)
                up_part = sb("up_part", [3 * CH, HEADS, HM], F32R, second)
                stage = sb("stage", [3 * CH, HEADS, HM], F32, second)
                hd = sb("hd", [HM, HEADS, CH], F32, second)
                gather = sb("gather", [P, J, LEN], F32R, second)
                scatter = sb("scatter", [P, J, LEN], F32R, second)
                z_hi_1 = sb("z_hi_1", [P, J, TOK], F32R, second)
                z_lo_1 = sb("z_lo_1", [P, J, TOK], F32R, second)
                prow_i = sb("prow_i", [P, LEN], I32, second)
                prow = sb("prow", [P, LEN], F32, second)
                posrow = sb("posrow", [P, LEN], F32, second)
                bd_1 = sb("bd_1", [P, LAYERS * KT * P], F32, second)
                pcol_i = sb("pcol_i", [P, J], I32, second)
                pcol = sb("pcol", [P, J], F32, second)
                poscol = sb("poscol", [P, J], F32, second)
                second_bytes = 4 * (3 * HEADS * HM + HEADS * CH + 2 * J * LEN + 2 * J * TOK + 3 * LEN
                                    + LAYERS * KT * P) + 3 * 64
            gu_hi = sb("gu_hi", [P, J, 2 * FF], F32R, ctx)
            gu_lo = sb("gu_lo", [P, J, 2 * FF], F32R, ctx)
            dn_hi = sb("dn_hi", [P, NF, LEN], F32R, ctx)
            dn_lo = sb("dn_lo", [P, NF, LEN], F32R, ctx)
            hid = sb("hid", [P, 2, TOK], F32, ctx)
            res = sb("res0", [P, 2, TOK], F32, ctx)
            with ExitStack() as pre:
                wide = GROUPS * SEG
                two, ta, bd = (sb(f"net_{n}_0", [P, w], F32, pre)[:] for n, w in
                               (("two", wide * NZ), ("ta", wide * NZ), ("bd", LAYERS * KT * P)))
                e = sb("net_e_0", [P, 2 * SEG * P], F32R, pre)[:]
                T = net_tiles(NetSteps(0, GROUPS, STEP_STYLED, 0), before_rows[:], two, ta, bd, e,
                              {1: bank[0:2], 2: (bank[2], bank[3], bank[6], bank[7]), 3: bank[2:4] + bank[6:8],
                               4: bank[6:7], 5: bank[7:8]}, 32)
            with ExitStack() as place:
                res_end = sb("res_end", [P, 2, TOK], F32, place)
            z_hi = sb("z_hi_0", [P, J, TOK], F32R, ctx)
            z_lo = sb("z_lo_0", [P, J, TOK], F32R, ctx)
            hid_hi = sb("hid_hi", [P, 2, TOK], F32R, ctx)
            hid_lo = sb("hid_lo", [P, 2, TOK], F32R, ctx)
            places = [hid[:, 0, :], hid[:, 1, :], res[:, 0, :], res[:, 1, :]]
            zero_rows = hid_lo[0:2 * SEG, 0, :]

            cuts = [(j, a, min(a + 512, 2 * FF)) for j in range(J) for a in range(0, 2 * FF, 512)]
            pieces = [(d["gu"][j, :, a:b], gu_hi[:, j, a:b], gu_lo[:, j, a:b]) for j, a, b in cuts]
            N_GU = len(pieces)
            pieces += [(d["dn"][i0:i0 + m, :], dn_hi[0:m, i, :], dn_lo[0:m, i, :])
                       for i, (i0, m) in enumerate(FCH)]

            def pair(c):
                return bank[2 * (c % 2)], bank[2 * (c % 2) + 1]

            BRIDGE = {1: {1: ("style", 0)}, 2: {0: ("style", 1)}, 3: {1: ("style", 2)}, 4: {1: ("net", 1)},
                      5: {0: ("net", 2)}, 6: {0: ("step", 0), 1: ("step", 1)},
                      7: {0: ("net", 3), 1: ("step", 2)}, 8: {0: ("net", 4), 1: ("net", 5)},
                      9: {0: ("step", 3), 1: ("step", 4)}, 10: {1: ("step", 5)}}
            NT = (GROUPS // 2) * SEG
            spots = np.cumsum([0, NT * NY, NT * NZ, NT * NZ]).tolist()
            T1 = net_tiles(NetSteps(0, GROUPS // 2, STEP_STYLED, 0),
                           *(middle[:, a:b] for a, b in zip(spots, spots[1:])),
                           before_rows[:, 0:LAYERS * KT * P], mid_e[0:GROUPS // 2 * J, :],
                           {1: pair(5)[0:1], 2: pair(6), 3: pair(8), 4: pair(9)[0:1], 5: pair(9)[1:2]}, 16)

            def bridge_banks(c, n):
                a, b = pair(c + 1)
                return (a, b) if n != 1 else (b, a)

            with nc.Block() as block:
                @block.sync
                def _(sp):
                    load_styles(sp, 0)
                    sp.dma_start(pick_raw, d["pick"]).then_inc(pick_in, 16)
                    load_lifts(sp, 0)
                    sp.dma_start(xe1[:], d["xe0"]).then_inc(S.net_in, 16)
                    sp.dma_start(T["bd"], d["bd"][0]).then_inc(S.net_in, 16)
                    sp.wait_ge(S.vec, STEP_A4[0])
                    sp.dma_start(a4_dram[0], a4t[:]).then_inc(S.a4_out, 16)
                    sp.wait_ge(S.a4_out, 16)
                    sp.wait_ge(pick_ready, 1)
                    load_a4(sp, 0, 0)
                    sp.wait_ge(S.vec, STEP_STYLED)
                    load_x(sp, 0, 0)
                    sp.wait_ge(zeroed, 2)
                    for hh in range(2):
                        sp.wait_ge(S.kept, 3 * (hh + 1))
                        spread(sp, 0, hh)
                    store_edges(sp, 0, T, 1)
                    load_rows(sp, 0, 0)
                    sp.wait_ge(S.piece_lo, len(pieces))
                    for s in range(2):
                        load_res(sp, 0, 0, s, res)
                    with sp.Fori(0, TURNS - 1) as t:
                        sync_turn(sp, 0, t, res)
                    t = TURNS - 1
                    sp.wait_ge(S.conv_ready, SUBS * TURNS)
                    load_styles(sp, 1)
                    load_lifts(sp, 1)
                    sp.dma_start(T1["bd"], d["bd"][1]).then_inc(N.net_in, 16)
                    sp.wait_ge(N.vec, STEP_A4[1])
                    sp.dma_start(a4_dram[1], a4t[:]).then_inc(N.a4_out, 16)
                    sp.wait_ge(N.a4_out, 16)
                    load_a4(sp, 1, 0)
                    load_x(sp, 1, 0)
                    store_edges(sp, 1, T1, 1)
                    sp.wait_ge(N.kept, 3)
                    spread(sp, 1, 0)
                    load_rows(sp, 1, 0)
                    sp.wait_ge(S.second_ready, NF * TURNS)
                    x_rows = x_of[0].rearrange("b c j n -> (b c) (j n)")
                    sp.dma_start(res_end[:], x_rows[t * TOK + 2 * P:(t + 1) * TOK, :]
                                 .rearrange("(s p) n -> p s n", p=P)).then_inc(S.res_end_in, 16)
                    sp.wait_ge(N.kept, 6)
                    spread(sp, 1, 1)
                    for s in range(SUBS):
                        store_out(sp, 0, t, s, res if s < 2 else res_end)

                @block.gpsimd
                def _(pool):
                    for i, (src, hi, lo) in enumerate(pieces):
                        if i == 2:
                            nc.gpsimd.memset(taps_e[:, 0:J - 1, :], 0.0).then_inc(zeroed, 1)
                            nc.gpsimd.memset(taps_e[:, 2 * J + 1:3 * J, :], 0.0).then_inc(zeroed, 1)
                        raw = places[i % 4][0:hi.shape[0], 0:hi.shape[1]]
                        pool.wait_ge(S.piece_hi, i + 1)
                        nc.gpsimd.tensor_tensor(lo, raw, hi.bitcast(F32), ALU.subtract).then_inc(S.piece_lo, 1)
                    def keep_ends(t, s, tile):
                        pool.wait_ge(S.out_ready, SUBS * t + s + 1 + OUT0)
                        tile = tile[:, s % 2, :].rearrange("p (j n) -> p n j", j=J)
                        ends = xe1[:, bass.ds(t * SUBS + s, 1), :, :]
                        for e, n0 in ((0, 0), (1, NBLK - 2)):
                            last = nc.gpsimd.tensor_copy(ends[:, 0, e, :].rearrange("p (n j) -> p n j", j=J),
                                                         tile[:, n0:n0 + 2, :])
                        last.then_inc(S.ends_kept, 1)

                    with pool.Fori(0, TURNS - 1) as t:
                        for s in range(SUBS):
                            keep_ends(t, s, res)
                    for s in range(SUBS):
                        keep_ends(TURNS - 1, s, res if s < 2 else res_end)
                    pool.wait_ge(S.ends_kept, SUBS * TURNS)
                    G = nc.gpsimd
                    for i in range(4):
                        h = slice(4 * i, 4 * i + 4)
                        pool.wait_ge(N.piece_hi, i + 1)
                        low = slice(2 * CH, 3 * CH)
                        G.tensor_tensor(up[low, h, :], stage[low, h, :], up_part[low, h, :].bitcast(F32),
                                        ALU.subtract).then_inc(N.piece_lo, 1)
                    pool.wait_ge(N.piece_in[1], 16 * 4)
                    pool.wait_ge(N.piece_lo, 4)
                    G.tensor_copy(pcol[:], pcol_i[:]).then_inc(N.onehot, 1)
                    pool.wait_ge(N.onehot, 1)
                    for j in range(J):
                        G.tensor_scalar(scatter[:, j, :], posrow[:], pcol[:, j:j + 1], None, ALU.is_equal).then_inc(N.onehot, 1)

                @block.tensor
                def _(pe):
                    def gate_up(t, c, between=None):
                        i0, m = FCH[c]
                        if c >= 2:
                            pe.wait_ge(S.mul_done, NF * t + c - 1)
                        for which, ready in ((0, S.first_ready), (1, S.second_ready)):
                            if which == 1 and between is not None:
                                between()
                            col = which * FF + i0
                            dst = pair(c)[which][0:m, :]
                            if c == 0 and which == 0:
                                pe.wait_ge(S.z_ready, SUBS * t + 2)
                                pe.wait_ge(S.z_high, SUBS * t + SUBS)
                                for j in range(J):
                                    MM(dst, gu_hi[:, j, col:col + m], z_hi[:, j, :], start=(j == 0), stop=False)
                                    MM(dst, gu_lo[:, j, col:col + m], z_hi[:, j, :], start=False, stop=False)
                                pe.wait_ge(S.z_ready, SUBS * t + SUBS)
                                for j in range(J):
                                    last = MM(dst, gu_hi[:, j, col:col + m], z_lo[:, j, :],
                                              start=False, stop=(j == J - 1))
                                last.then_inc(ready, 1)
                                continue
                            for j in range(J):
                                last = three(dst, gu_hi[:, j, col:col + m], gu_lo[:, j, col:col + m],
                                             z_hi[:, j, :], z_lo[:, j, :], j == 0, j == J - 1)
                            last.then_inc(ready, 1)

                    def down(t, c):
                        i0, m = FCH[c]
                        pe.wait_ge(S.hid_ready, NF * t + c + 1)
                        for s in range(SUBS):
                            hi = hid_hi[0:m, c % 2, P * s:P * (s + 1)]
                            lo = hid_lo[0:m, c % 2, P * s:P * (s + 1)]
                            last = three(bank[4 + s][:, :], hi, lo, dn_hi[0:m, c, :], dn_lo[0:m, c, :],
                                         c == 0, c == NF - 1)
                            if c == NF - 1:
                                last.then_inc(S.acc_ready, 1)
                        if c < NF - 1:
                            last.then_inc(S.down_done, 1)

                    def bridge(t, c, place):
                        kind, n = BRIDGE.get(c, {}).get(place, (None, 0))
                        if kind is not None:
                            pe.wait_ge(S.mul_done, NF * t + c)
                        if (kind, n) == ("step", 2):
                            net_left(pe, 1, T1, 3)
                        if kind == "style":
                            (style_products, style_sums, style_flip)[n](pe, 1, pair(c + 1)[0])
                        if kind == "net":
                            net_products(pe, 1, T1, n)
                        if kind == "step":
                            step(pe, 1, 0, n, bridge_banks(c, n))

                    def bridge_left(c):
                        for kind, n in BRIDGE.get(c, {}).values():
                            if kind == "style":
                                pe.wait_ge(N.vec, (STEP_STYLES, STEP_SUMS[1], STEP_A4[1])[n])
                            if kind == "net":
                                net_left(pe, 1, T1, n)
                            if kind == "step":
                                pe.wait_ge(N.kept, n + 1)

                    def turn(t, more):
                        pe.wait_ge(S.out_ready, SUBS * t + OUT0)
                        if more:
                            step(pe, 0, t + 1, 0, (bank[4], bank[5]))
                        for c in range(NF):
                            if more and 2 <= c <= STEPS:
                                pe.wait_ge(S.kept, STEPS * t + STEPS + c)
                            if not more:
                                bridge_left(c - 1)
                                gate_up(t, c, lambda: bridge(t, c, 0))
                            else:
                                gate_up(t, c)
                            other = pair(c + 1)
                            if c >= 1:
                                pe.wait_ge(S.mul_done, NF * t + c)
                            if more and 1 <= c < STEPS:
                                step(pe, 0, t + 1, c, other)
                            if not more:
                                bridge(t, c, 1)
                            if c == 1 and more:
                                pe.wait_ge(S.kept, STEPS * t + STEPS + 1)
                            if c >= 1:
                                down(t, c - 1)
                        down(t, NF - 1)
                        pe.wait_ge(S.mul_done, NF * t + NF)
                        if more:
                            convolve(pe, 0, t + 1)
                        else:
                            bridge_left(NF - 1)
                            convolve(pe, 1, 0)

                    style_products(pe, 0, bank[0])
                    style_sums(pe, 0, bank[1])
                    style_flip(pe, 0, bank[2])
                    first = (bank[4], bank[5])
                    step(pe, 0, 0, 0, first)
                    step(pe, 0, 0, 1, first)
                    net_products(pe, 0, T, 1)
                    step(pe, 0, 0, 2, first)
                    step(pe, 0, 0, 3, first)
                    net_products(pe, 0, T, 2)
                    step(pe, 0, 0, 4, first)
                    step(pe, 0, 0, 5, first)
                    net_products(pe, 0, T, 3)
                    pe.wait_ge(pick_ready, 1)
                    pe.wait_ge(zeros_ready, 1)
                    pe.wait_ge(S.x_in, 16 * J)
                    for g in range(2):
                        convolve_group(pe, 0, 0, g, zero_rows, False)
                    net_products(pe, 0, T, 4)
                    net_products(pe, 0, T, 5)
                    for g in range(2, SUBS):
                        convolve_group(pe, 0, 0, g, zero_rows, False)
                    pe.wait_ge(S.rows_in, 16 * J)
                    for g in range(SUBS):
                        MM(conv_bank(0, g)[:, :], pick[:], rows[:, g, :], start=False, stop=True).then_inc(S.conv_ready, 1)
                    net_left(pe, 0, T, 5)
                    pe.wait_ge(S.piece_lo, len(pieces))
                    with pe.Fori(0, TURNS - 1) as t:
                        turn(t, True)
                    turn(TURNS - 1, False)

                @block.scalar
                def _(act):
                    def load_piece(i):
                        src, hi, lo = pieces[i]
                        act.dma_start(places[i % 4][0:hi.shape[0], 0:hi.shape[1]], src).then_inc(S.piece_in[i % 4], 16)

                    for i in range(4):
                        load_piece(i)
                    act.wait_ge(pick_in, 16)
                    nc.scalar.activation(pick[:], pick_raw, ACT.Copy).then_inc(pick_ready, 1)
                    style_root(act, 0)
                    for i, (src, hi, lo) in enumerate(pieces):
                        act.wait_ge(S.piece_in[i % 4], 16 * (i // 4 + 1))
                        nc.scalar.activation(hi, places[i % 4][0:hi.shape[0], 0:hi.shape[1]],
                                             ACT.Copy).then_inc(S.piece_hi, 1)
                        if i >= 1 and i + 3 < len(pieces):
                            act.wait_ge(S.piece_lo, i)
                            load_piece(i + 3)
                    act.wait_ge(zeroed, 1)
                    nc.scalar.activation(zero_rows, taps_e[CH:CH + 2 * SEG, 0, :], ACT.Copy).then_inc(zeros_ready, 1)

                    def turn(t, more):
                        if more:
                            act.wait_ge(S.seed, 4 * t + 4)
                            load_a4(act, 0, t + 1)
                        z_high_parts(act, 0, t, z_hi)
                        for c in range(NF):
                            m = FCH[c][1]
                            act.wait_ge(S.first_ready, NF * t + c + 1)
                            if c >= 2:
                                act.wait_ge(S.hid_ready, NF * t + c - 1)
                            nc.scalar.activation(hid[0:m, c % 2, :], pair(c)[0][0:m, :], ACT.Silu).then_inc(S.act_done, 1)
                            if not more and c == 2:
                                style_root(act, 1)

                    with act.Fori(0, TURNS - 1) as t:
                        turn(t, True)
                    turn(TURNS - 1, False)
                    act.wait_ge(S.second_ready, NF * TURNS)
                    act.dma_start(stage[:], d["up"]).then_inc(N.piece_in[0], 16)
                    for dst, src in ((prow_i[:], d["perm_row"].partition_broadcast(P)), (pcol_i[:], d["perm_col"]),
                                     (posrow[:], d["pos_row"].partition_broadcast(P)), (poscol[:], d["pos_col"])):
                        act.dma_start(dst, src).then_inc(N.piece_in[1], 16)
                    act.dma_start(bd_1[:], d["bd"][1]).then_inc(N.net_in, 16)
                    act.dma_start(hd[:], d["hd"]).then_inc(N.piece_in[2], 16)
                    act.wait_ge(N.piece_in[0], 16)
                    for i in range(4):
                        h = slice(4 * i, 4 * i + 4)
                        nc.scalar.activation(up_part[2 * CH:3 * CH, h, :], stage[2 * CH:3 * CH, h, :],
                                             ACT.Copy).then_inc(N.piece_hi, 1)
                        nc.scalar.activation(up[0:2 * CH, h, :], stage[0:2 * CH, h, :], ACT.Copy).then_inc(N.up_high, 1)
                    z_high_parts(act, 1, 0, z_hi_1)

                @block.vector
                def _(dve):
                    link = Link(dve, S.vec)
                    style_weights(dve, 0, link)
                    styles(dve, 0, link, bank[0])
                    sums_of_squares(dve, 0, link, bank[1])
                    demodulation(dve, 0, link)
                    factor_tables(dve, 0, link)
                    last_factors(dve, 0, link, bank[2])
                    second_lifts(dve, 0, link)
                    first = (bank[4], bank[5])
                    dve.engine_nop().then_inc(S.out_ready, OUT0)
                    first_matrix(dve, 0, 0, 0)
                    group_factors(dve, 0, link)
                    keep(dve, 0, 0, 0, first)
                    net_values(dve, 0, T, link, 0)
                    keep(dve, 0, 0, 1, first)
                    net_values(dve, 0, T, link, 1)
                    keep(dve, 0, 0, 2, first)
                    keep(dve, 0, 0, 3, first)
                    keep(dve, 0, 0, 4, first)
                    net_values(dve, 0, T, link, 2)
                    net_values(dve, 0, T, link, "blur 2")
                    keep(dve, 0, 0, 5, first)
                    for n in (3, "blur 3", 4, 5):
                        net_values(dve, 0, T, link, n)
                    next_link = Link(dve, N.vec)

                    def bridge(c, place):
                        b = pair(c + 1)[0]
                        if (c, place) == (0, 1):
                            style_weights(dve, 1, next_link)
                        if (c, place) == (1, 1):
                            styles(dve, 1, next_link, b)
                            second_lifts(dve, 1, next_link)
                        if (c, place) == (2, 0):
                            sums_of_squares(dve, 1, next_link, b)
                        if (c, place) == (2, 1):
                            demodulation(dve, 1, next_link)
                        if (c, place) == (3, 0):
                            factor_tables(dve, 1, next_link)
                        if (c, place) == (3, 1):
                            last_factors(dve, 1, next_link, b)
                            group_factors(dve, 1, next_link)
                            net_values(dve, 1, T1, next_link, 0)
                        if (c, place) == (5, 1):
                            net_values(dve, 1, T1, next_link, "blur 2")
                        kind, n = BRIDGE.get(c, {}).get(place, (None, 0))
                        if kind == "net":
                            net_values(dve, 1, T1, next_link, n)
                        if kind == "step":
                            if n == 0:
                                first_matrix(dve, 1, 0, 0)
                            keep(dve, 1, 0, n, bridge_banks(c, n))
                        if (c, place) == (7, 1):
                            net_values(dve, 1, T1, next_link, "blur 3")

                    def hidden(t, c, m):
                        k = c % 2
                        if c >= 2:
                            dve.wait_ge(S.down_done, (NF - 1) * t + c - 1)
                        V.tensor_copy(hid_hi[0:m, k, :], hid[0:m, k, :]).then_inc(S.high_done, 1)
                        dve.wait_ge(S.high_done, NF * t + c + 1)
                        V.tensor_tensor(hid_lo[0:m, k, :], hid[0:m, k, :], hid_hi[0:m, k, :].bitcast(F32),
                                        ALU.subtract).then_inc(S.hid_ready, 1)

                    def turn(t, more):
                        if more:
                            first_matrix(dve, 0, t + 1, 0)
                        z_low_parts(dve, 0, t, z_hi, z_lo)
                        if more:
                            keep(dve, 0, t + 1, 0, (bank[4], bank[5]))
                        for c in range(NF):
                            m = FCH[c][1]
                            if not more:
                                bridge(c, 0)
                            dve.wait_ge(S.act_done, NF * t + c + 1)
                            dve.wait_ge(S.second_ready, NF * t + c + 1)
                            V.tensor_tensor(hid[0:m, c % 2, :], hid[0:m, c % 2, :], pair(c)[1][0:m, :],
                                            ALU.mult).then_inc(S.mul_done, 1)
                            dve.wait_ge(S.mul_done, NF * t + c + 1)
                            hidden(t, c, m)
                            other = pair(c + 1)
                            if more and 1 <= c < STEPS:
                                keep(dve, 0, t + 1, c, other)
                            if not more:
                                bridge(c, 1)
                        add_residual(dve, 0, t, res, bank[4:8], None if more else res_end)

                    with dve.Fori(0, TURNS - 1) as t:
                        turn(t, True)
                    turn(TURNS - 1, False)
                    dve.wait_ge(N.piece_in[1], 16 * 4)
                    V.tensor_copy(prow[:], prow_i[:]).then_inc(N.gathers, 1)
                    dve.wait_ge(N.gathers, 1)
                    for j in range(J):
                        V.tensor_scalar(gather[:, j, :], prow[:], poscol[:, j:j + 1], None, ALU.is_equal).then_inc(N.gathers, 1)
                    z_low_parts(dve, 1, 0, z_hi_1, z_lo_1)

        with ExitStack() as ctx:
            B, S = sems
            sb("second_tiles", [P, second_bytes // 4], F32, ctx)
            res = sb("res1", [P, SUBS, TOK], F32, ctx)
            wide = (GROUPS // 2) * SEG
            one, two, ta = (sb(f"net_{n}_1", [P, w], F32, ctx)[:] for n, w in
                            (("one", wide * NY), ("two", wide * NZ), ("ta", wide * NZ)))
            e = sb("net_e_1", [GROUPS // 2 * J, 2 * SEG * P], F32R, ctx)[:]
            z_hi, z_lo = z_hi_1, z_lo_1
            NH = 2 * HPQ
            STEP_AT = {0: 1, 2: 2, 5: 3, 8: 4, 12: 5}
            hid = sb("hid1", [P, NH, TOK], F32, ctx)
            tp = sb("tp", [3 * CH, NH, TOK], F32R, ctx)
            warm = sb("warm", [P, 1], F32, ctx)
            y_hi = sb("y_hi", [P, J, TOK], F32R, ctx)
            y_lo = sb("y_lo", [P, J, TOK], F32R, ctx)
            cbanks = (bank[6], bank[7])
            SUM_AT = {6: 0, 10: 1, 14: 2, HEADS + 1: 3}
            T2 = net_tiles(NetSteps(GROUPS // 2, GROUPS // 2, T1["steps"].edge, T1["steps"].p_end),
                           one, two, ta, bd_1[:], e, {1: cbanks[1:2], 2: cbanks, 3: cbanks, 4: cbanks[1:2],
                                                 5: cbanks[0:1]}, 32)
            NET_AT = {1: 1, 5: 2, 11: 3, 14: 4, 15: 5}
            STEP_AT_FIRST = {2: 1, 4: 2, 7: 3, 10: 4, 13: 5}
            obanks = (bank[0], bank[1], bank[6], bank[7])

            with nc.Block() as block:
                @block.sync
                def _(sp):
                    for s in range(2):
                        sp.wait_ge(B.out_done[s], 16 * (2 * TURNS))
                    for s in range(SUBS):
                        load_res(sp, 1, 0, s, res)
                    sync_turn(sp, 1, 0, res, T2)
                    with sp.Fori(1, TURNS - 1) as t:
                        sync_turn(sp, 1, t, res)
                    for s in range(SUBS):
                        store_out(sp, 1, TURNS - 1, s, res)
                    for s in range(SUBS):
                        sp.wait_ge(S.out_done[s], 16 * TURNS)

                @block.tensor
                def _(pe):
                    def permute(t, q):
                        if q >= 2:
                            pe.wait_ge(S.t_ready, HEADS * t + HPQ * (q - 1))
                        dst = bank[q % 2][:, :]
                        if q == 0:
                            pe.wait_ge(S.z_ready, SUBS * t + 3)
                            pe.wait_ge(S.z_high, SUBS * t + SUBS)
                        for z in (z_hi, z_lo):
                            if q == 0 and z is z_lo:
                                pe.wait_ge(S.z_ready, SUBS * t + SUBS)
                            for j in range(J):
                                last = MM(dst, gather[:, j, P * q:P * (q + 1)], z[:, j, :],
                                          start=(z is z_hi and j == 0), stop=(z is z_lo and j == J - 1))
                        last.then_inc(S.perm_ready, 1)

                    def head_up(t, h):
                        pe.wait_ge(S.t_ready, HEADS * t + h + 1)
                        if h >= 2:
                            pe.wait_ge(S.act_done, HEADS * t + h - 1)
                        MM(bank[2 + h % 2][:, :], up[:, h, :], tp[:, h % NH, :],
                           start=True, stop=True).then_inc(S.first_ready, 1)

                    def heads_down(t, q):
                        pe.wait_ge(S.act_done, HEADS * t + HPQ * (q + 1))
                        if q >= 2:
                            pe.wait_ge(S.y_ready, J * t + q - 1)
                        for r in range(HPQ):
                            h = HPQ * q + r
                            last = MM(bank[4 + q % 2][CH * r:CH * (r + 1), :], hd[:, h, :], hid[:, h % NH, :],
                                      start=True, stop=True)
                        last.then_inc(S.sum_ready, 1)

                    def permute_back(t, s, qs):
                        for q in qs:
                            if s == 0:
                                pe.wait_ge(S.y_ready, J * t + q + 1)
                            MM(obanks[s][:, :], y_hi[:, q, P * s:P * (s + 1)], scatter[:, q, :],
                               start=(q == 0), stop=False)
                            last = MM(obanks[s][:, :], y_lo[:, q, P * s:P * (s + 1)], scatter[:, q, :],
                                      start=False, stop=(q == J - 1))
                        if J - 1 in qs:
                            last.then_inc(S.acc_ready, 1)

                    def turn(t, more, first=False):
                        pe.wait_ge(S.out_ready, SUBS * t + OUT0)
                        if more and not first:
                            step(pe, 1, t + 1, 0, cbanks)
                        if first:
                            pe.wait_ge(S.gathers, 1 + J)
                        permute(t, 0)
                        permute(t, 1)
                        if first:
                            step(pe, 1, t + 1, 0, cbanks)
                        if first:
                            pe.wait_ge(S.up_high, 4)
                            pe.wait_ge(S.piece_lo, 4)
                            pe.wait_ge(S.piece_in[2], 16)
                        for h in range(HEADS):
                            head_up(t, h)
                            if h in (3, 7):
                                permute(t, 2 + h // 4)
                            steps = STEP_AT_FIRST if first else STEP_AT
                            if first and (h in NET_AT or h in steps):
                                pe.wait_ge(S.kept, STEPS + 1 + sum(a < h for a in steps))
                                net_left(pe, 1, T2, sum(a < h for a in NET_AT))
                            if more and h in steps:
                                step(pe, 1, t + 1, steps[h], cbanks)
                            if first and h in NET_AT:
                                net_products(pe, 1, T2, NET_AT[h])
                            if h in (5, 9, 13):
                                heads_down(t, (h - 5) // 4)
                            if first and h == HEADS - 2:
                                pe.wait_ge(S.onehot, 1 + J)
                            if h >= HEADS - 2:
                                permute_back(t, h - (HEADS - 2), (0, 1))
                        if more:
                            pe.wait_ge(S.kept, STEPS * t + 2 * STEPS)
                        if first:
                            net_left(pe, 1, T2, 5)
                        for s in range(2, SUBS):
                            permute_back(t, s, (0, 1))
                        heads_down(t, J - 1)
                        for q in (2, 3):
                            for s in range(SUBS):
                                permute_back(t, s, (q,))
                        if more:
                            convolve(pe, 1, t + 1)

                    turn(0, True, True)
                    with pe.Fori(1, TURNS - 1) as t:
                        turn(t, True)
                    turn(TURNS - 1, False)

                def split_high(act, t, h):
                    src = bank[h // HPQ % 2][CH * (h % HPQ):CH * (h % HPQ + 1), :]
                    if h % HPQ == 0:
                        act.wait_ge(S.perm_ready, J * t + h // HPQ + 1)
                    if h >= NH:
                        act.wait_ge(S.first_ready, HEADS * t + h - NH + 1)
                    if h % 2 == 0:
                        nc.scalar.activation(tp[2 * CH:3 * CH, h % NH, :], src, ACT.Copy)
                    nc.scalar.activation(tp[0:CH, h % NH, :], src, ACT.Copy).then_inc(S.t_high, 1)

                def split_low(dve, t, h):
                    src = bank[h // HPQ % 2][CH * (h % HPQ):CH * (h % HPQ + 1), :]
                    high = tp[0:CH, h % NH, :].bitcast(F32)
                    dve.wait_ge(S.t_high, HEADS * t + h + 1)
                    last = V.tensor_tensor(tp[CH:2 * CH, h % NH, :], src, high, ALU.subtract)
                    if h % 2 == 1:
                        last = V.tensor_copy(tp[2 * CH:3 * CH, h % NH, :], high)
                    last.then_inc(S.t_ready, 1)

                @block.scalar
                def _(act):
                    for s in range(2):
                        act.wait_ge(B.out_done[s], 16 * (2 * TURNS))

                    def turn(t, more, first=False):
                        if more:
                            act.wait_ge(S.seed, 4 * t + 4)
                            load_a4(act, 1, t + 1)
                        nc.scalar.activation(warm[:], bias[:, 0:1], ACT.Gelu)
                        if not first:
                            z_high_parts(act, 1, t, z_hi)
                        for h in range(HPQ):
                            split_high(act, t, h)
                        for h in range(HEADS + 2):
                            if h < HEADS:
                                act.wait_ge(S.first_ready, HEADS * t + h + 1)
                                if h >= NH:
                                    act.wait_ge(S.sum_ready, J * t + h // HPQ - 1)
                                nc.scalar.activation(hid[:, h % NH, :], bank[2 + h % 2][:, :], ACT.Gelu).then_inc(S.act_done, 1)
                            if h + HPQ < HEADS:
                                split_high(act, t, h + HPQ)
                            if h in SUM_AT:
                                q = SUM_AT[h]
                                act.wait_ge(S.sum_ready, J * t + q + 1)
                                nc.scalar.activation(y_hi[:, q, :], bank[4 + q % 2][:, :], ACT.Copy).then_inc(S.y_high, 1)

                    turn(0, True, True)
                    with act.Fori(1, TURNS - 1) as t:
                        turn(t, True)
                    turn(TURNS - 1, False)

                @block.vector
                def _(dve):
                    link = Link(dve, S.vec)
                    for s in range(2):
                        dve.wait_ge(B.out_done[s], 16 * (2 * TURNS))
                    link.done = T1["steps"].edge
                    dve.engine_nop().then_inc(S.out_ready, OUT0)

                    def turn(t, more, first=False):
                        if more and not first:
                            first_matrix(dve, 1, t + 1, 0)
                        if not first:
                            z_low_parts(dve, 1, t, z_hi, z_lo)
                        if first:
                            first_matrix(dve, 1, t + 1, 0)
                            net_values(dve, 1, T2, link, 0)
                        if more and not first:
                            keep(dve, 1, t + 1, 0, cbanks)
                        for h in range(HPQ):
                            split_low(dve, t, h)
                            if first and h == 1:
                                keep(dve, 1, t + 1, 0, cbanks)
                        for h in range(HEADS + 2):
                            steps = STEP_AT_FIRST if first else STEP_AT
                            if more and h in steps:
                                keep(dve, 1, t + 1, steps[h], cbanks)
                            if first and h in NET_AT:
                                net_values(dve, 1, T2, link, NET_AT[h])
                                if NET_AT[h] in (2, 3):
                                    net_values(dve, 1, T2, link, f"blur {NET_AT[h]}")
                            if h + HPQ < HEADS:
                                split_low(dve, t, h + HPQ)
                            if h in SUM_AT:
                                q = SUM_AT[h]
                                dve.wait_ge(S.y_high, J * t + q + 1)
                                V.tensor_tensor(y_lo[:, q, :], bank[4 + q % 2][:, :], y_hi[:, q, :].bitcast(F32),
                                                ALU.subtract).then_inc(S.y_ready, 1)
                        add_residual(dve, 1, t, res, obanks)

                    turn(0, True, True)
                    with dve.Fori(1, TURNS - 1) as t:
                        turn(t, True)
                    turn(TURNS - 1, False)


def layouts(x, cond_512, w, perm, L1_ffn_up, L1_ffn_down, L0_ffn_w_gate_up, L0_ffn_w_down):
    f = np.float32
    a = {}
    a["x0"] = x.reshape(BATCH, CH, NBLK, J).transpose(0, 1, 3, 2)
    ends = np.stack([x[:, :, 0:2 * J], x[:, :, LEN - 2 * J:]], 2)
    a["xe0"] = ends.reshape(GROUPS, GB * CH, 2, 2 * J).transpose(1, 0, 2, 3)
    a["cond"] = cond_512.T
    per = {k: [] for k in ("modw", "modb", "bias", "wio", "bd", "lift1", "w2r", "lift3a", "lift3b", "w4")}
    for weights, biases, mod_w, mod_b in w:
        per["modw"].append(np.tile(mod_w.transpose(2, 0, 1), (1, 1, J)))
        per["modb"].append(np.tile(mod_b.T, (J, 1)))
        per["bias"].append(np.tile(biases.T, (GB, 1)))
        per["wio"].append(weights.transpose(2, 0, 3, 1))
        bd = np.zeros((P, LAYERS * KT, P), f)
        for l in range(LAYERS):
            for k in range(KT):
                m = weights[l, :, :, k] if l == 1 else weights[l, :, :, k].T
                for g in range(GB):
                    bd[g * CH:(g + 1) * CH, l * KT + k, g * CH:(g + 1) * CH] = m
        per["bd"].append(bd)
        lift1 = np.zeros((KT, CH, TQ, CH), f)
        for k4 in range(KT):
            for k3 in range(KT):
                lift1[k4, :, k4 + k3, :] = weights[2, :, :, k3]
        per["lift1"].append(lift1.reshape(KT * CH, TQ * CH))
        per["w2r"].append(np.tile(weights[1].transpose(1, 2, 0), (J, 1, 1)))
        lift3 = np.zeros((TL, CH, TU, CH), f)
        for la in range(TL):
            for u in range(TU):
                k1 = (4 - u) - (la - 3) + 1
                if 0 <= k1 < KT:
                    lift3[la, :, u, :] = weights[0, :, :, k1]
        per["lift3a"].append(lift3[:4, :, 4:].reshape(P, 5 * CH))
        lift3b = lift3[3:, :, :8].copy()
        lift3b[0, :, 4:] = 0
        per["lift3b"].append(lift3b.reshape(P, 8 * CH))
        per["w4"].append(weights[3].transpose(2, 1, 0).reshape(KT * CH, CH))
    for k, v in per.items():
        a[k] = np.stack(v)
    c = compose_coefficients()
    coef = np.zeros((P, 2, KT, TL), f)
    coef[:, 0] = np.repeat(c[:4], CH, 0)
    coef[3 * CH:, 1] = c[4]
    a["coef"] = coef
    pick = np.zeros((2, SEG, P), f)
    pick[:, 0, P - 2] = 1
    pick[:, 1, P - 1] = 1
    pick[:, 2, :INNER] = 1
    a["pick"] = pick.reshape(2 * SEG, P)
    a["ident"] = np.eye(P, dtype=f)
    block_of = np.array(list(range(1, NBLK - 1)) + [0, NBLK - 1])
    pos = block_of[:, None] * J + np.arange(J)[None]
    a["gu"] = L0_ffn_w_gate_up.T[pos].transpose(1, 0, 2)
    natural = (np.arange(NBLK)[None] * J + np.arange(J)[:, None]).reshape(-1)
    a["dn"] = L0_ffn_w_down.T[:, natural]
    a["up"] = np.tile(L1_ffn_up.transpose(1, 0, 2), (3, 1, 1))
    a["hd"] = L1_ffn_down.transpose(1, 0, 2)
    a["perm_row"] = perm.reshape(1, LEN)
    a["perm_col"] = perm.reshape(J, P).T
    a["pos_row"] = natural.astype(f).reshape(1, LEN)
    a["pos_col"] = pos.astype(f)
    return a, natural


def kernel(x, cond_512, L0_cond_weights, L0_cond_biases, L0_cond_mod_w, L0_cond_mod_b, L0_ffn_w_gate_up,
           L0_ffn_w_down, L1_cond_weights, L1_cond_biases, L1_cond_mod_w, L1_cond_mod_b, L1_ffn_up,
           L1_ffn_down, L1_ffn_perm):
    import concourse.bacc as bacc
    from concourse.bass_utils import run_bass_kernel_spmd

    w = [(L0_cond_weights, L0_cond_biases, L0_cond_mod_w, L0_cond_mod_b),
         (L1_cond_weights, L1_cond_biases, L1_cond_mod_w, L1_cond_mod_b)]
    w = [tuple(np.asarray(v) for v in layer) for layer in w]
    arrays, natural = layouts(np.asarray(x), np.asarray(cond_512), w, np.asarray(L1_ffn_perm),
                              np.asarray(L1_ffn_up), np.asarray(L1_ffn_down),
                              np.asarray(L0_ffn_w_gate_up), np.asarray(L0_ffn_w_down))
    nc = bacc.Bacc("TRN2", target_bir_lowering=False, num_devices=1, dynamic_dma_scratch_size=1024)
    ins, d = {}, {}
    for name, v in arrays.items():
        v = np.ascontiguousarray(v)
        ins[f"in_{name}"] = v
        d[name] = nc.dram_tensor(f"in_{name}", v.shape, mybir.dt.from_np(v.dtype), kind="ExternalInput").ap()
    out = nc.dram_tensor("out_y", [BATCH, CH, J, NBLK], F32, kind="ExternalOutput").ap()
    build(nc, d, out)
    r = run_bass_kernel_spmd(nc, [ins], core_ids=[0])
    y = r.results[0]["out_y"]
    return np.ascontiguousarray(y.transpose(0, 1, 3, 2)).reshape(BATCH, CH, LEN)
```
